# Optimizing a Trainium2 kernel written in Bass

```python
import numpy as np
import jax
import jax.numpy as jnp

def _softmax(x, axis=-1):
    return jax.nn.softmax(x, axis=axis)

def _gelu(x):
    return jax.nn.gelu(x, approximate=True)

def _silu(x):
    return jax.nn.silu(x)

def _sigmoid(x):
    return jax.nn.sigmoid(x)

def _layernorm(x, axis=-1, eps=1e-05):
    m = jnp.mean(x, axis=axis, keepdims=True)
    v = jnp.var(x, axis=axis, keepdims=True)
    return (x - m) / jnp.sqrt(v + eps)

def _scatter_add(tgt, idx, src, axis=0):
    return tgt.at[idx].add(src)

def _segment_sum(src, seg, n):
    return jax.ops.segment_sum(src, seg, n)
kernel_name = 'mk_adaln_ffn_d2_seqx_r4_40b66a'

def setup_inputs(seed: int=0):
    np.random.seed(seed)
    _w = jnp.asarray

    def _rec_inputs():
        import jax
        import jax.numpy as jnp
        _rk = jax.random.key(seed)
        x = -0.0002928 + 1 * jax.random.normal(jax.random.fold_in(_rk, 1), (2, 1024, 256), jnp.float32)
        _lenS = 1024 - jax.random.randint(jax.random.fold_in(_rk, 7), (2,), 0, max(1, 1024 // 4) + 1, jnp.int32)
        _lenS2 = 1024 - jax.random.randint(jax.random.fold_in(_rk, 8), (2,), 0, max(1, 1024 // 4) + 1, jnp.int32)
        cond_256 = -0.0209273 + 1.04763 * jax.random.normal(jax.random.fold_in(_rk, 11), (2, 64), jnp.float32)
        return (x, cond_256)
    x, cond_256 = _rec_inputs()

    def _L0_cond_setup():
        import jax, jax.numpy as jnp
        import numpy as np
        B, S, E, H, CD = (4, 256, 256, 16, 64)
        HD = E // H
        FIELD_COHERENCE = 0.7
        COH_THRESHOLD = 0.5
        FIELD_COUPLING = 0.3

        def _layernorm(x, g, b, eps=1e-05):
            mu = x.mean(-1, keepdims=True)
            var = ((x - mu) ** 2).mean(-1, keepdims=True)
            return (x - mu) * jax.lax.rsqrt(var + eps) * g + b
        key = jax.random.key(seed)
        ks = jax.random.split(key, 10)
        s = 0.02
        f32 = jnp.float32
        return {'x': jax.random.normal(ks[0], (B, S, E), f32), 'consciousness_state': jax.random.normal(ks[1], (B, CD), f32), 'Wqkv': jax.random.normal(ks[2], (3 * E, E), f32) * s, 'bqkv': jnp.zeros((3 * E,), f32), 'Wout': jax.random.normal(ks[3], (E, E), f32) * s, 'bout': jnp.zeros((E,), f32), 'Wc1': jax.random.normal(ks[4], (E, E + CD), f32) * s, 'bc1': jnp.zeros((E,), f32), 'Wc2': jax.random.normal(ks[5], (H, E), f32) * s, 'bc2': jnp.zeros((H,), f32), 'We1': jax.random.normal(ks[6], (E, CD), f32) * s, 'be1': jnp.zeros((E,), f32), 'We2': jax.random.normal(ks[7], (E, E), f32) * s, 'be2': jnp.zeros((E,), f32), 'ln_g': jnp.ones((E,), f32), 'ln_b': jnp.zeros((E,), f32)}
    _L0_cond_all = _L0_cond_setup()
    _L0_cond_in = {k: v for k, v in _L0_cond_all.items() if k in ('Wqkv', 'bqkv', 'Wout', 'bout', 'Wc1', 'bc1', 'Wc2', 'bc2', 'We1', 'be1', 'We2', 'be2', 'ln_g', 'ln_b')}
    del _L0_cond_all

    def _L0_ffn_setup():
        import jax, jax.numpy as jnp
        import numpy as np
        B, M, D = (4, 512, 256)
        N, P = (64, 32)
        key = jax.random.key(seed)
        k1, k2, k3, k4 = jax.random.split(key, 4)
        x = jax.random.normal(k1, (B, M, D), dtype=jnp.float32)
        phi = jax.random.normal(k2, (D, N, P), dtype=jnp.float32) * (1.0 / np.sqrt(D))
        W = jax.random.normal(k3, (N, D, D), dtype=jnp.float32) * (1.0 / np.sqrt(D))
        b = jax.random.normal(k4, (N, D), dtype=jnp.float32) * 0.01
        return {'x': x, 'phi': phi, 'W': W, 'b': b}
    _L0_ffn_all = _L0_ffn_setup()
    _L0_ffn_in = {k: v for k, v in _L0_ffn_all.items() if k in ('phi', 'W', 'b')}
    del _L0_ffn_all

    def _L1_cond_setup():
        import jax, jax.numpy as jnp
        import numpy as np
        EPS = 1e-08

        def hamilton(q1, q2):
            w1, x1, y1, z1 = (q1[..., i, :] for i in range(4))
            w2, x2, y2, z2 = (q2[..., i, :] for i in range(4))
            w = w1 * w2 - x1 * x2 - y1 * y2 - z1 * z2
            x = w1 * x2 + x1 * w2 + y1 * z2 - z1 * y2
            y = w1 * y2 - x1 * z2 + y1 * w2 + z1 * x2
            z = w1 * z2 + x1 * y2 - y1 * x2 + z1 * w2
            return jnp.stack([w, x, y, z], axis=-2)

        def _normalize(q):
            return q / jnp.sqrt(jnp.sum(q * q, axis=0, keepdims=True) + EPS)
        key = jax.random.key(seed)
        k1, k2, k3, k4 = jax.random.split(key, 4)
        B, T, d_model = (4, 1024, 256)
        quat_dim = d_model // 4
        x = jax.random.normal(k1, (B, T, d_model), dtype=jnp.float32)
        q_left = jax.random.normal(k2, (4, quat_dim), dtype=jnp.float32)
        q_right = jax.random.normal(k3, (4, quat_dim), dtype=jnp.float32)
        spectral_gate = jax.random.uniform(k4, (1, 1, 1, quat_dim), dtype=jnp.float32)
        return {'x': x, 'q_left': q_left, 'q_right': q_right, 'spectral_gate': spectral_gate}
    _L1_cond_all = _L1_cond_setup()
    _L1_cond_in = {k: v for k, v in _L1_cond_all.items() if k in ('q_right', 'spectral_gate')}
    del _L1_cond_all

    def _L1_ffn_setup():
        import jax, jax.numpy as jnp
        import numpy as np
        DIM = 256
        DEPTH = 2
        HEADS = 8
        DIM_HEAD = 64
        WINDOW = 128
        INNER = HEADS * DIM_HEAD
        HID = int(DIM * 4 * 2 / 3)
        B, N = (2, 2048)
        QK_SCALE = 8.0

        def shift_token(t):
            t1, t2 = jnp.split(t, 2, axis=-1)
            t2 = jnp.pad(t2, ((0, 0), (1, 0), (0, 0)))[:, :-1]
            return jnp.concatenate([t1, t2], axis=-1)

        def l2norm(t):
            return t / jnp.clip(jnp.linalg.norm(t, axis=-1, keepdims=True), 1e-12)

        def rotate_half(x):
            x1, x2 = jnp.split(x, 2, axis=-1)
            return jnp.concatenate([-x2, x1], axis=-1)

        def rotary_xpos(q, k):
            n = q.shape[-2]
            half_idx = jnp.arange(0, DIM_HEAD, 2, dtype=jnp.float32)
            inv_freq = 1.0 / 10000.0 ** (half_idx / DIM_HEAD)
            t = jnp.arange(n, dtype=jnp.float32)
            freqs = t[:, None] * inv_freq[None, :]
            freqs = jnp.concatenate([freqs, freqs], axis=-1)
            base = (half_idx + 0.4 * DIM_HEAD) / (1.4 * DIM_HEAD)
            power = (t - n // 2) / float(WINDOW // 2)
            scale = base[None, :] ** power[:, None]
            scale = jnp.concatenate([scale, scale], axis=-1)
            cos, sin = (jnp.cos(freqs), jnp.sin(freqs))
            q = q * cos * scale + rotate_half(q) * sin * scale
            k = k * cos / scale + rotate_half(k) * sin / scale
            return (q, k)

        def local_attention(q, k, v):
            b, h, n, d = q.shape
            w = n // WINDOW
            bq = q.reshape(b, h, w, WINDOW, d) * QK_SCALE
            bk = k.reshape(b, h, w, WINDOW, d)
            bv = v.reshape(b, h, w, WINDOW, d)

            def look_around(t):
                p = jnp.pad(t, ((0, 0), (0, 0), (1, 0), (0, 0), (0, 0)))
                return jnp.concatenate([p[:, :, :w], p[:, :, 1:]], axis=3)
            bk, bv = (look_around(bk), look_around(bv))
            bt = jnp.arange(n).reshape(w, WINDOW)
            btp = jnp.pad(bt, ((1, 0), (0, 0)), constant_values=-1)
            btk = jnp.concatenate([btp[:w], btp[1:]], axis=1)
            sim = jnp.einsum('bhwid,bhwjd->bhwij', bq, bk)
            i = bt[:, :, None]
            j = btk[:, None, :]
            mask = (i < j) | (i > j + WINDOW) | (j == -1)
            sim = jnp.where(mask, -jnp.finfo(sim.dtype).max, sim)
            attn = jax.nn.softmax(sim, axis=-1)
            out = jnp.einsum('bhwij,bhwjd->bhwid', attn, bv)
            return out.reshape(b, h, n, d)

        def _layer(x, wqkv, qs, ksc, wo, lg, lb, w1, b1, w2, b2):
            b, n, _ = x.shape
            h = shift_token(x)
            qkv = h @ wqkv
            q, k, v = jnp.split(qkv, 3, axis=-1)
            to_heads = lambda t: t.reshape(b, n, HEADS, DIM_HEAD).transpose(0, 2, 1, 3)
            q, k, v = (to_heads(q), to_heads(k), to_heads(v))
            q = l2norm(q) * qs
            k = l2norm(k) * ksc
            q, k = rotary_xpos(q, k)
            o = local_attention(q, k, v)
            o = o.transpose(0, 2, 1, 3).reshape(b, n, INNER)
            x = x + o @ wo
            h = shift_token(x)
            mu = h.mean(-1, keepdims=True)
            var = h.var(-1, keepdims=True)
            h = (h - mu) / jnp.sqrt(var + 1e-05) * lg + lb
            h = h @ w1 + b1
            a, g = jnp.split(h, 2, axis=-1)
            h = a * jax.nn.gelu(g, approximate=False)
            x = x + h @ w2 + b2
            return x
        key = jax.random.key(seed)
        ks = jax.random.split(key, 6)
        return {'x': jax.random.normal(ks[0], (B, N, DIM), jnp.float32), 'wqkv': jax.random.normal(ks[1], (DEPTH, DIM, 3 * INNER), jnp.float32) * 0.02, 'q_scale': jnp.ones((DEPTH, DIM_HEAD), jnp.float32), 'k_scale': jnp.ones((DEPTH, DIM_HEAD), jnp.float32), 'wo': jax.random.normal(ks[2], (DEPTH, INNER, DIM), jnp.float32) * 0.02, 'ln_g': jnp.ones((DEPTH, DIM), jnp.float32), 'ln_b': jnp.zeros((DEPTH, DIM), jnp.float32), 'w1': jax.random.normal(ks[3], (DEPTH, DIM, 2 * HID), jnp.float32) * 0.02, 'b1': jnp.zeros((DEPTH, 2 * HID), jnp.float32), 'w2': jax.random.normal(ks[4], (DEPTH, HID, DIM), jnp.float32) * 0.02, 'b2': jnp.zeros((DEPTH, DIM), jnp.float32)}
    _L1_ffn_all = _L1_ffn_setup()
    _L1_ffn_in = {k: v for k, v in _L1_ffn_all.items() if k in ('wqkv', 'q_scale', 'k_scale', 'wo', 'ln_g', 'ln_b', 'w1', 'b1', 'w2', 'b2')}
    del _L1_ffn_all
    return {'x': x, 'cond_256': cond_256, 'L0_cond_Wqkv': _L0_cond_in['Wqkv'], 'L0_cond_bqkv': _L0_cond_in['bqkv'], 'L0_cond_Wout': _L0_cond_in['Wout'], 'L0_cond_bout': _L0_cond_in['bout'], 'L0_cond_Wc1': _L0_cond_in['Wc1'], 'L0_cond_bc1': _L0_cond_in['bc1'], 'L0_cond_Wc2': _L0_cond_in['Wc2'], 'L0_cond_bc2': _L0_cond_in['bc2'], 'L0_cond_We1': _L0_cond_in['We1'], 'L0_cond_be1': _L0_cond_in['be1'], 'L0_cond_We2': _L0_cond_in['We2'], 'L0_cond_be2': _L0_cond_in['be2'], 'L0_cond_ln_g': _L0_cond_in['ln_g'], 'L0_cond_ln_b': _L0_cond_in['ln_b'], 'L0_ffn_phi': _L0_ffn_in['phi'], 'L0_ffn_W': _L0_ffn_in['W'], 'L0_ffn_b': _L0_ffn_in['b'], 'L1_cond_q_right': _L1_cond_in['q_right'], 'L1_cond_spectral_gate': _L1_cond_in['spectral_gate'], 'L1_ffn_wqkv': _L1_ffn_in['wqkv'], 'L1_ffn_q_scale': _L1_ffn_in['q_scale'], 'L1_ffn_k_scale': _L1_ffn_in['k_scale'], 'L1_ffn_wo': _L1_ffn_in['wo'], 'L1_ffn_ln_g': _L1_ffn_in['ln_g'], 'L1_ffn_ln_b': _L1_ffn_in['ln_b'], 'L1_ffn_w1': _L1_ffn_in['w1'], 'L1_ffn_b1': _L1_ffn_in['b1'], 'L1_ffn_w2': _L1_ffn_in['w2'], 'L1_ffn_b2': _L1_ffn_in['b2']}

def reference(x, cond_256, L0_cond_Wqkv, L0_cond_bqkv, L0_cond_Wout, L0_cond_bout, L0_cond_Wc1, L0_cond_bc1, L0_cond_Wc2, L0_cond_bc2, L0_cond_We1, L0_cond_be1, L0_cond_We2, L0_cond_be2, L0_cond_ln_g, L0_cond_ln_b, L0_ffn_phi, L0_ffn_W, L0_ffn_b, L1_cond_q_right, L1_cond_spectral_gate, L1_ffn_wqkv, L1_ffn_q_scale, L1_ffn_k_scale, L1_ffn_wo, L1_ffn_ln_g, L1_ffn_ln_b, L1_ffn_w1, L1_ffn_b1, L1_ffn_w2, L1_ffn_b2):
    import jax
    import jax.numpy as jnp

    def _L0_cond_ref(x, consciousness_state, Wqkv, bqkv, Wout, bout, Wc1, bc1, Wc2, bc2, We1, be1, We2, be2, ln_g, ln_b):
        import jax, jax.numpy as jnp
        import numpy as np
        B, S, E, H, CD = (4, 256, 256, 16, 64)
        HD = E // H
        FIELD_COHERENCE = 0.7
        COH_THRESHOLD = 0.5
        FIELD_COUPLING = 0.3

        def _layernorm(x, g, b, eps=1e-05):
            mu = x.mean(-1, keepdims=True)
            var = ((x - mu) ** 2).mean(-1, keepdims=True)
            return (x - mu) * jax.lax.rsqrt(var + eps) * g + b
        Bb, Ss, Ee = x.shape
        qkv = (x @ Wqkv.T + bqkv).reshape(Bb, Ss, 3, H, HD).transpose(2, 0, 3, 1, 4)
        q, k, v = (qkv[0], qkv[1], qkv[2])
        attn = jax.nn.softmax(jnp.einsum('bhid,bhjd->bhij', q, k) / jnp.sqrt(jnp.float32(HD)), axis=-1)
        cs_exp = jnp.broadcast_to(consciousness_state[:, None, :], (Bb, Ss, CD))
        comb = jnp.concatenate([x, cs_exp], axis=-1)
        coh = jax.nn.sigmoid(jnp.tanh(comb @ Wc1.T + bc1) @ Wc2.T + bc2).transpose(0, 2, 1)
        mod = attn * coh[..., None]
        mod = mod / (mod.sum(-1, keepdims=True) + 1e-08)
        fp = _layernorm(jax.nn.relu(consciousness_state @ We1.T + be1) @ We2.T + be2, ln_g, ln_b)
        pos = jnp.arange(Ss, dtype=jnp.float32)
        inv = 10000.0 ** jnp.repeat(jnp.arange(0, Ee, 2, dtype=jnp.float32) / Ee, 2)
        pe = jnp.sin(pos[:, None] / inv[None, :])
        fa = jax.nn.softmax(jnp.einsum('be,se->bs', fp, pe), axis=-1)
        fi = FIELD_COUPLING * FIELD_COHERENCE
        mod = (1.0 - fi) * mod + fi * fa[:, None, :, None]
        out = jnp.einsum('bhij,bhjd->bhid', mod, v).transpose(0, 2, 1, 3).reshape(Bb, Ss, Ee)
        return out @ Wout.T + bout

    def _L0_ffn_ref(x, phi, W, b):
        import jax, jax.numpy as jnp
        import numpy as np
        B, M, D = (4, 512, 256)
        N, P = (64, 32)
        logits = jnp.einsum('bmd,dnp->bmnp', x, phi)
        dispatch = jax.nn.softmax(logits, axis=0)
        bsz, m, n, p = logits.shape
        combine = jax.nn.softmax(logits.reshape(bsz, m, n * p), axis=-1).reshape(bsz, m, n, p)
        slots = jnp.einsum('bmd,bmnp->bnpd', x, dispatch)
        y = jnp.einsum('bnpd,nde->bnpe', slots, W) + b[None, :, None, :]
        out = jnp.einsum('bnpd,bmnp->bmd', y, combine)
        return out

    def _L1_cond_ref(x, q_left, q_right, spectral_gate):
        import jax, jax.numpy as jnp
        import numpy as np
        EPS = 1e-08

        def hamilton(q1, q2):
            w1, x1, y1, z1 = (q1[..., i, :] for i in range(4))
            w2, x2, y2, z2 = (q2[..., i, :] for i in range(4))
            w = w1 * w2 - x1 * x2 - y1 * y2 - z1 * z2
            x = w1 * x2 + x1 * w2 + y1 * z2 - z1 * y2
            y = w1 * y2 - x1 * z2 + y1 * w2 + z1 * x2
            z = w1 * z2 + x1 * y2 - y1 * x2 + z1 * w2
            return jnp.stack([w, x, y, z], axis=-2)

        def _normalize(q):
            return q / jnp.sqrt(jnp.sum(q * q, axis=0, keepdims=True) + EPS)
        B, T, d_model = x.shape
        quat_dim = d_model // 4
        x_quat = x.reshape(B, T, 4, quat_dim)
        x_spectral = jnp.fft.fft(x_quat, axis=1)
        x_filtered = jnp.fft.ifft(x_spectral * spectral_gate, axis=1).real.astype(x.dtype)
        q_left_n = _normalize(q_left)
        q_right_n = _normalize(q_right)
        conj_sign = jnp.array([1.0, -1.0, -1.0, -1.0], dtype=x.dtype)[:, None]
        q_right_conj = q_right_n * conj_sign
        x_right = hamilton(x_filtered, q_right_conj)
        x_rotated = hamilton(q_left_n, x_right)
        return x_rotated.reshape(B, T, d_model)

    def _L1_ffn_ref(x, wqkv, q_scale, k_scale, wo, ln_g, ln_b, w1, b1, w2, b2):
        import jax, jax.numpy as jnp
        import numpy as np
        DIM = 256
        DEPTH = 2
        HEADS = 8
        DIM_HEAD = 64
        WINDOW = 128
        INNER = HEADS * DIM_HEAD
        HID = int(DIM * 4 * 2 / 3)
        B, N = (2, 2048)
        QK_SCALE = 8.0

        def shift_token(t):
            t1, t2 = jnp.split(t, 2, axis=-1)
            t2 = jnp.pad(t2, ((0, 0), (1, 0), (0, 0)))[:, :-1]
            return jnp.concatenate([t1, t2], axis=-1)

        def l2norm(t):
            return t / jnp.clip(jnp.linalg.norm(t, axis=-1, keepdims=True), 1e-12)

        def rotate_half(x):
            x1, x2 = jnp.split(x, 2, axis=-1)
            return jnp.concatenate([-x2, x1], axis=-1)

        def rotary_xpos(q, k):
            n = q.shape[-2]
            half_idx = jnp.arange(0, DIM_HEAD, 2, dtype=jnp.float32)
            inv_freq = 1.0 / 10000.0 ** (half_idx / DIM_HEAD)
            t = jnp.arange(n, dtype=jnp.float32)
            freqs = t[:, None] * inv_freq[None, :]
            freqs = jnp.concatenate([freqs, freqs], axis=-1)
            base = (half_idx + 0.4 * DIM_HEAD) / (1.4 * DIM_HEAD)
            power = (t - n // 2) / float(WINDOW // 2)
            scale = base[None, :] ** power[:, None]
            scale = jnp.concatenate([scale, scale], axis=-1)
            cos, sin = (jnp.cos(freqs), jnp.sin(freqs))
            q = q * cos * scale + rotate_half(q) * sin * scale
            k = k * cos / scale + rotate_half(k) * sin / scale
            return (q, k)

        def local_attention(q, k, v):
            b, h, n, d = q.shape
            w = n // WINDOW
            bq = q.reshape(b, h, w, WINDOW, d) * QK_SCALE
            bk = k.reshape(b, h, w, WINDOW, d)
            bv = v.reshape(b, h, w, WINDOW, d)

            def look_around(t):
                p = jnp.pad(t, ((0, 0), (0, 0), (1, 0), (0, 0), (0, 0)))
                return jnp.concatenate([p[:, :, :w], p[:, :, 1:]], axis=3)
            bk, bv = (look_around(bk), look_around(bv))
            bt = jnp.arange(n).reshape(w, WINDOW)
            btp = jnp.pad(bt, ((1, 0), (0, 0)), constant_values=-1)
            btk = jnp.concatenate([btp[:w], btp[1:]], axis=1)
            sim = jnp.einsum('bhwid,bhwjd->bhwij', bq, bk)
            i = bt[:, :, None]
            j = btk[:, None, :]
            mask = (i < j) | (i > j + WINDOW) | (j == -1)
            sim = jnp.where(mask, -jnp.finfo(sim.dtype).max, sim)
            attn = jax.nn.softmax(sim, axis=-1)
            out = jnp.einsum('bhwij,bhwjd->bhwid', attn, bv)
            return out.reshape(b, h, n, d)

        def _layer(x, wqkv, qs, ksc, wo, lg, lb, w1, b1, w2, b2):
            b, n, _ = x.shape
            h = shift_token(x)
            qkv = h @ wqkv
            q, k, v = jnp.split(qkv, 3, axis=-1)
            to_heads = lambda t: t.reshape(b, n, HEADS, DIM_HEAD).transpose(0, 2, 1, 3)
            q, k, v = (to_heads(q), to_heads(k), to_heads(v))
            q = l2norm(q) * qs
            k = l2norm(k) * ksc
            q, k = rotary_xpos(q, k)
            o = local_attention(q, k, v)
            o = o.transpose(0, 2, 1, 3).reshape(b, n, INNER)
            x = x + o @ wo
            h = shift_token(x)
            mu = h.mean(-1, keepdims=True)
            var = h.var(-1, keepdims=True)
            h = (h - mu) / jnp.sqrt(var + 1e-05) * lg + lb
            h = h @ w1 + b1
            a, g = jnp.split(h, 2, axis=-1)
            h = a * jax.nn.gelu(g, approximate=False)
            x = x + h @ w2 + b2
            return x
        for l in range(DEPTH):
            x = _layer(x, wqkv[l], q_scale[l], k_scale[l], wo[l], ln_g[l], ln_b[l], w1[l], b1[l], w2[l], b2[l])
        return x
    x = x + _L0_ffn_ref(_L0_cond_ref(x, cond_256, L0_cond_Wqkv, L0_cond_bqkv, L0_cond_Wout, L0_cond_bout, L0_cond_Wc1, L0_cond_bc1, L0_cond_Wc2, L0_cond_bc2, L0_cond_We1, L0_cond_be1, L0_cond_We2, L0_cond_be2, L0_cond_ln_g, L0_cond_ln_b), L0_ffn_phi, L0_ffn_W, L0_ffn_b)
    x = x + _L1_ffn_ref(_L1_cond_ref(x, cond_256, L1_cond_q_right, L1_cond_spectral_gate), L1_ffn_wqkv, L1_ffn_q_scale, L1_ffn_k_scale, L1_ffn_wo, L1_ffn_ln_g, L1_ffn_ln_b, L1_ffn_w1, L1_ffn_b1, L1_ffn_w2, L1_ffn_b2)
    return x

_drawn_inputs = setup_inputs


def setup_inputs(seed=0):
    import zlib

    import numpy as np

    out = dict(_drawn_inputs(seed))
    spreads = {'L0_cond_bqkv': (0.0, 0.1),
     'L0_cond_bout': (0.0, 0.1),
     'L0_cond_bc1': (0.0, 2.0),
     'L0_cond_bc2': (0.0, 2.0),
     'L0_cond_be1': (0.0, 0.362),
     'L0_cond_be2': (0.0, 0.1),
     'L0_cond_ln_g': (1.0, 0.6),
     'L0_cond_ln_b': (0.0, 0.691),
     'L1_ffn_q_scale': (1.0, 0.6),
     'L1_ffn_k_scale': (1.0, 0.6),
     'L1_ffn_ln_g': (1.0, 0.6),
     'L1_ffn_ln_b': (0.0, 0.8),
     'L1_ffn_b1': (0.0, 0.8),
     'L1_ffn_b2': (0.0, 2.0)}
    factors = {'L0_cond_Wc1': 64.0,
     'L0_cond_Wc2': 64.0,
     'L0_ffn_b': 200.0,
     'L1_ffn_w1': 8.0,
     'L1_ffn_w2': 8.0}
    for name, (base, spread) in spreads.items():
        noise = np.random.default_rng([zlib.crc32(name.encode()), seed]).standard_normal(out[name].shape)
        drawn = base * np.exp(spread * noise) if base else spread * noise
        out[name] = jnp.asarray(drawn.astype(out[name].dtype))
    for name, factor in factors.items():
        out[name] = (out[name] * factor).astype(out[name].dtype)
    return out
```

```python
import itertools
from contextlib import ExitStack

import numpy as np

import concourse.bass as bass
from concourse import mybir

F32 = mybir.dt.float32
BF16 = mybir.dt.bfloat16
ACT = mybir.ActivationFunctionType
ALU = mybir.AluOpType
X = mybir.AxisListType.X
ds = bass.ds

P = 128
B, T, D = 2, 1024, 256
N = B * T
KD = D // P
TT = T // P
HALF = 512
H0, HD0 = 16, 16
HG = 4
KS = 6 * HD0
KA = KS + 3
Q_PART = (0, 0, 1, 1, 0, 2)
K_PART = (0, 1, 0, 1, 2, 0)
COUPLING = 0.3 * 0.7
COH_EPS = 1e-8
CD = 64
NE, NP_ = 64, 32
SLOTS = NE * NP_
CH = 4
CS = SLOTS // CH
CE = NE // CH
LAYERS = 2
H1, HD1 = 8, 64
INNER = H1 * HD1
HP = H1 // 2
WIN = 128
NW = T // WIN
HID = 682
FT = -(-HID // P)
HIDP = FT * P
QK_SCALE = 8.0
LN_EPS = 1e-5
MASKED = -1e30
LOWEST = -3e38


def chain(eng, sem, start=0):
    n = [0]

    def link(ins):
        n[0] += 1
        ins.then_inc(sem, 1)
        eng.wait_ge(sem, start + n[0])

    link.count = n
    return link


def stage_project(nc, G, A):
    with ExitStack() as ctx:
        sb = lambda n, s, dt=F32: ctx.enter_context(nc.sbuf_tensor(n, s, dt))
        sem = lambda n: ctx.enter_context(nc.semaphore(n))
        PB = G["PB"]
        xT = sb("p_xT", [P, KD, N])
        wqkv = sb("p_wqkv", [P, KD, 3 * D])
        wc1x = sb("p_wc1x", [P, KD, D])
        wc2 = sb("p_wc2", [P, KD, H0])
        we2 = sb("p_we2", [P, KD, D])
        peT = sb("p_peT", [P, KD, T])
        wc1c = sb("p_wc1c", [CD, D])
        we1 = sb("p_we1", [CD, D])
        csT = sb("p_csT", [CD, B])
        bqk = sb("p_bqk", [P, 4])
        bvB = sb("p_bvB", [P, D])
        bc1 = sb("p_bc1", [P, KD])
        be1 = sb("p_be1", [P, KD])
        bc2B = sb("p_bc2B", [P, H0])
        rows2 = sb("p_rows2", [B, 3, D])
        ql = sb("p_ql", [16, 64])
        qr = sb("p_qr", [16, 64])
        gate = sb("p_gate", [16, 64])
        qall = sb("p_qall", [16, 6, 64])
        sgn = sb("p_sgn", [16, 16])
        parts = sb("p_parts", [P, 4, 3, HALF], BF16)
        rest = sb("p_rest", [P, 4, HALF])
        c1T = sb("p_c1T", [P, KD, N])
        cbias = sb("p_cbias", [P, KD, B])
        h1T = sb("p_h1T", [P, KD, B])
        fpw = sb("p_fpw", [B, 4, D])
        fst = sb("p_fst", [B, 8])
        fpT = sb("p_fpT", [P, KD, B])
        faw = sb("p_faw", [B, 3, T])
        zt = sb("p_zt", [P, 3, B * TT * H0])
        xsum = sb("p_xsum", [P, KD, B])
        xsB = sb("p_xsB", [P, KD, B, P])
        qsq = sb("p_qsq", [16, 6, 64])
        qn = sb("p_qn", [16, 2, 64])
        qsd = sb("p_qsd", [16, 2, 64])
        qpr = sb("p_qpr", [16, 4, 64])
        pp2 = sb("p_pp2", [16, 2, 64])
        mco = sb("p_mco", [P, 16])
        ones = sb("p_ones", [P, P])
        eps5 = sb("p_eps5", [B, 1])

        ld_small, ld_x, ld_pe = sem("ld_small"), sem("ld_x"), sem("ld_pe")
        consts = sem("consts")
        dve_step, act_step = sem("dve_step"), sem("act_step")
        cond_ps, h1_ready, fp_ps, ln_var, ln_sd, fp_ready = (sem(n) for n in (
            "cond_ps", "h1_ready", "fp_ps", "ln_var", "ln_sd", "fp_ready"))
        fpT_ps, fpT_ready, fa_ps, fa_max, fa_exp, fa_ready, faT_ps = (sem(n) for n in (
            "fpT_ps", "fpT_ready", "fa_ps", "fa_max", "fa_exp", "fa_ready", "faT_ps"))
        q_norm, q_sd, pp_ready, mco_ps = sem("q_norm"), sem("q_sd"), sem("pp_ready"), sem("mco_ps")
        cb_ready = sem("cb_ready")
        qk_ps, qk_p1, qk_rest, qk_p2, qk_p3 = (sem(n) for n in ("qk_ps", "qk_p1", "qk_rest", "qk_p2", "qk_p3"))
        qk_stored = [sem(f"qk_stored{i}") for i in range(4)]
        v_ps, v_done, c1_ps, c1_done, z_ps, z_clip, z_exp = (sem(n) for n in (
            "v_ps", "v_done", "c1_ps", "c1_done", "z_ps", "z_clip", "z_exp"))
        xs_ready, vs_ps = sem("xs_ready"), sem("vs_ps")
        UNITS = [(b, hf, m) for b in range(B) for hf in range(T // HALF) for m in range(4)]
        small = [(wc1c, A["wc1cT"]), (we1, A["we1T"]), (csT, A["csT"]), (be1, A["be1"]), (bc1, A["bc1"]),
                 (rows2, A["rows2"]), (ql, A["ql"]), (qr, A["qr"]), (gate, A["gate"]), (qall, A["qall"]),
                 (sgn, A["sgn"]), (G["ident"], A["ident"]), (bqk, A["bqk"]), (bvB, A["bvB"]), (bc2B, A["bc2B"])]
        NSMALL = 16 * (len(small) + 2)
        kp = lambda a: a.rearrange("(k p) n -> p k n", p=P)
        scr = G["scr"]
        ring = lambda u: PB[(u % 4) // 2][:, HALF * (u % 2):HALF * (u % 2) + HALF]
        misc = lambda r, a, b: PB[3][0:r, HALF + a:HALF + b]

        with nc.Block() as block:
            @block.sync
            def _(sp):
                for dst, src in small:
                    sp.dma_start(dst[:], src).then_inc(ld_small, 16)
                sp.dma_start(we2[:, :, :], kp(A["we2T"])).then_inc(ld_small, 16)
                sp.dma_start(wc2[:, :, :], kp(A["wc2T"])).then_inc(ld_small, 16)
                sp.dma_start(peT[:, :, :], kp(A["peT"])).then_inc(ld_pe, 16)
                for u, (b, hf, m) in enumerate(UNITS):
                    sp.wait_ge(qk_p3, u + 1)
                    t0 = b * T + hf * HALF
                    dst = scr[m // 2, :, (m % 2) * P:(m % 2) * P + P, t0:t0 + HALF].rearrange("c p t -> p c t")
                    sp.dma_start(dst, parts[:, u % 4, :, :]).then_inc(qk_stored[u % 4], 16)
                for s in qk_stored:
                    sp.wait_ge(s, 16 * len(UNITS) // 4)

            @block.gpsimd
            def _(pool):
                nc.gpsimd.memset(ones[:, :], 1.0).then_inc(consts, 1)
                nc.gpsimd.memset(eps5[:, :], LN_EPS).then_inc(consts, 1)
                for u in range(len(UNITS)):
                    pool.wait_ge(qk_p2, u + 1)
                    nc.gpsimd.tensor_tensor(parts[:, u % 4, 2, :], rest[:, u % 4, :], parts[:, u % 4, 1, :],
                                            ALU.subtract).then_inc(qk_p3, 1)

            @block.scalar
            def _(act):
                act.dma_start(xT[:, :, :], kp(A["xT"])).then_inc(ld_x, 16)
                act.dma_start(wqkv[:, :, :], kp(A["wqkv0T"])).then_inc(ld_x, 16)
                act.dma_start(wc1x[:, :, :], kp(A["wc1xT"])).then_inc(ld_x, 16)
                act.wait_ge(ld_small, NSMALL)
                act.wait_ge(consts, 2)
                act.wait_ge(cb_ready, KD)
                for k in range(KD):
                    nc.scalar.activation(h1T[:, k, :], misc(P, 4 + 2 * k, 6 + 2 * k), ACT.Relu,
                                         bias=be1[:, k:k + 1]).then_inc(h1_ready, 1)
                act.wait_ge(q_norm, 1)
                nc.scalar.activation(qsd[:, :, :], qn[:, :, :], ACT.Sqrt).then_inc(q_sd, 1)
                act.wait_ge(ln_var, 1)
                nc.scalar.activation(fst[:, 4:5], fst[:, 3:4], ACT.Sqrt, bias=eps5[:, 0:1]).then_inc(ln_sd, 1)
                for u, (b, hf, m) in enumerate(UNITS):
                    s = u % 4
                    act.wait_ge(qk_ps, u + 1)
                    if u >= 4:
                        act.wait_ge(qk_stored[s], 16 * (u // 4))
                    nc.scalar.activation(parts[:, s, 0, :], ring(u), ACT.Identity,
                                         bias=bqk[:, m:m + 1]).then_inc(qk_p1, 1)
                    if u >= 1:
                        act.wait_ge(qk_rest, u)
                        nc.scalar.activation(parts[:, (u - 1) % 4, 1, :], rest[:, (u - 1) % 4, :],
                                             ACT.Copy).then_inc(qk_p2, 1)
                act.wait_ge(qk_rest, len(UNITS))
                nc.scalar.activation(parts[:, 3, 1, :], rest[:, 3, :], ACT.Copy).then_inc(qk_p2, 1)
                act.wait_ge(cb_ready, KD)
                for v in range(KD * N // HALF):
                    e, n = v % KD, v // KD
                    act.wait_ge(c1_ps, v + 1)
                    nc.scalar.activation(c1T[:, e, n * HALF:(n + 1) * HALF], ring(v), ACT.Tanh,
                                         bias=cbias[:, e, n // 2:n // 2 + 1]).then_inc(c1_done, 1)
                act.wait_ge(fa_max, 1)
                nc.scalar.activation(faw[:, 1, :], faw[:, 0, :], ACT.Exp, bias=fst[:, 6:7],
                                     accum_out=fst[:, 7:8]).then_inc(fa_exp, 1)
                act.wait_ge(z_clip, 1)
                nc.scalar.activation(zt[:, 2, :], zt[:, 1, :], ACT.Exp).then_inc(z_exp, 1)

            @block.vector
            def _(dve):
                link = chain(dve, dve_step)
                V = nc.vector
                dve.wait_ge(ld_small, NSMALL)
                dve.wait_ge(consts, 2)
                link(V.tensor_tensor(qsq[:, :, :], qall[:, :, :], qall[:, :, :], ALU.mult))
                link(V.tensor_reduce(qn[:, 0, :], qsq[:, 0:2, :].rearrange("p r d -> p d r"), X, ALU.add))
                link(V.tensor_reduce(qn[:, 1, :], qsq[:, 2:6, :].rearrange("p r d -> p d r"), X, ALU.add))
                V.tensor_scalar_add(qn[:, :, :], qn[:, :, :], 1e-8).then_inc(q_norm, 1)
                dve.wait_ge(cond_ps, 1)
                for k in range(KD):
                    V.tensor_scalar_add(cbias[:, k, :], misc(P, 2 * k, 2 * k + 2), bc1[:, k:k + 1]).then_inc(cb_ready, 1)
                dve.wait_ge(q_sd, 1)
                link(V.tensor_tensor(qpr[:, 0, :], qsd[:, 0, :], qsd[:, 1, :], ALU.mult))
                link(V.reciprocal(qpr[:, 1, :], qpr[:, 0, :]))
                link(V.tensor_tensor(qpr[:, 2, :], ql[:, :], qr[:, :], ALU.mult))
                link(V.tensor_tensor(qpr[:, 3, :], qpr[:, 2, :], gate[:, :], ALU.mult))
                for r in range(2):
                    V.tensor_tensor(pp2[:, r, :], qpr[:, 3, :], qpr[:, 1, :], ALU.mult).then_inc(pp_ready, 1)
                dve.wait_ge(fp_ps, 1)
                link(V.tensor_tensor(fpw[:, 0, :], misc(B, 16, 16 + D), rows2[:, 0, :], ALU.add))
                link(V.reduce_sum(fst[:, 0:1], fpw[:, 0, :], X))
                link(V.tensor_scalar_mul(fst[:, 1:2], fst[:, 0:1], 1.0 / D))
                link(V.tensor_scalar(fpw[:, 1, :], fpw[:, 0, :], fst[:, 1:2], None, ALU.subtract))
                link(V.tensor_tensor(fpw[:, 2, :], fpw[:, 1, :], fpw[:, 1, :], ALU.mult))
                link(V.reduce_sum(fst[:, 2:3], fpw[:, 2, :], X))
                V.tensor_scalar_mul(fst[:, 3:4], fst[:, 2:3], 1.0 / D).then_inc(ln_var, 1)
                dve.wait_ge(ln_sd, 1)
                link(V.reciprocal(fst[:, 5:6], fst[:, 4:5]))
                link(V.scalar_tensor_tensor(out=fpw[:, 3, :], in0=fpw[:, 1, :], scalar=fst[:, 5:6],
                                            in1=rows2[:, 1, :], op0=ALU.mult, op1=ALU.mult))
                link(V.tensor_tensor(fpw[:, 0, :], fpw[:, 3, :], rows2[:, 2, :], ALU.add))
                dve.sem_inc(fp_ready, 1)
                dve.wait_ge(fpT_ps, 1)
                V.tensor_copy(fpT[:, :, :], misc(P, 288, 292).rearrange("p (k b) -> p k b", b=B)).then_inc(fpT_ready, 1)
                dve.wait_ge(mco_ps, 1)
                link(V.tensor_copy(mco[:, :], misc(P, 304, 320)))
                for i in range(4):
                    for j in range(4):
                        r = slice(64 * (j % 2), 64 * (j % 2) + 64)
                        mc = V.tensor_scalar_mul(G["rot"][r, j // 2, 64 * i:64 * i + 64], G["ident"][r, r],
                                                 mco[r, 4 * i + j:4 * i + j + 1])
                mc.then_inc(dve_step, 1)
                for u, (b, hf, m) in enumerate(UNITS):
                    dve.wait_ge(qk_p1, u + 1)
                    if u >= 4:
                        dve.wait_ge(qk_p3, u - 3)
                    V.scalar_tensor_tensor(out=rest[:, u % 4, :], in0=ring(u), scalar=bqk[:, m:m + 1],
                                           in1=parts[:, u % 4, 0, :], op0=ALU.add,
                                           op1=ALU.subtract).then_inc(qk_rest, 1)
                for k in range(KD):
                    V.reduce_sum(xsum[:, k, :], xT[:, k, :].rearrange("p (b t) -> p b t", b=B), X).then_inc(dve_step, 1)
                dve.wait_ge(dve_step, link.count[0] + 1 + KD)
                for k in range(KD):
                    for b in range(B):
                        V.tensor_scalar_mul(xsB[:, k, b, :], ones[:, :], xsum[:, k, b:b + 1]).then_inc(xs_ready, 1)
                for tt in range(B * TT):
                    b, jt = tt // TT, tt % TT
                    dve.wait_ge(v_ps, tt + 1)
                    V.tensor_tensor(G["v"][:, 2 * b:2 * b + 2, jt, :],
                                    PB[2][:, HALF * (tt % 2):HALF * (tt % 2) + D].rearrange("p (m d) -> p m d", m=2),
                                    bvB[:, :].rearrange("p (m d) -> p m d", m=2), ALU.add).then_inc(v_done, 1)
                dve.wait_ge(vs_ps, 1)
                for b in range(B):
                    V.scalar_tensor_tensor(out=G["vsum"][:, b, :], in0=bvB[:, :], scalar=float(T),
                                           in1=PB[1][:, HALF + b * D:HALF + (b + 1) * D], op0=ALU.mult, op1=ALU.add)
                dve.wait_ge(fa_ps, 1)
                link2 = chain(dve, act_step)
                link2(V.tensor_copy(faw[:, 0, :], PB[2][0:B, 0:T]))
                link2(V.reduce_max(fst[:, 0:1], faw[:, 0, :], X))
                V.tensor_scalar_mul(fst[:, 6:7], fst[:, 0:1], -1.0).then_inc(fa_max, 1)
                dve.wait_ge(fa_exp, 1)
                link2(V.reciprocal(fst[:, 1:2], fst[:, 7:8]))
                V.tensor_scalar(faw[:, 2, :], faw[:, 1, :], fst[:, 1:2], COUPLING, ALU.mult, ALU.mult).then_inc(fa_ready, 1)
                dve.wait_ge(z_ps, 1)
                link2(V.tensor_tensor(zt[:, 0, :].rearrange("p (t h) -> p t h", h=H0),
                                      PB[3][:, 0:B * TT * H0].rearrange("p (t h) -> p t h", h=H0),
                                      bc2B[:, :].unsqueeze(1).to_broadcast([P, B * TT, H0]), ALU.add))
                V.tensor_scalar(zt[:, 1, :], zt[:, 0, :], -87.0, -1.0, ALU.max, ALU.mult).then_inc(z_clip, 1)
                dve.wait_ge(z_exp, 1)
                c = 1.0 / (1.0 - COUPLING)
                V.tensor_scalar(G["gate"][:, :], zt[:, 2, :], COH_EPS * c, (1.0 + COH_EPS) * c, ALU.mult, ALU.add)
                dve.wait_ge(faT_ps, 1)
                link2(V.tensor_copy(G["fa"][:, :, :], misc(P, 320, 320 + B * TT).rearrange("p (t b) -> p t b", b=B)))

            @block.tensor
            def _(pe):
                mm, tr, ident = nc.tensor.matmul, nc.tensor.transpose, G["ident"]
                pe.wait_ge(ld_small, NSMALL)
                for k in range(KD):
                    mm(misc(P, 2 * k, 2 * k + 2), wc1c[:, k * P:(k + 1) * P], csT[:, :], start=True, stop=True)
                    last = mm(misc(P, 4 + 2 * k, 6 + 2 * k), we1[:, k * P:(k + 1) * P], csT[:, :], start=True, stop=True)
                last.then_inc(cond_ps, 1)
                pe.wait_ge(h1_ready, KD)
                pe.wait_ge(pp_ready, 2)
                mm(misc(P, 304, 320), pp2[:, :, :].rearrange("p r d -> p (r d)"), sgn[:, :], start=True,
                   stop=True).then_inc(mco_ps, 1)
                for k in range(KD):
                    last = mm(misc(B, 16, 16 + D), h1T[:, k, :], we2[:, k, :], start=(k == 0), stop=(k == KD - 1))
                last.then_inc(fp_ps, 1)
                pe.wait_ge(fp_ready, 1)
                for k in range(KD):
                    last = tr(misc(P, 288 + 2 * k, 290 + 2 * k), fpw[:, 0, k * P:(k + 1) * P], ident[0:B, 0:B])
                last.then_inc(fpT_ps, 1)
                pe.wait_ge(ld_x, 48)
                for u, (b, hf, m) in enumerate(UNITS):
                    if u >= 4:
                        pe.wait_ge(qk_rest, u - 3)
                    t0 = b * T + hf * HALF
                    for k in range(KD):
                        last = mm(ring(u), wqkv[:, k, m * P:(m + 1) * P], xT[:, k, t0:t0 + HALF],
                                  start=(k == 0), stop=(k == KD - 1))
                    last.then_inc(qk_ps, 1)
                for tt in range(B * TT):
                    if tt >= 2:
                        pe.wait_ge(v_done, tt - 1)
                    for k in range(KD):
                        last = mm(PB[2][:, HALF * (tt % 2):HALF * (tt % 2) + D], xT[:, k, tt * P:(tt + 1) * P],
                                  wqkv[:, k, 2 * D:3 * D], start=(k == 0), stop=(k == KD - 1))
                    last.then_inc(v_ps, 1)
                pe.wait_ge(qk_rest, len(UNITS))
                for v in range(KD * N // HALF):
                    e, n = v % KD, v // KD
                    if v >= 4:
                        pe.wait_ge(c1_done, v - 3)
                    for k in range(KD):
                        last = mm(ring(v), wc1x[:, k, e * P:(e + 1) * P], xT[:, k, n * HALF:(n + 1) * HALF],
                                  start=(k == 0), stop=(k == KD - 1))
                    last.then_inc(c1_ps, 1)
                pe.wait_ge(fpT_ready, 1)
                pe.wait_ge(ld_pe, 16)
                pe.wait_ge(v_done, B * TT)
                for n in range(T // HALF):
                    for k in range(KD):
                        last = mm(PB[2][0:B, n * HALF:(n + 1) * HALF], fpT[:, k, :], peT[:, k, n * HALF:(n + 1) * HALF],
                                  start=(k == 0), stop=(k == KD - 1))
                last.then_inc(fa_ps, 1)
                pe.wait_ge(c1_done, KD * N // HALF)
                pe.wait_ge(xs_ready, KD * B)
                for b in range(B):
                    for k in range(KD):
                        last = mm(PB[1][:, HALF + b * D:HALF + (b + 1) * D], xsB[:, k, b, :], wqkv[:, k, 2 * D:3 * D],
                                  start=(k == 0), stop=(k == KD - 1))
                last.then_inc(vs_ps, 1)
                for tt in range(B * TT):
                    for k in range(KD):
                        last = mm(PB[3][:, tt * H0:(tt + 1) * H0], c1T[:, k, tt * P:(tt + 1) * P], wc2[:, k, :],
                                  start=(k == 0), stop=(k == KD - 1))
                last.then_inc(z_ps, 1)
                pe.wait_ge(fa_ready, 1)
                for it in range(TT):
                    last = tr(misc(P, 320 + 2 * it, 322 + 2 * it), faw[:, 2, it * P:(it + 1) * P], ident[0:B, 0:B])
                last.then_inc(faT_ps, 1)


def stage_attention0(nc, G, A):
    with ExitStack() as ctx:
        sb = lambda n, s, dt=F32: ctx.enter_context(nc.sbuf_tensor(n, s, dt))
        sem = lambda n: ctx.enter_context(nc.semaphore(n))
        PB, scr, ident = G["PB"], G["scr"], G["ident"]
        GB = H0 // HG
        qa = [sb(f"a_qa{s}", [KA, HG, T], BF16) for s in range(GB)]
        ka = [sb(f"a_ka{s}", [KA, HG, T], BF16) for s in range(GB)]
        vst = [sb(f"a_vst{s}", [P, TT, HG, 32]) for s in range(2)]
        pt = [sb(f"a_pt{s}", [P, HG, HALF]) for s in range(2)]
        mx = [sb(f"a_mx{s}", [P, HG * TT, 2]) for s in range(2)]
        mcol = [sb(f"a_mcol{s}", [P, HG * TT]) for s in range(2)]
        mrow = [sb(f"a_mrow{s}", [HG * TT, 3, P], BF16) for s in range(2)]
        mrest = [sb(f"a_mrest{s}", [HG * TT, P]) for s in range(2)]
        passed = G["passed"]
        consts, staged = sem("a_consts"), [sem(f"a_staged{s}") for s in range(GB)]
        shifted = [sem(f"a_shifted{s}") for s in range(GB)]
        v_in, st_ps, p_ready, pv_done = sem("a_v_in"), sem("a_st_ps"), sem("a_p_ready"), sem("a_pv_done")
        o_out = [sem("a_o_out0"), sem("a_o_out1")]
        max_ps, max_done, m_ready, m_rows, row_step, row_ready = (sem(n) for n in (
            "a_max_ps", "a_max_done", "a_m_ready", "a_m_rows", "a_row_step", "a_row_ready"))
        STEPS = 2 * TT
        MU = HG * TT * 2
        SHARE = 5
        DMAS = 16 * len(Q_PART) * 2
        OT = G["OT"]

        mbank = (PB[3][:, 0:HALF], PB[3][:, HALF:T], PB[2][:, HALF:T])
        MB = len(mbank)

        def following(b, k):
            return (b, k + 1) if k + 1 < GB else (1 - b, 0)

        with nc.Block() as block:
            @block.sync
            def _(sp):
                def stage(slot, b, k):
                    for s, (dst, which) in enumerate(((qa, Q_PART), (ka, K_PART))):
                        for c, part in enumerate(which):
                            r0 = k * HG * HD0
                            src = scr[s, part, r0:r0 + HG * HD0, ds(b * T, T)].rearrange("(h p) t -> p h t", p=HD0)
                            sp.dma_start(dst[slot][c * HD0:(c + 1) * HD0, :, :], src).then_inc(staged[slot], 16)

                def shift_rows(slot, par, count):
                    sp.wait_ge(row_ready, count)
                    for c in range(3):
                        sp.dma_start(qa[slot][KS + c:KS + c + 1, :, :], mrow[par][:, c, :]).then_inc(shifted[slot], 16)

                for k in range(GB - 1):
                    stage(k, 0, k)
                shift_rows(0, 0, 1)
                with sp.Fori(0, B) as b:
                    for k in range(GB):
                        sp.wait_ge(pv_done, STEPS * (b * GB + k))
                        sp.sem_inc(passed, 1)
                        b3, k3 = (b, GB - 1) if k == 0 else (1 - b, k - 1)
                        stage(k3, b3, k3)
                        shift_rows((k + 1) % GB, (k + 1) % 2, b * GB + k + 2)
                for s in range(GB):
                    sp.wait_ge(staged[s], DMAS * (B + (s < GB - 1)))
                    sp.wait_ge(shifted[s], 48 * (B + (s == 0)))

            @block.gpsimd
            def _(pool):
                for s in range(GB):
                    nc.gpsimd.memset(ka[s][KS:KA, :, :], 1.0).then_inc(consts, 1)
                pool.wait_ge(consts, GB)
                for s in range(2):
                    nc.gpsimd.memset(vst[s][:, :, :, HD0:HD0 + 1], 1.0).then_inc(consts, 1)
                    nc.gpsimd.memset(vst[s][:, :, :, HD0 + 1:32], 0.0).then_inc(consts, 1)

                def stage_v(par, b, k):
                    w = HG * HD0
                    src = G["v"][:, ds(2 * b + k // 2, 1), :, (k % 2) * w:(k % 2 + 1) * w]
                    nc.gpsimd.tensor_copy(vst[par][:, :, :, 0:HD0],
                                          src.rearrange("p o j (h d) -> p (o j) h d", h=HG)).then_inc(v_in, 1)

                stage_v(0, 0, 0)
                with pool.Fori(0, B) as b:
                    for k in range(GB):
                        pool.wait_ge(pv_done, STEPS * (b * GB + k))
                        pool.sem_inc(passed, 1)
                        stage_v((k + 1) % 2, *following(b, k))

            @block.scalar
            def _(act):
                with act.Fori(0, B) as b:
                    for k in range(GB):
                        g = b * GB + k
                        for n in range(STEPS):
                            act.wait_ge(pv_done, STEPS * g + max(n - 1, 0))
                            for ab in range(2):
                                act.wait_ge(st_ps, 2 * STEPS * g + 2 * n + ab + 1)
                                nc.scalar.activation(pt[n % 2][:, 2 * ab:2 * ab + 2, :].rearrange("p h t -> p (h t)"),
                                                     PB[ab][:, :], ACT.Exp, scale=HD0 ** -0.5).then_inc(p_ready, 1)
                            if n == TT + 1:
                                act.wait_ge(pv_done, STEPS * g + TT)
                                nc.scalar.activation(OT[:, ds(g, 1), 0:HALF].rearrange("p o t -> p (o t)"),
                                                     PB[2][:, 0:HALF], ACT.Copy).then_inc(o_out[0], 1)

            @block.vector
            def _(dve):
                V = nc.vector

                def maxima(par, g, when=None):
                    for u in range(MU):
                        dve.wait_ge(max_ps, MU * g + u + 1)
                        V.reduce_max(mx[par][:, u // 2, u % 2:u % 2 + 1], mbank[u % MB], X).then_inc(max_done, 1)
                    dve.wait_ge(max_done, MU * (g + 1))
                    V.reduce_max(mcol[par][:, :], mx[par][:, :, :], X).then_inc(m_ready, 1)

                def rows(par, g, old):
                    if old is not None:
                        dve.wait_ge(*old)
                    dve.wait_ge(m_rows, g + 1)
                    src = PB[3][0:HG * TT, 0:P]
                    V.tensor_scalar_mul(mrow[par][:, 0, :], src, -1.0).then_inc(row_step, 1)
                    dve.wait_ge(row_step, 3 * g + 1)
                    V.scalar_tensor_tensor(out=mrest[par][:, :], in0=src, scalar=-1.0, in1=mrow[par][:, 0, :],
                                           op0=ALU.mult, op1=ALU.subtract).then_inc(row_step, 1)
                    dve.wait_ge(row_step, 3 * g + 2)
                    V.tensor_copy(mrow[par][:, 1, :], mrest[par][:, :]).then_inc(row_step, 1)
                    dve.wait_ge(row_step, 3 * g + 3)
                    V.tensor_tensor(mrow[par][:, 2, :], mrest[par][:, :], mrow[par][:, 1, :],
                                    ALU.subtract).then_inc(row_ready, 1)

                maxima(0, 0)
                rows(0, 0, None)
                with dve.Fori(0, B) as b:
                    for k in range(GB):
                        g, par = b * GB + k, (k + 1) % 2
                        maxima(par, g + 1)
                        rows(par, g + 1, (shifted[(k - 1) % GB], 48 * (b + 1) if k else 48 * b))
                        dve.wait_ge(pv_done, STEPS * g + STEPS)
                        V.tensor_copy(OT[:, ds(g, 1), HALF:T].rearrange("p o t -> p (o t)"),
                                      PB[2][:, 0:HALF]).then_inc(o_out[1], 1)

            @block.tensor
            def _(pe):
                mm = nc.tensor.matmul

                def max_unit(slot, u):
                    h, it, jh = u // (2 * TT), u // 2 % TT, u % 2
                    mm(mbank[u % MB], qa[slot][0:KS, h, it * P:(it + 1) * P],
                       ka[slot][0:KS, h, jh * HALF:(jh + 1) * HALF], start=True, stop=True).then_inc(max_ps, 1)

                def max_rows(par, g):
                    pe.wait_ge(m_ready, g + 1)
                    nc.tensor.transpose(PB[3][0:HG * TT, 0:P], mcol[par][:, :], ident[:, :]).then_inc(m_rows, 1)

                def weighted(k, g, n):
                    ih, jt = n // TT, n % TT
                    if jt == 0:
                        pe.wait_ge(o_out[1 - ih], g + ih)
                    pe.wait_ge(p_ready, 2 * STEPS * g + 2 * n + 2)
                    for q in range(HG):
                        last = mm(PB[2][32 * q:32 * q + 32, 0:HALF], vst[k % 2][:, jt, q, :],
                                  pt[n % 2][:, q, :], start=(jt == 0), stop=(jt == TT - 1))
                    last.then_inc(pv_done, 1)

                pe.wait_ge(consts, GB + 4)
                pe.wait_ge(staged[0], DMAS)
                for u in range(MU):
                    if u >= MB:
                        pe.wait_ge(max_done, u - MB + 1)
                    max_unit(0, u)
                max_rows(0, 0)
                with pe.Fori(0, B) as b:
                    for k in range(GB):
                        g, nxt = b * GB + k, (k + 1) % GB
                        pe.wait_ge(shifted[k], 48 * (b + 1))
                        pe.wait_ge(v_in, g + 1)
                        units = iter(range(MU))

                        def maxima(count):
                            for u in itertools.islice(units, count):
                                pe.wait_ge(max_done, MU * (g + 1) + max(u - MB + 1, 0))
                                max_unit(nxt, u)

                        for n in range(STEPS):
                            ih, jt = n // TT, n % TT
                            for ab in range(2):
                                pe.wait_ge(p_ready, 2 * STEPS * g + (2 * n + ab - 1 if n else 0))
                                for q in (2 * ab, 2 * ab + 1):
                                    last = mm(PB[ab][:, (q % 2) * HALF:(q % 2 + 1) * HALF], ka[k][:, q, jt * P:(jt + 1) * P],
                                              qa[k][:, q, ih * HALF:(ih + 1) * HALF], start=True, stop=True)
                                last.then_inc(st_ps, 1)
                                if n == 0 and ab == 0:
                                    pe.wait_ge(staged[nxt], DMAS * (b + 1) if k < GB - 1 else DMAS * (b + 2))
                                    pe.wait_ge(row_ready, g + 1)
                                maxima(1)
                            maxima(1)
                            if n >= 1:
                                weighted(k, g, n - 1)
                            maxima(SHARE - 3)
                            if n == STEPS - 2:
                                max_rows((k + 1) % 2, g + 1)
                        weighted(k, g, STEPS - 1)


def stage_out0(nc, G, A):
    with ExitStack() as ctx:
        sb = lambda n, s, dt=F32: ctx.enter_context(nc.sbuf_tensor(n, s, dt))
        sem = lambda n: ctx.enter_context(nc.semaphore(n))
        PB, ident, OT = G["PB"], G["ident"], G["OT"]
        wout = sb("o_wout", [P, KD, D])
        bout = sb("o_bout", [P, KD])
        boutB = sb("o_boutB", [P, D])
        outT = sb("o_outT", [P, KD, N])
        dg = sb("o_dg", [P, 2, 2, H0])
        ot = sb("o_ot", [P, 2, D])
        og = sb("o_og", [P, 2, D])
        csum = sb("o_csum", [P, KD, B])
        ld, t1_ps, ot_step, og_ready, t2_ps, outT_ready, x0_ps, x0_done, xt_ps, xt_done = (sem("o_" + n) for n in (
            "ld", "t1_ps", "ot_step", "og_ready", "t2_ps", "outT_ready", "x0_ps", "x0_done", "xt_ps", "xt_done"))
        TILES = B * TT

        with nc.Block() as block:
            @block.sync
            def _(sp):
                sp.dma_start(wout[:, :, :], A["woutT"].rearrange("(k p) n -> p k n", p=P)).then_inc(ld, 16)
                sp.dma_start(bout[:, :], A["bout"]).then_inc(ld, 16)
                sp.dma_start(boutB[:, :], A["boutB"]).then_inc(ld, 16)

            @block.tensor
            def _(pe):
                mm, tr = nc.tensor.matmul, nc.tensor.transpose
                pe.wait_ge(ld, 48)
                for i in range(TILES + 2):
                    if i < TILES:
                        if i >= 2:
                            pe.wait_ge(og_ready, i - 1)
                        b, it = i // TT, i % TT
                        for hg in range(4):
                            last = tr(PB[0][:, HALF * (i % 2) + hg * P:HALF * (i % 2) + (hg + 1) * P],
                                      OT[:, 4 * b + hg, it * P:(it + 1) * P], ident[:, :])
                        last.then_inc(t1_ps, 1)
                    if 1 <= i <= TILES:
                        t = i - 1
                        pe.wait_ge(og_ready, t + 1)
                        if t >= 2:
                            pe.wait_ge(outT_ready, t - 1)
                        for k in range(KD):
                            last = tr(PB[1][:, HALF * (t % 2) + k * P:HALF * (t % 2) + (k + 1) * P],
                                      og[:, t % 2, k * P:(k + 1) * P], ident[:, :])
                        last.then_inc(t2_ps, 1)
                    if i >= 2:
                        t = i - 2
                        pe.wait_ge(outT_ready, t + 1)
                        if t >= 2:
                            pe.wait_ge(x0_done, t - 1)
                        for k in range(KD):
                            last = mm(PB[2][:, HALF * (t % 2):HALF * (t % 2) + D], outT[:, k, t * P:(t + 1) * P],
                                      wout[:, k, :], start=(k == 0), stop=(k == KD - 1))
                        last.then_inc(x0_ps, 1)
                        if t % 4 == 3:
                            n = t // 4
                            for m in range(KD):
                                if n >= 1:
                                    pe.wait_ge(xt_done, KD * (n - 1) + m + 1)
                                for k in range(KD):
                                    last = mm(PB[3][:, m * HALF:(m + 1) * HALF], wout[:, k, m * P:(m + 1) * P],
                                              outT[:, k, n * HALF:(n + 1) * HALF], start=(k == 0), stop=(k == KD - 1))
                                last.then_inc(xt_ps, 1)

            def project(act, n):
                for m in range(KD):
                    act.wait_ge(xt_ps, KD * n + m + 1)
                    nc.scalar.activation(G["X0T"][:, m, n * HALF:(n + 1) * HALF], PB[3][:, m * HALF:(m + 1) * HALF],
                                         ACT.Identity, bias=bout[:, m:m + 1]).then_inc(xt_done, 1)

            @block.scalar
            def _(act):
                act.wait_ge(ld, 48)
                for t in range(TILES):
                    act.wait_ge(t2_ps, t + 1)
                    nc.scalar.activation(outT[:, :, t * P:(t + 1) * P],
                                         PB[1][:, HALF * (t % 2):HALF * (t % 2) + D].rearrange("p (k t) -> p k t", k=KD),
                                         ACT.Copy).then_inc(outT_ready, 1)
                    if t % 4 == 0 and t >= 4:
                        project(act, t // 4 - 1)
                project(act, TILES // 4 - 1)

            @block.vector
            def _(dve):
                V = nc.vector
                dve.wait_ge(ld, 48)
                link = chain(dve, ot_step)
                for t in range(TILES + 1):
                    if t < TILES:
                        b, it, s = t // TT, t % TT, t % 2
                        dve.wait_ge(t1_ps, t + 1)
                        if t >= 2:
                            dve.wait_ge(t2_ps, t - 1)
                        heads = PB[0][:, HALF * s:HALF * s + HALF].rearrange("p (h r) -> p h r", r=32)
                        link(V.tensor_tensor(dg[:, s, 0, :], heads[:, :, HD0], G["gate"][:, t * H0:(t + 1) * H0], ALU.mult))
                        link(V.reciprocal(dg[:, s, 1, :], dg[:, s, 0, :]))
                        link(V.tensor_tensor(ot[:, s, :].rearrange("p (h d) -> p h d", d=HD0), heads[:, :, 0:HD0],
                                             dg[:, s, 1, :].unsqueeze(2).to_broadcast([P, H0, HD0]), ALU.mult))
                        V.scalar_tensor_tensor(out=og[:, s, :], in0=G["vsum"][:, b, :], scalar=G["fa"][:, it, b:b + 1],
                                               in1=ot[:, s, :], op0=ALU.mult, op1=ALU.add).then_inc(og_ready, 1)
                    if t >= 1:
                        r = t - 1
                        dve.wait_ge(x0_ps, r + 1)
                        V.tensor_tensor(G["X0"][:, r, :], PB[2][:, HALF * (r % 2):HALF * (r % 2) + D], boutB[:, :],
                                        ALU.add).then_inc(x0_done, 1)
                dve.wait_ge(xt_done, KD * TILES // 4)
                for k in range(KD):
                    link(V.reduce_sum(csum[:, k, :], G["X0T"][:, k, :].rearrange("p (b t) -> p b t", b=B), X))
                V.tensor_scalar_mul(G["csum"][:, :, :], csum[:, :, :], 0.5)


def stage_moe(nc, G, A):
    with ExitStack() as ctx:
        sb = lambda n, s, dt=F32: ctx.enter_context(nc.sbuf_tensor(n, s, dt))
        sem = lambda n: ctx.enter_context(nc.semaphore("f_" + n))
        PB, ident, X0T, X0 = G["PB"], G["ident"], G["X0T"], G["X0"]
        TILES = B * TT
        NT = CS // P
        phi = sb("f_phi", [P, KD, SLOTS])
        wex = sb("f_wex", [P, CE, KD, D])
        bex = sb("f_bex", [P, NT, D])
        l1s = sb("f_l1s", [P, 2, CS])
        dl = sb("f_dl", [P, 2, CS])
        th = sb("f_th", [P, 2, CS])
        E = sb("f_E", [P, TILES, CS])
        ET = sb("f_ET", [P, 2, NT, P])
        slT = sb("f_slT", [P, B, KD, CS])
        ysb = sb("f_ysb", [P, NT, B, D])
        mc = sb("f_mc", [P, TILES])
        nmc = sb("f_nmc", [P, TILES])
        dc = sb("f_dc", [P, TILES])
        mrun = sb("f_mrun", [P, 2, TILES])
        arg = sb("f_arg", [P, 2, TILES])
        fac = sb("f_fac", [P, 2, TILES])
        dtmp = sb("f_dtmp", [P, 2, TILES])
        passed = G["passed"]
        ld_phi, w_in, init = sem("ld_phi"), sem("w_in"), sem("init")
        lg_ps, l1_sb, mx_done, neg_done, dl_done, e_done, th_done, sl_done = (sem(n) for n in (
            "lg_ps", "l1_sb", "mx_done", "neg_done", "dl_done", "e_done", "th_done", "sl_done"))
        sl_out, et_ps, et_out, y_ps, y_out, oc_ps, oc_out = (sem(n) for n in (
            "sl_out", "et_ps", "et_out", "y_ps", "y_out", "oc_ps", "oc_out"))
        run_step, run_arg, run_fac = sem("run_step"), sem("run_arg"), sem("run_fac")
        LW = 48
        O, DEN = G["O"], G["den"]

        with nc.Block() as block:
            @block.sync
            def _(sp):
                for k in range(KD):
                    sp.dma_start(phi[:, k, :], A["phi"][k * P:(k + 1) * P, :]).then_inc(ld_phi, 16)
                sp.dma_start(G["x1T"][:, :, :], A["xT"].rearrange("(k p) n -> p k n", p=P)).then_inc(G["ld_x1"], 16)
                with sp.Fori(0, CH) as c:
                    sp.wait_ge(y_ps, NT * c)
                    sp.wait_ge(y_out, NT * c)
                    sp.sem_inc(passed, 1)
                    for k in range(KD):
                        sp.dma_start(wex[:, :, k, :], A["W"][ds(c * CE, CE), k * P:(k + 1) * P, :]
                                     .rearrange("n p e -> p n e")).then_inc(w_in, 16)
                    sp.dma_start(bex[:, :, :], A["bexp"][ds(c * CS, CS), :]
                                 .rearrange("(t p) e -> p t e", p=P)).then_inc(w_in, 16)

            @block.gpsimd
            def _(pool):
                nc.gpsimd.memset(O[:, :, :], 0.0).then_inc(init, 1)
                nc.gpsimd.memset(DEN[:, :], 0.0).then_inc(init, 1)
                nc.gpsimd.memset(mrun[:, 0, :], LOWEST).then_inc(init, 1)

            @block.tensor
            def _(pe):
                mm, tr = nc.tensor.matmul, nc.tensor.transpose
                pe.wait_ge(ld_phi, 16 * KD)
                with pe.Fori(0, CH) as c:
                    def dispatch(mt):
                        pe.wait_ge(th_done, TT * c + mt + 1)
                        for b in range(B):
                            for k in range(KD):
                                last = mm(PB[2 + b][:, k * HALF:(k + 1) * HALF], X0[:, b * TT + mt, k * P:(k + 1) * P],
                                          th[:, mt % 2, :], start=(mt == 0), stop=(mt == TT - 1))
                        last.then_inc(sl_done, 1)

                    def expo_rows(t):
                        for n in range(NT):
                            last = tr(PB[0][:, HALF * (t % 2) + n * P:HALF * (t % 2) + (n + 1) * P],
                                      E[:, t, n * P:(n + 1) * P], ident[:, :])
                        last.then_inc(et_ps, 1)

                    for mt in range(TT):
                        if mt < 2:
                            pe.wait_ge(et_out, TILES * c)
                            pe.wait_ge(oc_out, TILES * c)
                        else:
                            pe.wait_ge(e_done, TT * c + mt - 1)
                            pe.wait_ge(dl_done, TT * c + mt - 1)
                        for b in range(B):
                            for k in range(KD):
                                last = mm(PB[mt % 2][:, b * HALF:(b + 1) * HALF],
                                          X0T[:, k, b * T + mt * P:b * T + (mt + 1) * P], phi[:, k, ds(c * CS, CS)],
                                          start=(k == 0), stop=(k == KD - 1))
                        last.then_inc(lg_ps, 1)
                        if mt == 0:
                            pe.wait_ge(y_out, NT * c)
                        else:
                            dispatch(mt - 1)
                    dispatch(TT - 1)
                    pe.wait_ge(e_done, TT * c + TT)
                    pe.wait_ge(dl_done, TT * c + TT)
                    expo_rows(0)
                    expo_rows(1)
                    pe.wait_ge(sl_out, B * KD * (c + 1))
                    pe.wait_ge(w_in, LW * (c + 1))
                    for n in range(NT):
                        for b in range(B):
                            for k in range(KD):
                                for q in range(4):
                                    s0 = n * P + 32 * q
                                    last = mm(PB[2 + n // 2][32 * q:32 * q + 32, (n % 2) * HALF + b * D:(n % 2) * HALF + (b + 1) * D],
                                              slT[:, b, k, s0:s0 + 32], wex[:, 4 * n + q, k, :],
                                              start=(k == 0), stop=(k == KD - 1))
                        last.then_inc(y_ps, 1)
                    pe.wait_ge(y_out, NT * (c + 1))
                    for t in range(TILES):
                        pe.wait_ge(et_out, TILES * c + t + 1)
                        if t >= 2:
                            pe.wait_ge(oc_out, TILES * c + t - 1)
                        for n in range(NT):
                            last = mm(PB[1][:, HALF * (t % 2):HALF * (t % 2) + D], ET[:, t % 2, n, :],
                                      ysb[:, n, t // TT, :], start=(n == 0), stop=(n == NT - 1))
                        last.then_inc(oc_ps, 1)
                        if t + 2 < TILES:
                            expo_rows(t + 2)

            @block.scalar
            def _(act):
                S = nc.scalar.activation
                act.wait_ge(init, 3)
                with act.Fori(0, CH) as c:
                    for mt in range(TT):
                        s, a = mt % 2, TT * c + mt
                        act.wait_ge(lg_ps, a + 1)
                        act.wait_ge(dl_done, TT * c + max(mt - 1, 0))
                        S(l1s[:, s, :], PB[s][:, HALF:2 * HALF], ACT.Copy).then_inc(l1_sb, 1)
                        act.wait_ge(neg_done, a + 1)
                        act.wait_ge(dl_done, a + 1)
                        for b in range(B):
                            t = b * TT + mt
                            last = S(E[:, t, :], PB[s][:, b * HALF:(b + 1) * HALF], ACT.Exp, bias=nmc[:, t:t + 1],
                                     accum_out=dc[:, t:t + 1])
                        last.then_inc(e_done, 1)
                        act.wait_ge(sl_done, TT * c + max(mt - 1, 0))
                        S(th[:, s, :], dl[:, s, :], ACT.Tanh, scale=0.5).then_inc(th_done, 1)
                    act.wait_ge(run_arg, c + 1)
                    S(fac[:, :, :], arg[:, :, :], ACT.Exp).then_inc(run_fac, 1)
                    act.wait_ge(sl_done, TT * (c + 1))
                    for b in range(B):
                        for k in range(KD):
                            S(slT[:, b, k, :], PB[2 + b][:, k * HALF:(k + 1) * HALF], ACT.Identity,
                              bias=G["csum"][:, k, b:b + 1], scale=0.5 - b).then_inc(sl_out, 1)
                    for t in range(TILES):
                        act.wait_ge(et_ps, TILES * c + t + 1)
                        act.wait_ge(oc_ps, TILES * c + max(t - 1, 0))
                        S(ET[:, t % 2, :, :].rearrange("p n m -> p (n m)"), PB[0][:, HALF * (t % 2):HALF * (t % 2) + HALF],
                          ACT.Copy).then_inc(et_out, 1)

            @block.vector
            def _(dve):
                V = nc.vector
                dve.wait_ge(init, 3)
                with dve.Fori(0, CH) as c:
                    for mt in range(TT):
                        s, a = mt % 2, TT * c + mt
                        dve.wait_ge(l1_sb, a + 1)
                        pair = mc[:, :].rearrange("p (b t) -> p b t", b=B)[:, :, mt]
                        npair = nmc[:, :].rearrange("p (b t) -> p b t", b=B)[:, :, mt]
                        V.reduce_max(pair, PB[s][:, :].rearrange("p (b n) -> p b n", b=B), X).then_inc(mx_done, 1)
                        dve.wait_ge(th_done, TT * c + max(mt - 1, 0))
                        V.tensor_tensor(dl[:, s, :], PB[s][:, 0:HALF], l1s[:, s, :], ALU.subtract).then_inc(dl_done, 1)
                        dve.wait_ge(mx_done, a + 1)
                        V.tensor_scalar_mul(npair, pair, -1.0).then_inc(neg_done, 1)
                    link = chain(dve, run_step, 7 * c)
                    link(V.tensor_tensor(mrun[:, 1, :], mrun[:, 0, :], mc[:, :], ALU.max))
                    link(V.tensor_tensor(arg[:, 0, :], mrun[:, 0, :], mrun[:, 1, :], ALU.subtract))
                    V.tensor_tensor(arg[:, 1, :], mc[:, :], mrun[:, 1, :], ALU.subtract).then_inc(run_arg, 1)
                    link(V.tensor_copy(mrun[:, 0, :], mrun[:, 1, :]))
                    dve.wait_ge(run_fac, c + 1)
                    link(V.tensor_tensor(dtmp[:, 0, :], DEN[:, :], fac[:, 0, :], ALU.mult))
                    link(V.tensor_tensor(dtmp[:, 1, :], dc[:, :], fac[:, 1, :], ALU.mult))
                    link(V.tensor_tensor(DEN[:, :], dtmp[:, 0, :], dtmp[:, 1, :], ALU.add))
                    link(V.tensor_tensor(O[:, :, :], O[:, :, :], fac[:, 0, :].unsqueeze(2).to_broadcast([P, TILES, D]),
                                         ALU.mult))
                    dve.wait_ge(w_in, LW * (c + 1))
                    for n in range(NT):
                        dve.wait_ge(y_ps, NT * c + n + 1)
                        V.tensor_tensor(ysb[:, n, :, :],
                                        PB[2 + n // 2][:, (n % 2) * HALF:(n % 2 + 1) * HALF].rearrange("p (b e) -> p b e", b=B),
                                        bex[:, n, :].unsqueeze(1).to_broadcast([P, B, D]), ALU.add).then_inc(y_out, 1)
                    for t in range(TILES):
                        dve.wait_ge(oc_ps, TILES * c + t + 1)
                        V.scalar_tensor_tensor(out=O[:, t, :], in0=PB[1][:, HALF * (t % 2):HALF * (t % 2) + D],
                                               scalar=fac[:, 1, t:t + 1], in1=O[:, t, :], op0=ALU.mult,
                                               op1=ALU.add).then_inc(oc_out, 1)
                    dve.wait_ge(oc_out, TILES * (c + 1))


def load_attention1(sp, G, A, l):
    sp.dma_start(G["wqkv1"][:, :, :], A["wqkv1"][l].rearrange("(k p) n -> p k n", p=P)).then_inc(G["ld_att"], 16)
    sp.dma_start(G["wo"][:, :, :], A["wo"][l].rearrange("(k p) n -> p k n", p=P)).then_inc(G["ld_att"], 16)


def load_ffn1(sp, G, A, l):
    sp.dma_start(G["w1"][:, :, :], A["w1"][l].rearrange("(k p) n -> p k n", p=P)).then_inc(G["ld_ffn"], 16)
    sp.dma_start(G["w2"][:, :, :], A["w2"][l].rearrange("(k p) n -> p k n", p=P)).then_inc(G["ld_ffn"], 16)
    for name in ("lg", "lb", "b1", "b2"):
        sp.dma_start(G[name][:, :], A[name][l]).then_inc(G["ld_ffn"], 16)


LD_ATT, LD_FFN = 32, 96


def stage_rotate(nc, G, A):
    with ExitStack() as ctx:
        sb = lambda n, s, dt=F32: ctx.enter_context(nc.sbuf_tensor(n, s, dt))
        sem = lambda n: ctx.enter_context(nc.semaphore("r_" + n))
        PB, ident, x1T, xr = G["PB"], G["ident"], G["x1T"], G["xr"]
        TILES = B * TT
        rden = sb("r_rden", [P, TILES])
        on = sb("r_on", [P, 2, D])
        step, on_ready, t_ps, x1_done, rot_ps, rot_out, zeroed = (sem(n) for n in (
            "step", "on_ready", "t_ps", "x1_done", "rot_ps", "rot_out", "zeroed"))
        with nc.Block() as block:
            @block.sync
            def _(sp):
                load_attention1(sp, G, A, 0)
                sp.dma_start(G["mask"][:, :], A["mask"]).then_inc(G["ld_tab"], 16)
                sp.dma_start(G["qks"][:, :, :, :], A["qks"]).then_inc(G["ld_tab"], 16)

            @block.gpsimd
            def _(pool):
                nc.gpsimd.memset(xr[:, :, :, 0:1], 0.0).then_inc(zeroed, 1)

            @block.vector
            def _(dve):
                V = nc.vector
                link = chain(dve, step)
                link(V.reciprocal(rden[:, :], G["den"][:, :]))
                dve.wait_ge(G["ld_x1"], 16)
                for t in range(TILES + 1):
                    if t < TILES:
                        if t >= 2:
                            dve.wait_ge(t_ps, t - 1)
                        V.tensor_scalar_mul(on[:, t % 2, :], G["O"][:, t, :], rden[:, t:t + 1]).then_inc(on_ready, 1)
                    if t >= 1:
                        r = t - 1
                        dve.wait_ge(t_ps, r + 1)
                        V.tensor_tensor(x1T[:, :, r * P:(r + 1) * P],
                                        PB[0][:, HALF * (r % 2):HALF * (r % 2) + D].rearrange("p (k t) -> p k t", k=KD),
                                        x1T[:, :, r * P:(r + 1) * P], ALU.add).then_inc(x1_done, 1)

            @block.tensor
            def _(pe):
                for t in range(TILES):
                    pe.wait_ge(on_ready, t + 1)
                    if t >= 2:
                        pe.wait_ge(x1_done, t - 1)
                    for k in range(KD):
                        last = nc.tensor.transpose(PB[0][:, HALF * (t % 2) + k * P:HALF * (t % 2) + (k + 1) * P],
                                                   on[:, t % 2, k * P:(k + 1) * P], ident[:, :])
                    last.then_inc(t_ps, 1)
                for n in range(N // HALF):
                    pe.wait_ge(x1_done, 4 * n + 4)
                    for m in range(KD):
                        if n >= 1:
                            pe.wait_ge(rot_out, KD * (n - 1) + m + 1)
                        for k in range(KD):
                            last = nc.tensor.matmul(PB[1 + m][:, 0:HALF], G["rot"][:, k, m * P:(m + 1) * P],
                                                    x1T[:, k, n * HALF:(n + 1) * HALF], start=(k == 0), stop=(k == KD - 1))
                        last.then_inc(rot_ps, 1)

            @block.scalar
            def _(act):
                for n in range(N // HALF):
                    for m in range(KD):
                        act.wait_ge(rot_ps, KD * n + m + 1)
                        c0 = 1 + (n % 2) * HALF
                        nc.scalar.activation(xr[:, m, n // 2, c0:c0 + HALF], PB[1 + m][:, 0:HALF],
                                             ACT.Copy).then_inc(rot_out, 1)
                act.wait_ge(zeroed, 1)


def stage_attention1(nc, G, A, l):
    with ExitStack() as ctx:
        sb = lambda n, s, dt=F32: ctx.enter_context(nc.sbuf_tensor(f"w{l}_{n}", s, dt))
        sem = lambda n: G["layer_sem"](f"w_{n}")
        PB, ident, xr, mask = G["PB"], G["ident"], G["xr"], G["mask"]
        wqkv, wo = G["wqkv1"], G["wo"]
        tab = [sb(f"tab{i}", [P, NW, HD1]) for i in range(4)]
        qkr = sb("qkr", [P, NW, 2 * INNER])
        vsb = sb("vsb", [P, NW, INNER])
        ss = sb("ss", [P, NW, 2 * H1])
        nrm = sb("nrm", [P, NW, 2 * H1])
        rn = sb("rn", [P, NW, 2 * H1])
        cosp = sb("cosp", [P, 2 * INNER])
        sinp = sb("sinp", [P, 2 * INNER])
        turned = sb("turned", [P, 2, 2 * INNER])
        kT = sb("kT", [P, HP, T])
        qz = sb("qz", [P, 2, HP, 2, P])
        sm = sb("sm", [P, 2, H1, 2 * WIN])
        sq = sm[:, 1, 0:4, :].rearrange("p h n -> p (h n)")
        PT = sb("PT", [P, 2, 4, P])
        oT = sb("oT", [P, HP, T])
        hst = oT[:, 0:KD, :]
        st = sb("st", [P, 2, 4, H1])
        (ld_tab, tabs, zeroed, h_ready, qk_ps, v_ps, qk_sb, v_sb, sq_done, ss_done, n_sqrt, n_step) = (sem(n) for n in (
            "ld_tab", "tabs", "zeroed", "h_ready", "qk_ps", "v_ps", "qk_sb", "v_sb", "sq_done", "ss_done", "n_sqrt", "n_step"))
        (qn_done, cos_done, sin_done, turn_done, tq_ps, tk_ps, qz_done, kT_done, s_ps, s_masked, m_done, e_done,
         d_done, p_done, pt_ps, pt_act, pt_dve, pv_ps, oT_done, wo_ps, wo_done) = (sem(n) for n in (
            "qn_done", "cos_done", "sin_done", "turn_done", "tq_ps", "tk_ps", "qz_done", "kT_done", "s_ps", "s_masked",
            "m_done", "e_done", "d_done", "p_done", "pt_ps", "pt_act", "pt_dve", "pv_ps", "oT_done", "wo_ps", "wo_done"))
        passed = G["passed"]
        C = HD1 // 2
        NN = NW // 2

        def keys(w):
            return slice(0, 2 * WIN) if w else slice(WIN, 2 * WIN)

        with nc.Block() as block:
            @block.sync
            def _(sp):
                for i in range(4):
                    sp.dma_start(tab[i][:, :, :], A["tables"][i].rearrange("(w p) d -> p w d", p=P)).then_inc(ld_tab, 16)
                load_ffn1(sp, G, A, l)

            @block.gpsimd
            def _(pool):
                V = nc.gpsimd
                for s in range(2):
                    V.memset(qz[64:128, s, :, 0, :], 0.0).then_inc(zeroed, 1)
                    V.memset(qz[0:64, s, :, 1, :], 0.0).then_inc(zeroed, 1)
                pool.wait_ge(zeroed, 4 * (l + 1))
                pool.wait_ge(ld_tab, 16 * 4 * (l + 1))
                pool.wait_ge(G["ld_tab"], 32)
                for i in range(4):
                    V.tensor_tensor(tab[i][:, :, :], tab[i][:, :, :],
                                    G["qks"][:, l, i, :].unsqueeze(1).to_broadcast([P, NW, HD1]), ALU.mult).then_inc(tabs, 1)
                pool.wait_ge(tabs, 4 * (l + 1))
                with pool.Fori(l * B, (l + 1) * B) as b:
                    def turn(w):
                        pool.wait_ge(qn_done, NW * b + w + 1)
                        pool.wait_ge(turn_done, NW * b + w)
                        for j in range(2):
                            V.tensor_tensor(
                                cosp[:, j * INNER:(j + 1) * INNER].rearrange("p (h d) -> p h d", d=HD1),
                                qkr[:, w, j * INNER:(j + 1) * INNER].rearrange("p (h d) -> p h d", d=HD1),
                                tab[2 * j][:, w, :].unsqueeze(1).to_broadcast([P, H1, HD1]), ALU.mult).then_inc(cos_done, 1)

                    def probabilities(w, j):
                        hs = slice(4 * j, 4 * j + 4)
                        pool.wait_ge(d_done, 2 * (NW * b + w) + j + 1)
                        V.tensor_tensor(sm[:, w % 2, hs, keys(w)], sm[:, w % 2, hs, keys(w)],
                                        st[:, w % 2, 3, hs].unsqueeze(2).to_broadcast([P, 4, 2 * WIN if w else WIN]),
                                        ALU.mult).then_inc(p_done, 1)

                    turn(0)
                    for i in range(NW + 2):
                        if i >= 2:
                            probabilities(i - 2, 1)
                        if i + 1 < NW:
                            turn(i + 1)
                        if 1 <= i <= NW:
                            probabilities(i - 1, 0)

            @block.tensor
            def _(pe):
                mm, tr = nc.tensor.matmul, nc.tensor.transpose
                pe.wait_ge(G["ld_att"], LD_ATT * (l + 1))
                pe.wait_ge(zeroed, 4 * (l + 1))
                with pe.Fori(l * B, (l + 1) * B) as b:
                    pe.wait_ge(h_ready, KD * (b + 1))
                    pe.wait_ge(oT_done, NW * b)
                    pe.wait_ge(wo_done, 2 * KD * b)
                    pe.wait_ge(pt_act, 2 * NW * b)
                    pe.wait_ge(pt_dve, 2 * NW * b)
                    for w in range(NW):
                        if w >= 2:
                            pe.wait_ge(sq_done, NW * b + w - 1)
                        for j in range(2):
                            for k in range(KD):
                                last = mm(PB[w % 2][:, j * HALF:(j + 1) * HALF], hst[:, k, w * P:(w + 1) * P],
                                          wqkv[:, k, j * INNER:(j + 1) * INNER], start=(k == 0), stop=(k == KD - 1))
                        last.then_inc(qk_ps, 1)
                        if w >= 2:
                            pe.wait_ge(v_sb, NW * b + w - 1)
                        for k in range(KD):
                            last = mm(PB[2][:, (w % 2) * HALF:(w % 2 + 1) * HALF], hst[:, k, w * P:(w + 1) * P],
                                      wqkv[:, k, 2 * INNER:3 * INNER], start=(k == 0), stop=(k == KD - 1))
                        last.then_inc(v_ps, 1)

                    def to_rows(w):
                        pe.wait_ge(turn_done, NW * b + w + 1)
                        if w == 0:
                            pe.wait_ge(sq_done, NW * (b + 1))
                        if w >= 3:
                            pe.wait_ge(oT_done, NW * b + w - 2)
                        if w >= 1:
                            pe.wait_ge(qz_done, NW * b + w)
                        for p in range(HP):
                            last = tr(PB[0][:, p * P:(p + 1) * P], turned[:, w % 2, p * P:(p + 1) * P], ident[:, :])
                        last.then_inc(tq_ps, 1)
                        if w >= 1:
                            pe.wait_ge(kT_done, NW * b + w)
                        for p in range(HP):
                            last = tr(PB[0][:, HALF + p * P:HALF + (p + 1) * P],
                                      turned[:, w % 2, INNER + p * P:INNER + (p + 1) * P], ident[:, :])
                        last.then_inc(tk_ps, 1)

                    def scores(w):
                        pe.wait_ge(qz_done, NW * b + w + 1)
                        pe.wait_ge(kT_done, NW * b + w + 1)
                        if w == 0:
                            pe.wait_ge(v_sb, NW * (b + 1))
                        k0 = (w - 1) * WIN if w else 0
                        for h in range(H1):
                            if h % 2 == 0 and w >= 1:
                                pe.wait_ge(s_masked, H1 * (NW * b + w - 1) + h + 2)
                            c0 = (h % 4) * 2 * WIN + keys(w).start
                            n = keys(w).stop - keys(w).start
                            mm(PB[1 + h // 4][:, c0:c0 + n], qz[:, w % 2, h // 2, h % 2, :],
                               kT[:, h // 2, k0:k0 + n], start=True, stop=True).then_inc(s_ps, 1)

                    def sums(w):
                        tiles = (0, 1) if w else (1,)

                        def prob_rows(p):
                            pe.wait_ge(p_done, 2 * (NW * b + w) + p // 2 + 1)
                            if p >= 2:
                                pe.wait_ge((pt_act, pt_dve)[p % 2], 2 * (NW * b + w) + 1)
                            elif w >= 1:
                                pe.wait_ge((pt_act, pt_dve)[p % 2], 2 * (NW * b + w))
                            for e in range(2):
                                for j in tiles:
                                    c0 = (p % 2) * HALF + (2 * e + j) * P
                                    last = tr(PB[3][:, c0:c0 + P], sm[:, w % 2, 2 * p + e, j * P:(j + 1) * P], ident[:, :])
                            last.then_inc(pt_ps, 1)

                        def weighted(p):
                            pe.wait_ge((pt_act, pt_dve)[p % 2], 2 * (NW * b + w) + p // 2 + 1)
                            for j in tiles:
                                for e in range(2):
                                    h = 2 * p + e
                                    last = mm(PB[0][64 * e:64 * e + 64, p * P:(p + 1) * P],
                                              vsb[:, w - 1 + j, h * HD1:(h + 1) * HD1], PT[:, p % 2, 2 * e + j, :],
                                              start=(j == tiles[0]), stop=(j == 1))
                            last.then_inc(pv_ps, 1)

                        prob_rows(0)
                        prob_rows(1)
                        pe.wait_ge(qz_done, NW * b + min(w + 3, NW))
                        weighted(0)
                        prob_rows(2)
                        weighted(1)
                        prob_rows(3)
                        weighted(2)
                        weighted(3)

                    for i in range(NW + 2):
                        if 1 <= i <= NW:
                            scores(i - 1)
                        if i < NW:
                            to_rows(i)
                        if i >= 2:
                            sums(i - 2)
                        if i in (NW // 2 + 2, NW + 1):
                            hf = 0 if i < NW else 1
                            pe.wait_ge(oT_done, NW * b + (NW // 2) * (hf + 1))
                            pe.wait_ge(s_masked, H1 * (NW * b + min(i, NW)))
                            for m in range(KD):
                                for p in range(HP):
                                    last = mm(PB[1][:, m * HALF:(m + 1) * HALF], wo[:, p, m * P:(m + 1) * P],
                                              oT[:, p, hf * HALF:(hf + 1) * HALF], start=(p == 0), stop=(p == HP - 1))
                                last.then_inc(wo_ps, 1)
                            if i < NW:
                                pe.wait_ge(wo_done, 2 * KD * b + KD)

            @block.scalar
            def _(act):
                S = nc.scalar.activation
                with act.Fori(l * B, (l + 1) * B) as b:
                    act.wait_ge(wo_done, 2 * KD * b)
                    S(hst[:, 0, :], xr[:, 0, ds(b - l * B, 1), 1:1 + T].rearrange("p o t -> p (o t)"), ACT.Copy).then_inc(h_ready, 1)
                    for w in range(NW):
                        act.wait_ge(qk_ps, NW * b + w + 1)
                        S(qkr[:, w, :], PB[w % 2][:, :], ACT.Copy).then_inc(qk_sb, 1)
                        act.wait_ge(ss_done, NW * b + w)
                        S(sq[:, :], PB[w % 2][:, :], ACT.Square).then_inc(sq_done, 1)
                        act.wait_ge(v_ps, NW * b + w + 1)
                        S(vsb[:, w, :], PB[2][:, (w % 2) * HALF:(w % 2 + 1) * HALF], ACT.Copy).then_inc(v_sb, 1)
                        if w % NN == NN - 1:
                            act.wait_ge(ss_done, NW * b + w + 1)
                            S(nrm[:, w + 1 - NN:w + 1, :], ss[:, w + 1 - NN:w + 1, :], ACT.Sqrt).then_inc(n_sqrt, 1)
                    def exponentials(w, hs):
                        for h in hs:
                            if h % 4 == 0:
                                act.wait_ge(m_done, 2 * (NW * b + w) + h // 4 + 1)
                            last = S(sm[:, w % 2, h, keys(w)], sm[:, w % 2, h, keys(w)], ACT.Exp,
                                     bias=st[:, w % 2, 1, h:h + 1], scale=QK_SCALE, accum_out=st[:, w % 2, 2, h:h + 1])
                            if h % 4 == 3:
                                last.then_inc(e_done, 1)

                    def prob_rows(w, p):
                        act.wait_ge(pt_ps, HP * (NW * b + w) + p + 1)
                        if p or w:
                            act.wait_ge(pv_ps, HP * (NW * b + w) + p - 1)
                        c0 = slice(0, 4) if w else slice(1, 4, 2)
                        S(PT[:, 0, c0, :], PB[3][:, 0:HALF].rearrange("p (a t) -> p a t", t=P)[:, c0, :],
                          ACT.Copy).then_inc(pt_act, 1)

                    for i in range(NW + 2):
                        if 1 <= i <= NW:
                            exponentials(i - 1, range(0, 2))
                        if i < NW:
                            act.wait_ge(tq_ps, NW * b + i + 1)
                            for e in range(2):
                                last = S(qz[64 * e:64 * e + 64, i % 2, :, e, :],
                                         PB[0][64 * e:64 * e + 64, 0:HALF].rearrange("p (a t) -> p a t", a=HP), ACT.Copy)
                            last.then_inc(qz_done, 1)
                        if i >= 2:
                            prob_rows(i - 2, 0)
                        if 1 <= i <= NW:
                            exponentials(i - 1, range(2, 4))
                        if i < NW:
                            act.wait_ge(tk_ps, NW * b + i + 1)
                            S(kT[:, :, i * WIN:(i + 1) * WIN], PB[0][:, HALF:2 * HALF].rearrange("p (a t) -> p a t", a=HP),
                              ACT.Copy).then_inc(kT_done, 1)
                        if 1 <= i <= NW:
                            exponentials(i - 1, range(4, 6))
                        if i >= 2:
                            prob_rows(i - 2, 2)
                        if 1 <= i <= NW:
                            exponentials(i - 1, range(6, 8))
                        if i >= 2:
                            w = i - 2
                            act.wait_ge(pv_ps, HP * (NW * b + w + 1))
                            S(oT[:, :, w * WIN:(w + 1) * WIN], PB[0][:, 0:HALF].rearrange("p (a t) -> p a t", a=HP),
                              ACT.Copy).then_inc(oT_done, 1)

            @block.vector
            def _(dve):
                V = nc.vector
                with dve.Fori(l * B, (l + 1) * B) as b:
                    dve.wait_ge(wo_done, 2 * KD * b)
                    V.tensor_copy(hst[:, 1, :], xr[:, 1, ds(b - l * B, 1), 0:T].rearrange("p o t -> p (o t)")).then_inc(h_ready, 1)
                    def products(w):
                        dve.wait_ge(qk_sb, NW * b + w + 1)
                        V.tensor_tensor(qkr[:, w, :].rearrange("p (h d) -> p h d", d=HD1),
                                        qkr[:, w, :].rearrange("p (h d) -> p h d", d=HD1),
                                        rn[:, w, :].unsqueeze(2).to_broadcast([P, 2 * H1, HD1]), ALU.mult).then_inc(qn_done, 1)
                        dve.wait_ge(qn_done, NW * b + w + 1)
                        dve.wait_ge(tabs, 4 * (l + 1))
                        for j in range(2):
                            src = qkr[:, w, j * INNER:(j + 1) * INNER].rearrange("p (h d) -> p h d", d=HD1)
                            dst = sinp[:, j * INNER:(j + 1) * INNER].rearrange("p (h d) -> p h d", d=HD1)
                            for r in range(2):
                                a, z = slice(r * C, (r + 1) * C), slice((1 - r) * C, (2 - r) * C)
                                last = V.tensor_tensor(dst[:, :, a], src[:, :, z],
                                                       tab[2 * j + 1][:, w, a].unsqueeze(1).to_broadcast([P, H1, C]), ALU.mult)
                        last.then_inc(sin_done, 1)

                    def turn(w):
                        dve.wait_ge(sin_done, NW * b + w + 1)
                        dve.wait_ge(cos_done, 2 * (NW * b + w + 1))
                        if w >= 2:
                            dve.wait_ge(tk_ps, NW * b + w - 1)
                        V.tensor_tensor(turned[:, w % 2, :], cosp[:, :], sinp[:, :], ALU.add).then_inc(turn_done, 1)
                        dve.wait_ge(turn_done, NW * b + w + 1)

                    def maxima(w):
                        s = w % 2
                        if w >= 2:
                            dve.wait_ge(pt_ps, HP * (NW * b + w - 1))
                        for h in range(H1):
                            if h % 2 == 0:
                                dve.wait_ge(s_ps, H1 * (NW * b + w) + h + 2)
                                dve.sem_inc(passed, 1)
                            c0 = (h % 4) * 2 * WIN
                            V.tensor_tensor_reduce(sm[:, s, h, keys(w)], PB[1 + h // 4][:, c0:c0 + 2 * WIN][:, keys(w)],
                                                   mask[:, keys(w)], 1.0, 0.0, ALU.add, ALU.max,
                                                   st[:, s, 0, h:h + 1]).then_inc(s_masked, 1)
                            if h % 4 == 3:
                                hs = slice(h - 3, h + 1)
                                dve.wait_ge(s_masked, H1 * (NW * b + w) + h + 1)
                                V.tensor_scalar_mul(st[:, s, 1, hs], st[:, s, 0, hs], -QK_SCALE).then_inc(m_done, 1)

                    def inverse_sums(w, j):
                        hs = slice(4 * j, 4 * j + 4)
                        dve.wait_ge(e_done, 2 * (NW * b + w) + j + 1)
                        V.reciprocal(st[:, w % 2, 3, hs], st[:, w % 2, 2, hs]).then_inc(d_done, 1)

                    def prob_rows(w, p):
                        dve.wait_ge(pt_ps, HP * (NW * b + w) + p + 1)
                        if p > 1 or w:
                            dve.wait_ge(pv_ps, HP * (NW * b + w) + p - 1)
                        c0 = slice(0, 4) if w else slice(1, 4, 2)
                        V.tensor_copy(PT[:, 1, c0, :],
                                      PB[3][:, HALF:2 * HALF].rearrange("p (a t) -> p a t", t=P)[:, c0, :]).then_inc(pt_dve, 1)

                    dve.wait_ge(G["ld_tab"], 32)
                    for w in range(NW):
                        dve.wait_ge(sq_done, NW * b + w + 1)
                        V.reduce_sum(ss[:, w, :], sq[:, :].rearrange("p (h d) -> p h d", d=HD1), X).then_inc(ss_done, 1)
                        if w % NN == NN - 1:
                            half, hs = w // NN, slice(w + 1 - NN, w + 1)
                            dve.wait_ge(n_sqrt, 2 * b + half + 1)
                            V.tensor_scalar_max(nrm[:, hs, :], nrm[:, hs, :], 1e-12).then_inc(n_step, 1)
                            dve.wait_ge(n_step, 4 * b + 2 * half + 1)
                            V.reciprocal(rn[:, hs, :], nrm[:, hs, :]).then_inc(n_step, 1)
                            dve.wait_ge(n_step, 4 * b + 2 * half + 2)
                        if w == NN:
                            products(0)
                            turn(0)
                    for i in range(NW + 2):
                        if i >= 2:
                            inverse_sums(i - 2, 1)
                        if 1 <= i <= NW:
                            maxima(i - 1)
                        if i + 1 < NW:
                            products(i + 1)
                        if i >= 2:
                            prob_rows(i - 2, 1)
                        if 1 <= i <= NW:
                            inverse_sums(i - 1, 0)
                        if i >= 2:
                            prob_rows(i - 2, 3)
                        if i + 1 < NW:
                            turn(i + 1)
                        if i in (NW // 2 + 2, NW + 1):
                            hf = 0 if i < NW else 1
                            for m in range(KD):
                                dve.wait_ge(wo_ps, KD * (2 * b + hf) + m + 1)
                                xs = xr[:, m, ds(b - l * B, 1), 1 + hf * HALF:1 + (hf + 1) * HALF].rearrange("p o t -> p (o t)")
                                V.tensor_tensor(xs, PB[1][:, m * HALF:(m + 1) * HALF], xs, ALU.add).then_inc(wo_done, 1)


def stage_ffn1(nc, G, A, l):
    with ExitStack() as ctx:
        sb = lambda n, s, dt=F32: ctx.enter_context(nc.sbuf_tensor(f"m{l}_{n}", s, dt))
        sem = lambda n: G["layer_sem"](f"m_{n}")
        PB, xr = G["PB"], G["xr"]
        w1, w2, lg, lb, b1, b2 = (G[n] for n in ("w1", "w2", "lg", "lb", "b1", "b2"))
        mean = sb("mean", [P, P])
        eps = sb("eps", [P, 1])
        xc = sb("xc", [P, 2, KD, HALF])
        sq = sb("sq", [P, 2, KD, HALF])
        sd = sb("sd", [P, 2, HALF])
        rs = sb("rs", [P, 2, HALF])
        xn = sb("xn", [P, 2, KD, HALF])
        hn = sb("hn", [P, 2, KD, HALF])
        gl = sb("gl", [P, 2, HALF])
        hid = sb("hid", [P, 2, FT, HALF])
        consts, mu_ps, xc_done, sq_done, var_ps, sd_done, rs_done, xn_done, hn_done = (sem(n) for n in (
            "consts", "mu_ps", "xc_done", "sq_done", "var_ps", "sd_done", "rs_done", "xn_done", "hn_done"))
        g_ps, a_ps, gl_done, hid_done, y_ps, y_done = (sem(n) for n in ("g_ps", "a_ps", "gl_done", "hid_done", "y_ps", "y_done"))
        NH = T // HALF

        def shifted(b, k, hf):
            c0 = hf * HALF + (1 if k == 0 else 0)
            return xr[:, k, ds(b - l * B, 1), c0:c0 + HALF].rearrange("p o t -> p (o t)")

        with nc.Block() as block:
            if l + 1 < LAYERS:
                @block.sync
                def _(sp):
                    load_attention1(sp, G, A, l + 1)

            @block.gpsimd
            def _(pool):
                nc.gpsimd.memset(mean[:, :], 1.0 / D).then_inc(consts, 1)
                nc.gpsimd.memset(eps[:, :], LN_EPS).then_inc(consts, 1)

            @block.tensor
            def _(pe):
                mm = nc.tensor.matmul
                pe.wait_ge(consts, 2 * (l + 1))
                pe.wait_ge(G["ld_ffn"], LD_FFN * (l + 1))
                with pe.Fori(l * B, (l + 1) * B) as b:
                    pe.wait_ge(y_done, NH * KD * b)
                    for hf in range(NH):
                        for k in range(KD):
                            last = mm(PB[hf][:, 0:HALF], mean[:, :], shifted(b, k, hf), start=(k == 0), stop=(k == KD - 1))
                        last.then_inc(mu_ps, 1)
                    for hf in range(NH):
                        pe.wait_ge(sq_done, KD * (NH * b + hf + 1))
                        for k in range(KD):
                            last = mm(PB[hf][:, HALF:2 * HALF], mean[:, :], sq[:, hf, k, :], start=(k == 0), stop=(k == KD - 1))
                        last.then_inc(var_ps, 1)
                    for hf in range(NH):
                        pe.wait_ge(hn_done, KD * (NH * b + hf + 1))
                        for f in range(FT):
                            u = FT * (NH * b + hf) + f
                            for part, (col, ready) in enumerate(((HIDP, g_ps), (0, a_ps))):
                                if f >= 2:
                                    pe.wait_ge(hid_done, u - 1)
                                elif hf:
                                    pe.wait_ge(hid_done, u - 1)
                                else:
                                    pe.wait_ge(hid_done, FT * NH * b)
                                for k in range(KD):
                                    last = mm(PB[2 + f % 2][:, part * HALF:(part + 1) * HALF],
                                              w1[:, k, col + f * P:col + (f + 1) * P], hn[:, hf, k, :],
                                              start=(k == 0), stop=(k == KD - 1))
                                last.then_inc(ready, 1)
                        pe.wait_ge(hid_done, FT * (NH * b + hf + 1))
                        for m in range(KD):
                            for f in range(FT):
                                last = mm(PB[hf][:, m * HALF:(m + 1) * HALF], w2[:, f, m * P:(m + 1) * P], hid[:, hf, f, :],
                                          start=(f == 0), stop=(f == FT - 1))
                            last.then_inc(y_ps, 1)

            @block.scalar
            def _(act):
                S = nc.scalar.activation
                act.wait_ge(consts, 2 * (l + 1))
                act.wait_ge(G["ld_ffn"], LD_FFN * (l + 1))
                with act.Fori(l * B, (l + 1) * B) as b:
                    for hf in range(NH):
                        for k in range(KD):
                            act.wait_ge(xc_done, KD * (NH * b + hf) + k + 1)
                            S(sq[:, hf, k, :], xc[:, hf, k, :], ACT.Square).then_inc(sq_done, 1)
                    for hf in range(NH):
                        act.wait_ge(var_ps, NH * b + hf + 1)
                        S(sd[:, hf, :], PB[hf][:, HALF:2 * HALF], ACT.Sqrt, bias=eps[:, 0:1]).then_inc(sd_done, 1)
                    for hf in range(NH):
                        for k in range(KD):
                            act.wait_ge(xn_done, KD * (NH * b + hf) + k + 1)
                            S(hn[:, hf, k, :], xn[:, hf, k, :], ACT.Identity, bias=lb[:, k:k + 1],
                              scale=lg[:, k:k + 1]).then_inc(hn_done, 1)
                    for hf in range(NH):
                        for f in range(FT):
                            u = FT * (NH * b + hf) + f
                            act.wait_ge(g_ps, u + 1)
                            if f >= 2 or hf:
                                act.wait_ge(hid_done, u - 1)
                            S(gl[:, f % 2, :], PB[2 + f % 2][:, 0:HALF], ACT.Gelu, bias=b1[:, FT + f:FT + f + 1]).then_inc(gl_done, 1)

            @block.vector
            def _(dve):
                V = nc.vector
                dve.wait_ge(G["ld_ffn"], LD_FFN * (l + 1))
                with dve.Fori(l * B, (l + 1) * B) as b:
                    for hf in range(NH):
                        dve.wait_ge(mu_ps, NH * b + hf + 1)
                        for k in range(KD):
                            V.tensor_tensor(xc[:, hf, k, :], shifted(b, k, hf), PB[hf][:, 0:HALF], ALU.subtract).then_inc(xc_done, 1)
                    for hf in range(NH):
                        dve.wait_ge(sd_done, NH * b + hf + 1)
                        V.reciprocal(rs[:, hf, :], sd[:, hf, :]).then_inc(rs_done, 1)
                        dve.wait_ge(rs_done, NH * b + hf + 1)
                        for k in range(KD):
                            V.tensor_tensor(xn[:, hf, k, :], xc[:, hf, k, :], rs[:, hf, :], ALU.mult).then_inc(xn_done, 1)
                    for hf in range(NH):
                        for f in range(FT):
                            u = FT * (NH * b + hf) + f
                            dve.wait_ge(gl_done, u + 1)
                            dve.wait_ge(a_ps, u + 1)
                            V.scalar_tensor_tensor(out=hid[:, hf, f, :], in0=PB[2 + f % 2][:, HALF:2 * HALF],
                                                   scalar=b1[:, f:f + 1], in1=gl[:, f % 2, :], op0=ALU.add,
                                                   op1=ALU.mult).then_inc(hid_done, 1)
                        for m in range(KD):
                            dve.wait_ge(y_ps, KD * (NH * b + hf) + m + 1)
                            xs = xr[:, m, ds(b - l * B, 1), 1 + hf * HALF:1 + (hf + 1) * HALF].rearrange("p o t -> p (o t)")
                            V.scalar_tensor_tensor(out=xs, in0=PB[hf][:, m * HALF:(m + 1) * HALF], scalar=b2[:, m:m + 1],
                                                   in1=xs, op0=ALU.add, op1=ALU.add).then_inc(y_done, 1)


def stage_store(nc, G, A, out):
    with ExitStack() as ctx:
        added = ctx.enter_context(nc.semaphore("e_added"))
        stored = ctx.enter_context(nc.semaphore("e_stored"))
        x1T, xr = G["x1T"], G["xr"]
        with nc.Block() as block:
            @block.vector
            def _(dve):
                for k in range(KD):
                    for b in range(B):
                        nc.vector.tensor_tensor(x1T[:, k, b * T:(b + 1) * T], x1T[:, k, b * T:(b + 1) * T],
                                                xr[:, k, b, 1:1 + T], ALU.add).then_inc(added, 1)

            @block.sync
            def _(sp):
                for k in range(KD):
                    for b in range(B):
                        sp.wait_ge(added, k * B + b + 1)
                        sp.dma_start(out[k * P:(k + 1) * P, b * T:(b + 1) * T], x1T[:, k, b * T:(b + 1) * T]).then_inc(stored, 16)
                sp.wait_ge(stored, 16 * KD * B)


def program(nc, A, out):
    with ExitStack() as top:
        def sb(n, s, dt=F32, ctx=top, side="left"):
            return ctx.enter_context(nc.sbuf_tensor(n, s, dt, side=side))

        G = {"PB": [top.enter_context(nc.psum_tensor(f"bank{i}", [P, 2 * HALF], F32)) for i in range(4)],
             "scr": nc.dram_tensor("qk_parts", [2, 3, D, N], BF16, kind="Internal").ap()}
        for n in ("ld_x1", "ld_att", "ld_ffn", "ld_tab", "passed"):
            G[n] = top.enter_context(nc.semaphore("g_" + n))
        layer_sems = {}

        def layer_sem(n):
            if n not in layer_sems:
                layer_sems[n] = top.enter_context(nc.semaphore(n))
            return layer_sems[n]

        G["layer_sem"] = layer_sem
        G["ident"] = sb("ident", [P, P])
        G["rot"] = sb("rot", [P, KD, D])
        G["csum"] = sb("csum", [P, KD, B])
        heads, values, mixed, moe = ExitStack(), ExitStack(), ExitStack(), ExitStack()
        G["gate"] = sb("gate", [P, B * TT * H0], ctx=heads, side="right")
        G["fa"] = sb("fa", [P, TT, B], ctx=heads, side="right")
        G["vsum"] = sb("vsum", [P, B, D], ctx=heads, side="right")
        G["v"] = sb("v", [P, 2 * B, TT, P], ctx=values)
        stage_project(nc, G, A)
        G["OT"] = sb("OT", [P, 2 * HG, T], ctx=heads, side="right")
        stage_attention0(nc, G, A)
        values.close()
        G["X0T"] = sb("X0T", [P, KD, N], ctx=mixed)
        G["X0"] = sb("X0", [P, B * TT, D], ctx=mixed)
        stage_out0(nc, G, A)
        heads.close()
        G["x1T"] = sb("x1T", [P, KD, N], side="right")
        G["O"] = sb("O", [P, B * TT, D], ctx=moe, side="right")
        G["den"] = sb("den", [P, B * TT], ctx=moe, side="right")
        stage_moe(nc, G, A)
        mixed.close()
        G["xr"] = sb("xr", [P, KD, B, 1 + T])
        G["wqkv1"] = sb("wqkv1", [P, KD, 3 * INNER])
        G["wo"] = sb("wo", [P, HP, D])
        G["mask"] = sb("mask", [P, 2 * WIN])
        G["qks"] = sb("qks", [P, LAYERS, 4, HD1])
        G["w1"] = sb("w1", [P, KD, 2 * HIDP])
        G["w2"] = sb("w2", [P, FT, D])
        G["lg"], G["lb"], G["b2"] = (sb(n, [P, KD]) for n in ("lg", "lb", "b2"))
        G["b1"] = sb("b1", [P, 2 * FT])
        stage_rotate(nc, G, A)
        moe.close()
        for l in range(LAYERS):
            stage_attention1(nc, G, A, l)
            stage_ffn1(nc, G, A, l)
        stage_store(nc, G, A, out)


def constants():
    f = np.float32
    c = {}
    inv = f(10000.0) ** np.repeat(np.arange(0, D, 2, dtype=f) / f(D), 2)
    c["peT"] = np.sin(np.arange(T, dtype=f)[:, None] / inv[None, :]).astype(f).T
    half = np.arange(0, HD1, 2, dtype=f)
    t = np.arange(T, dtype=f)
    freqs = t[:, None] * (f(1.0) / f(10000.0) ** (half / f(HD1)))[None, :]
    freqs = np.concatenate([freqs, freqs], -1)
    scale = ((half + f(0.4 * HD1)) / f(1.4 * HD1))[None, :] ** ((t - T // 2) / f(WIN // 2))[:, None]
    scale = np.concatenate([scale, scale], -1)
    cos, sin = np.cos(freqs), np.sin(freqs)
    sin = np.concatenate([-sin[:, :HD1 // 2], sin[:, HD1 // 2:]], -1)
    c["tables"] = np.stack([cos * scale, sin * scale, cos / scale, sin / scale]).astype(f)
    i, j = np.arange(WIN)[:, None], np.arange(WIN)[None, :]
    c["mask"] = np.concatenate([np.where(j >= i, 0.0, MASKED), np.where(j <= i, 0.0, MASKED)], 1).astype(f)
    c["ident"] = np.eye(P, dtype=f)
    ham = np.zeros((4, 4, 4))
    for k, terms in enumerate((((0, 0, 1), (1, 1, -1), (2, 2, -1), (3, 3, -1)), ((0, 1, 1), (1, 0, 1), (2, 3, 1), (3, 2, -1)),
                               ((0, 2, 1), (1, 3, -1), (2, 0, 1), (3, 1, 1)), ((0, 3, 1), (1, 2, 1), (2, 1, -1), (3, 0, 1)))):
        for a, b, s in terms:
            ham[k, a, b] = s
    conj = np.array([1.0, -1.0, -1.0, -1.0])
    c["sgn"] = np.einsum("iak,kjb,b->abij", ham, ham, conj).reshape(16, 16).astype(f)
    return c


def kernel(**inputs):
    import concourse.bacc as _bacc
    from concourse.bass_utils import run_bass_kernel_spmd as _run

    I = {n: np.asarray(v) for n, v in inputs.items()}
    c0, f1 = "L0_cond_", "L1_ffn_"
    col = lambda v: v.reshape(-1, P).T
    rep = lambda v, n: np.broadcast_to(v, (n,) + v.shape)
    pad = lambda a, n: np.pad(a, [(0, 0)] * (a.ndim - 1) + [(0, n - a.shape[-1])])
    cond, qr = I["cond_256"], I["L1_cond_q_right"]
    w1, b1 = I[f1 + "w1"], I[f1 + "b1"]
    w1 = np.concatenate([pad(w1[..., :HID], HIDP), pad(w1[..., HID:], HIDP)], -1)
    b1 = np.concatenate([pad(b1[..., :HID], HIDP), pad(b1[..., HID:], HIDP)], -1)
    qs, ks = I[f1 + "q_scale"], I[f1 + "k_scale"]
    swap = lambda v: np.concatenate([v[:, HD1 // 2:], v[:, :HD1 // 2]], -1)
    rows = [0] * 4 + [1] * 12
    arrays = {
        **constants(),
        "xT": I["x"].reshape(N, D).T,
        "wqkv0T": I[c0 + "Wqkv"].T, "bqk": col(I[c0 + "bqkv"][:2 * D]), "bvB": rep(I[c0 + "bqkv"][2 * D:], P),
        "wc1xT": I[c0 + "Wc1"][:, :D].T, "wc1cT": I[c0 + "Wc1"][:, D:].T, "bc1": col(I[c0 + "bc1"]),
        "wc2T": I[c0 + "Wc2"].T, "bc2B": rep(I[c0 + "bc2"], P),
        "csT": cond.T, "we1T": I[c0 + "We1"].T, "be1": col(I[c0 + "be1"]), "we2T": I[c0 + "We2"].T,
        "rows2": rep(np.stack([I[c0 + "be2"], I[c0 + "ln_g"], I[c0 + "ln_b"]]), B),
        "woutT": I[c0 + "Wout"].T, "bout": col(I[c0 + "bout"]), "boutB": rep(I[c0 + "bout"], P),
        "phi": I["L0_ffn_phi"].reshape(D, SLOTS), "W": I["L0_ffn_W"], "bexp": np.repeat(I["L0_ffn_b"], NP_, 0),
        "ql": cond[rows], "qr": np.tile(qr, (4, 1)), "gate": rep(I["L1_cond_spectral_gate"].reshape(64), 16),
        "qall": rep(np.concatenate([cond, qr], 0), 16),
        "wqkv1": I[f1 + "wqkv"], "wo": I[f1 + "wo"], "w1": w1,
        "w2": np.pad(I[f1 + "w2"], [(0, 0), (0, HIDP - HID), (0, 0)]),
        "lg": np.stack([col(v) for v in I[f1 + "ln_g"]]), "lb": np.stack([col(v) for v in I[f1 + "ln_b"]]),
        "b1": np.stack([col(v) for v in b1]), "b2": np.stack([col(v) for v in I[f1 + "b2"]]),
        "qks": rep(np.stack([qs, swap(qs), ks, swap(ks)], 1), P),
    }
    arrays = {f"in_{n}": np.ascontiguousarray(a) for n, a in arrays.items()}
    nc = _bacc.Bacc("TRN2", target_bir_lowering=False, num_devices=1)
    A = {n[3:]: nc.dram_tensor(n, a.shape, mybir.dt.from_np(a.dtype), kind="ExternalInput").ap() for n, a in arrays.items()}
    out = nc.dram_tensor("out_T", (D, N), F32, kind="ExternalOutput").ap()
    program(nc, A, out)
    r = _run(nc, [arrays], core_ids=[0])
    return np.ascontiguousarray(r.results[0]["out_T"].T).reshape(B, T, D)
```

```python
import itertools
from contextlib import ExitStack

import numpy as np

import concourse.bass as bass
from concourse import mybir

F32 = mybir.dt.float32
F32R = mybir.dt.float32r
BF16 = mybir.dt.bfloat16
ACT = mybir.ActivationFunctionType
ALU = mybir.AluOpType
X = mybir.AxisListType.X
ds = bass.ds

P = 128
B, T, D = 2, 1024, 256
N = B * T
KD = D // P
TT = T // P
HALF = 512
H0, HD0 = 16, 16
HG = 4
KS = 6 * HD0
KA = KS + 3
Q_PART = (0, 0, 1, 1, 0, 2)
K_PART = (0, 1, 0, 1, 2, 0)
COUPLING = 0.3 * 0.7
COH_EPS = 1e-8
CD = 64
NE, NP_ = 64, 32
SLOTS = NE * NP_
CH = 4
CS = SLOTS // CH
CE = NE // CH
LAYERS = 2
H1, HD1 = 8, 64
INNER = H1 * HD1
HP = H1 // 2
WIN = 128
NW = T // WIN
HID = 682
FT = -(-HID // P)
HIDP = FT * P
QK_SCALE = 8.0
LN_EPS = 1e-5
PRODUCTS = ((0, 0), (0, 1), (1, 0))
MASKED = -1e30
LOWEST = -3e38


def chain(eng, sem, start=0):
    n = [0]

    def link(ins):
        n[0] += 1
        ins.then_inc(sem, 1)
        eng.wait_ge(sem, start + n[0])

    link.count = n
    return link


def stage_project(nc, G, A):
    with ExitStack() as ctx:
        sb = lambda n, s, dt=F32: ctx.enter_context(nc.sbuf_tensor(n, s, dt))
        sem = G["early_sem"]
        PB = G["PB"]
        xT = sb("p_xT", [P, KD, N])
        wqkv = sb("p_wqkv", [P, KD, 3 * D])
        wc1x = sb("p_wc1x", [P, KD, D])
        wc2 = sb("p_wc2", [P, KD, H0])
        we2 = sb("p_we2", [P, KD, D])
        peT = sb("p_peT", [P, KD, T])
        wc1c = sb("p_wc1c", [CD, D])
        we1 = sb("p_we1", [CD, D])
        csT = sb("p_csT", [CD, B])
        bqk = sb("p_bqk", [P, 4])
        bvB = sb("p_bvB", [P, D])
        bc1 = sb("p_bc1", [P, KD])
        be1 = sb("p_be1", [P, KD])
        bc2B = sb("p_bc2B", [P, H0])
        rows2 = sb("p_rows2", [B, 3, D])
        ql = sb("p_ql", [16, 64])
        qr = sb("p_qr", [16, 64])
        gate = sb("p_gate", [16, 64])
        qall = sb("p_qall", [16, 6, 64])
        sgn = sb("p_sgn", [16, 16])
        parts = sb("p_parts", [P, 4, 3, HALF], BF16)
        rest = sb("p_rest", [P, 4, HALF])
        c1T = sb("p_c1T", [P, KD, N])
        cbias = sb("p_cbias", [P, KD, B])
        h1T = sb("p_h1T", [P, KD, B])
        fpw = sb("p_fpw", [B, 4, D])
        fst = sb("p_fst", [B, 8])
        fpT = sb("p_fpT", [P, KD, B])
        faw = sb("p_faw", [B, 3, T])
        zt = sb("p_zt", [P, 3, B * TT * H0])
        xsum = sb("p_xsum", [P, KD, B])
        xsB = sb("p_xsB", [P, KD, B, P])
        qsq = sb("p_qsq", [16, 6, 64])
        qn = sb("p_qn", [16, 2, 64])
        qsd = sb("p_qsd", [16, 2, 64])
        qpr = sb("p_qpr", [16, 4, 64])
        pp2 = sb("p_pp2", [16, 2, 64])
        mco = sb("p_mco", [P, 16])
        ones = sb("p_ones", [P, P])
        eps5 = sb("p_eps5", [B, 1])

        ld_small, ld_x, ld_pe = sem("ld_small"), sem("ld_x"), sem("ld_pe")
        consts = sem("consts")
        dve_step, act_step = sem("dve_step"), sem("act_step")
        cond_ps, h1_ready, fp_ps, ln_var, ln_sd, fp_ready = (sem(n) for n in (
            "cond_ps", "h1_ready", "fp_ps", "ln_var", "ln_sd", "fp_ready"))
        fpT_ps, fpT_ready, fa_ps, fa_max, fa_exp, fa_ready, faT_ps = (sem(n) for n in (
            "fpT_ps", "fpT_ready", "fa_ps", "fa_max", "fa_exp", "fa_ready", "faT_ps"))
        q_norm, q_sd, pp_ready, mco_ps = sem("q_norm"), sem("q_sd"), sem("pp_ready"), sem("mco_ps")
        cb_ready = sem("cb_ready")
        qk_ps, qk_p1, qk_rest, qk_p2, qk_p3 = (sem(n) for n in ("qk_ps", "qk_p1", "qk_rest", "qk_p2", "qk_p3"))
        qk_stored = [sem(f"qk_stored{i}") for i in range(4)]
        v_ps, v_done, c1_ps, c1_done, z_ps, z_clip, z_exp = (sem(n) for n in (
            "v_ps", "v_done", "c1_ps", "c1_done", "z_ps", "z_clip", "z_exp"))
        xs_ready, vs_ps = sem("xs_ready"), sem("vs_ps")
        UNITS = [(b, hf, m) for b in range(B) for hf in range(T // HALF) for m in range(4)]
        small = [(wc1c, A["wc1cT"]), (we1, A["we1T"]), (csT, A["csT"]), (be1, A["be1"]), (bc1, A["bc1"]),
                 (rows2, A["rows2"]), (ql, A["ql"]), (qr, A["qr"]), (gate, A["gate"]), (qall, A["qall"]),
                 (sgn, A["sgn"]), (G["ident"], A["ident"]), (bqk, A["bqk"]), (bvB, A["bvB"]), (bc2B, A["bc2B"])]
        NSMALL = 16 * (len(small) + 2)
        kp = lambda a: a.rearrange("(k p) n -> p k n", p=P)
        scr = G["scr"]
        ring = lambda u: PB[(u % 4) // 2][:, HALF * (u % 2):HALF * (u % 2) + HALF]
        misc = lambda r, a, b: PB[3][0:r, HALF + a:HALF + b]

        with nc.Block() as block:
            @block.sync
            def _(sp):
                for dst, src in small:
                    sp.dma_start(dst[:], src).then_inc(ld_small, 16)
                sp.dma_start(we2[:, :, :], kp(A["we2T"])).then_inc(ld_small, 16)
                sp.dma_start(wc2[:, :, :], kp(A["wc2T"])).then_inc(ld_small, 16)
                sp.dma_start(peT[:, :, :], kp(A["peT"])).then_inc(ld_pe, 16)
                for u, (b, hf, m) in enumerate(UNITS):
                    sp.wait_ge(qk_p3, u + 1)
                    t0 = b * T + hf * HALF
                    dst = scr[m // 2, :, (m % 2) * P:(m % 2) * P + P, t0:t0 + HALF].rearrange("c p t -> p c t")
                    sp.dma_start(dst, parts[:, u % 4, :, :]).then_inc(qk_stored[u % 4], 16)
                for s in qk_stored:
                    sp.wait_ge(s, 16 * len(UNITS) // 4)

            @block.gpsimd
            def _(pool):
                nc.gpsimd.memset(ones[:, :], 1.0).then_inc(consts, 1)
                nc.gpsimd.memset(eps5[:, :], LN_EPS).then_inc(consts, 1)
                for u in range(len(UNITS)):
                    pool.wait_ge(qk_p2, u + 1)
                    nc.gpsimd.tensor_tensor(parts[:, u % 4, 2, :], rest[:, u % 4, :], parts[:, u % 4, 1, :],
                                            ALU.subtract).then_inc(qk_p3, 1)

            @block.scalar
            def _(act):
                act.dma_start(xT[:, :, :], kp(A["xT"])).then_inc(ld_x, 16)
                act.dma_start(wqkv[:, :, :], kp(A["wqkv0T"])).then_inc(ld_x, 16)
                act.dma_start(wc1x[:, :, :], kp(A["wc1xT"])).then_inc(ld_x, 16)
                act.wait_ge(ld_small, NSMALL)
                act.wait_ge(consts, 2)
                act.wait_ge(cb_ready, KD)
                for k in range(KD):
                    nc.scalar.activation(h1T[:, k, :], misc(P, 4 + 2 * k, 6 + 2 * k), ACT.Relu,
                                         bias=be1[:, k:k + 1]).then_inc(h1_ready, 1)
                act.wait_ge(q_norm, 1)
                nc.scalar.activation(qsd[:, :, :], qn[:, :, :], ACT.Sqrt).then_inc(q_sd, 1)
                act.wait_ge(ln_var, 1)
                nc.scalar.activation(fst[:, 4:5], fst[:, 3:4], ACT.Sqrt, bias=eps5[:, 0:1]).then_inc(ln_sd, 1)
                for u, (b, hf, m) in enumerate(UNITS):
                    s = u % 4
                    act.wait_ge(qk_ps, u + 1)
                    if u >= 4:
                        act.wait_ge(qk_stored[s], 16 * (u // 4))
                    nc.scalar.activation(parts[:, s, 0, :], ring(u), ACT.Identity,
                                         bias=bqk[:, m:m + 1]).then_inc(qk_p1, 1)
                    if u >= 1:
                        act.wait_ge(qk_rest, u)
                        nc.scalar.activation(parts[:, (u - 1) % 4, 1, :], rest[:, (u - 1) % 4, :],
                                             ACT.Copy).then_inc(qk_p2, 1)
                act.wait_ge(qk_rest, len(UNITS))
                nc.scalar.activation(parts[:, 3, 1, :], rest[:, 3, :], ACT.Copy).then_inc(qk_p2, 1)
                act.wait_ge(cb_ready, KD)
                for v in range(KD * N // HALF):
                    e, n = v % KD, v // KD
                    act.wait_ge(c1_ps, v + 1)
                    nc.scalar.activation(c1T[:, e, n * HALF:(n + 1) * HALF], ring(v), ACT.Tanh,
                                         bias=cbias[:, e, n // 2:n // 2 + 1]).then_inc(c1_done, 1)
                act.wait_ge(fa_max, 1)
                nc.scalar.activation(faw[:, 1, :], faw[:, 0, :], ACT.Exp, bias=fst[:, 6:7],
                                     accum_out=fst[:, 7:8]).then_inc(fa_exp, 1)
                act.wait_ge(z_clip, 1)
                nc.scalar.activation(zt[:, 2, :], zt[:, 1, :], ACT.Exp).then_inc(z_exp, 1)

            @block.vector
            def _(dve):
                link = chain(dve, dve_step)
                V = nc.vector
                dve.wait_ge(ld_small, NSMALL)
                dve.wait_ge(consts, 2)
                link(V.tensor_tensor(qsq[:, :, :], qall[:, :, :], qall[:, :, :], ALU.mult))
                link(V.tensor_reduce(qn[:, 0, :], qsq[:, 0:2, :].rearrange("p r d -> p d r"), X, ALU.add))
                link(V.tensor_reduce(qn[:, 1, :], qsq[:, 2:6, :].rearrange("p r d -> p d r"), X, ALU.add))
                V.tensor_scalar_add(qn[:, :, :], qn[:, :, :], 1e-8).then_inc(q_norm, 1)
                dve.wait_ge(cond_ps, 1)
                for k in range(KD):
                    V.tensor_scalar_add(cbias[:, k, :], misc(P, 2 * k, 2 * k + 2), bc1[:, k:k + 1]).then_inc(cb_ready, 1)
                dve.wait_ge(q_sd, 1)
                link(V.tensor_tensor(qpr[:, 0, :], qsd[:, 0, :], qsd[:, 1, :], ALU.mult))
                link(V.reciprocal(qpr[:, 1, :], qpr[:, 0, :]))
                link(V.tensor_tensor(qpr[:, 2, :], ql[:, :], qr[:, :], ALU.mult))
                link(V.tensor_tensor(qpr[:, 3, :], qpr[:, 2, :], gate[:, :], ALU.mult))
                for r in range(2):
                    V.tensor_tensor(pp2[:, r, :], qpr[:, 3, :], qpr[:, 1, :], ALU.mult).then_inc(pp_ready, 1)
                dve.wait_ge(fp_ps, 1)
                link(V.tensor_tensor(fpw[:, 0, :], misc(B, 16, 16 + D), rows2[:, 0, :], ALU.add))
                link(V.reduce_sum(fst[:, 0:1], fpw[:, 0, :], X))
                link(V.tensor_scalar_mul(fst[:, 1:2], fst[:, 0:1], 1.0 / D))
                link(V.tensor_scalar(fpw[:, 1, :], fpw[:, 0, :], fst[:, 1:2], None, ALU.subtract))
                link(V.tensor_tensor(fpw[:, 2, :], fpw[:, 1, :], fpw[:, 1, :], ALU.mult))
                link(V.reduce_sum(fst[:, 2:3], fpw[:, 2, :], X))
                V.tensor_scalar_mul(fst[:, 3:4], fst[:, 2:3], 1.0 / D).then_inc(ln_var, 1)
                dve.wait_ge(ln_sd, 1)
                link(V.reciprocal(fst[:, 5:6], fst[:, 4:5]))
                link(V.scalar_tensor_tensor(out=fpw[:, 3, :], in0=fpw[:, 1, :], scalar=fst[:, 5:6],
                                            in1=rows2[:, 1, :], op0=ALU.mult, op1=ALU.mult))
                link(V.tensor_tensor(fpw[:, 0, :], fpw[:, 3, :], rows2[:, 2, :], ALU.add))
                dve.sem_inc(fp_ready, 1)
                dve.wait_ge(fpT_ps, 1)
                V.tensor_copy(fpT[:, :, :], misc(P, 288, 292).rearrange("p (k b) -> p k b", b=B)).then_inc(fpT_ready, 1)
                dve.wait_ge(mco_ps, 1)
                link(V.tensor_copy(mco[:, :], misc(P, 304, 320)))
                for i in range(4):
                    for j in range(4):
                        r = slice(64 * (j % 2), 64 * (j % 2) + 64)
                        mc = V.tensor_scalar_mul(G["rot"][r, j // 2, 64 * i:64 * i + 64], G["ident"][r, r],
                                                 mco[r, 4 * i + j:4 * i + j + 1])
                mc.then_inc(dve_step, 1)
                for u, (b, hf, m) in enumerate(UNITS):
                    dve.wait_ge(qk_p1, u + 1)
                    if u >= 4:
                        dve.wait_ge(qk_p3, u - 3)
                    V.scalar_tensor_tensor(out=rest[:, u % 4, :], in0=ring(u), scalar=bqk[:, m:m + 1],
                                           in1=parts[:, u % 4, 0, :], op0=ALU.add,
                                           op1=ALU.subtract).then_inc(qk_rest, 1)
                for k in range(KD):
                    V.reduce_sum(xsum[:, k, :], xT[:, k, :].rearrange("p (b t) -> p b t", b=B), X).then_inc(dve_step, 1)
                dve.wait_ge(dve_step, link.count[0] + 1 + KD)
                for k in range(KD):
                    for b in range(B):
                        V.tensor_scalar_mul(xsB[:, k, b, :], ones[:, :], xsum[:, k, b:b + 1]).then_inc(xs_ready, 1)
                for tt in range(B * TT):
                    b, jt = tt // TT, tt % TT
                    dve.wait_ge(v_ps, tt + 1)
                    V.tensor_tensor(G["v"][:, 2 * b:2 * b + 2, jt, :],
                                    PB[2][:, HALF * (tt % 2):HALF * (tt % 2) + D].rearrange("p (m d) -> p m d", m=2),
                                    bvB[:, :].rearrange("p (m d) -> p m d", m=2), ALU.add).then_inc(v_done, 1)
                dve.wait_ge(vs_ps, 1)
                for b in range(B):
                    V.scalar_tensor_tensor(out=G["vsum"][:, b, :], in0=bvB[:, :], scalar=float(T),
                                           in1=PB[1][:, HALF + b * D:HALF + (b + 1) * D], op0=ALU.mult, op1=ALU.add)
                dve.wait_ge(fa_ps, 1)
                link2 = chain(dve, act_step)
                link2(V.tensor_copy(faw[:, 0, :], PB[2][0:B, 0:T]))
                link2(V.reduce_max(fst[:, 0:1], faw[:, 0, :], X))
                V.tensor_scalar_mul(fst[:, 6:7], fst[:, 0:1], -1.0).then_inc(fa_max, 1)
                dve.wait_ge(fa_exp, 1)
                link2(V.reciprocal(fst[:, 1:2], fst[:, 7:8]))
                V.tensor_scalar(faw[:, 2, :], faw[:, 1, :], fst[:, 1:2], COUPLING, ALU.mult, ALU.mult).then_inc(fa_ready, 1)
                dve.wait_ge(z_ps, 1)
                link2(V.tensor_tensor(zt[:, 0, :].rearrange("p (t h) -> p t h", h=H0),
                                      PB[3][:, 0:B * TT * H0].rearrange("p (t h) -> p t h", h=H0),
                                      bc2B[:, :].unsqueeze(1).to_broadcast([P, B * TT, H0]), ALU.add))
                V.tensor_scalar(zt[:, 1, :], zt[:, 0, :], -87.0, -1.0, ALU.max, ALU.mult).then_inc(z_clip, 1)
                dve.wait_ge(z_exp, 1)
                c = 1.0 / (1.0 - COUPLING)
                V.tensor_scalar(G["gate"][:, :], zt[:, 2, :], COH_EPS * c, (1.0 + COH_EPS) * c, ALU.mult, ALU.add)
                dve.wait_ge(faT_ps, 1)
                link2(V.tensor_copy(G["fa"][:, :, :], misc(P, 320, 320 + B * TT).rearrange("p (t b) -> p t b", b=B)))

            @block.tensor
            def _(pe):
                mm, tr, ident = nc.tensor.matmul, nc.tensor.transpose, G["ident"]
                pe.wait_ge(ld_small, NSMALL)
                for k in range(KD):
                    mm(misc(P, 2 * k, 2 * k + 2), wc1c[:, k * P:(k + 1) * P], csT[:, :], start=True, stop=True)
                    last = mm(misc(P, 4 + 2 * k, 6 + 2 * k), we1[:, k * P:(k + 1) * P], csT[:, :], start=True, stop=True)
                last.then_inc(cond_ps, 1)
                pe.wait_ge(h1_ready, KD)
                pe.wait_ge(pp_ready, 2)
                mm(misc(P, 304, 320), pp2[:, :, :].rearrange("p r d -> p (r d)"), sgn[:, :], start=True,
                   stop=True).then_inc(mco_ps, 1)
                for k in range(KD):
                    last = mm(misc(B, 16, 16 + D), h1T[:, k, :], we2[:, k, :], start=(k == 0), stop=(k == KD - 1))
                last.then_inc(fp_ps, 1)
                pe.wait_ge(fp_ready, 1)
                for k in range(KD):
                    last = tr(misc(P, 288 + 2 * k, 290 + 2 * k), fpw[:, 0, k * P:(k + 1) * P], ident[0:B, 0:B])
                last.then_inc(fpT_ps, 1)
                pe.wait_ge(ld_x, 48)
                for u, (b, hf, m) in enumerate(UNITS):
                    if u >= 4:
                        pe.wait_ge(qk_rest, u - 3)
                    t0 = b * T + hf * HALF
                    for k in range(KD):
                        last = mm(ring(u), wqkv[:, k, m * P:(m + 1) * P], xT[:, k, t0:t0 + HALF],
                                  start=(k == 0), stop=(k == KD - 1))
                    last.then_inc(qk_ps, 1)
                for tt in range(B * TT):
                    if tt >= 2:
                        pe.wait_ge(v_done, tt - 1)
                    for k in range(KD):
                        last = mm(PB[2][:, HALF * (tt % 2):HALF * (tt % 2) + D], xT[:, k, tt * P:(tt + 1) * P],
                                  wqkv[:, k, 2 * D:3 * D], start=(k == 0), stop=(k == KD - 1))
                    last.then_inc(v_ps, 1)
                pe.wait_ge(qk_rest, len(UNITS))
                for v in range(KD * N // HALF):
                    e, n = v % KD, v // KD
                    if v >= 4:
                        pe.wait_ge(c1_done, v - 3)
                    for k in range(KD):
                        last = mm(ring(v), wc1x[:, k, e * P:(e + 1) * P], xT[:, k, n * HALF:(n + 1) * HALF],
                                  start=(k == 0), stop=(k == KD - 1))
                    last.then_inc(c1_ps, 1)
                pe.wait_ge(fpT_ready, 1)
                pe.wait_ge(ld_pe, 16)
                pe.wait_ge(v_done, B * TT)
                for n in range(T // HALF):
                    for k in range(KD):
                        last = mm(PB[2][0:B, n * HALF:(n + 1) * HALF], fpT[:, k, :], peT[:, k, n * HALF:(n + 1) * HALF],
                                  start=(k == 0), stop=(k == KD - 1))
                last.then_inc(fa_ps, 1)
                pe.wait_ge(c1_done, KD * N // HALF)
                pe.wait_ge(xs_ready, KD * B)
                for b in range(B):
                    for k in range(KD):
                        last = mm(PB[1][:, HALF + b * D:HALF + (b + 1) * D], xsB[:, k, b, :], wqkv[:, k, 2 * D:3 * D],
                                  start=(k == 0), stop=(k == KD - 1))
                last.then_inc(vs_ps, 1)
                for tt in range(B * TT):
                    for k in range(KD):
                        last = mm(PB[3][:, tt * H0:(tt + 1) * H0], c1T[:, k, tt * P:(tt + 1) * P], wc2[:, k, :],
                                  start=(k == 0), stop=(k == KD - 1))
                last.then_inc(z_ps, 1)
                pe.wait_ge(fa_ready, 1)
                for it in range(TT):
                    last = tr(misc(P, 320 + 2 * it, 322 + 2 * it), faw[:, 2, it * P:(it + 1) * P], ident[0:B, 0:B])
                last.then_inc(faT_ps, 1)


def stage_attention0(nc, G, A):
    with ExitStack() as ctx:
        sb = lambda n, s, dt=F32: ctx.enter_context(nc.sbuf_tensor(n, s, dt))
        sem = lambda n: ctx.enter_context(nc.semaphore(n))
        PB, scr, ident = G["PB"], G["scr"], G["ident"]
        GB = H0 // HG
        qa = [sb(f"a_qa{s}", [KA, HG, T], BF16) for s in range(GB)]
        ka = [sb(f"a_ka{s}", [KA, HG, T], BF16) for s in range(GB)]
        vst = [sb(f"a_vst{s}", [P, TT, HG, 32]) for s in range(2)]
        pt = [sb(f"a_pt{s}", [P, HG, HALF]) for s in range(2)]
        mx = [sb(f"a_mx{s}", [P, HG * TT, 2]) for s in range(2)]
        mcol = [sb(f"a_mcol{s}", [P, HG * TT]) for s in range(2)]
        mrow = [sb(f"a_mrow{s}", [HG * TT, 3, P], BF16) for s in range(2)]
        mrest = [sb(f"a_mrest{s}", [HG * TT, P]) for s in range(2)]
        passed = G["passed"]
        consts, staged = sem("a_consts"), [sem(f"a_staged{s}") for s in range(GB)]
        shifted = [sem(f"a_shifted{s}") for s in range(GB)]
        v_in, st_ps, p_ready, pv_done = sem("a_v_in"), sem("a_st_ps"), sem("a_p_ready"), sem("a_pv_done")
        o_out = [sem("a_o_out0"), sem("a_o_out1")]
        max_ps, max_done, m_ready, m_rows, row_step, row_ready = (sem(n) for n in (
            "a_max_ps", "a_max_done", "a_m_ready", "a_m_rows", "a_row_step", "a_row_ready"))
        STEPS = 2 * TT
        MU = HG * TT * 2
        SHARE = 5
        DMAS = 16 * len(Q_PART) * 2
        OT = G["OT"]

        mbank = (PB[3][:, 0:HALF], PB[3][:, HALF:T], PB[2][:, HALF:T])
        MB = len(mbank)

        def following(b, k):
            return (b, k + 1) if k + 1 < GB else (1 - b, 0)

        with nc.Block() as block:
            @block.sync
            def _(sp):
                def stage(slot, b, k):
                    for s, (dst, which) in enumerate(((qa, Q_PART), (ka, K_PART))):
                        for c, part in enumerate(which):
                            r0 = k * HG * HD0
                            src = scr[s, part, r0:r0 + HG * HD0, ds(b * T, T)].rearrange("(h p) t -> p h t", p=HD0)
                            sp.dma_start(dst[slot][c * HD0:(c + 1) * HD0, :, :], src).then_inc(staged[slot], 16)

                def shift_rows(slot, par, count):
                    sp.wait_ge(row_ready, count)
                    for c in range(3):
                        sp.dma_start(qa[slot][KS + c:KS + c + 1, :, :], mrow[par][:, c, :]).then_inc(shifted[slot], 16)

                for k in range(GB - 1):
                    stage(k, 0, k)
                shift_rows(0, 0, 1)
                with sp.Fori(0, B) as b:
                    for k in range(GB):
                        sp.wait_ge(pv_done, STEPS * (b * GB + k))
                        sp.sem_inc(passed, 1)
                        b3, k3 = (b, GB - 1) if k == 0 else (1 - b, k - 1)
                        stage(k3, b3, k3)
                        shift_rows((k + 1) % GB, (k + 1) % 2, b * GB + k + 2)
                for s in range(GB):
                    sp.wait_ge(staged[s], DMAS * (B + (s < GB - 1)))
                    sp.wait_ge(shifted[s], 48 * (B + (s == 0)))

            @block.gpsimd
            def _(pool):
                nc.clear_and_free_semaphores(G["early_sems"])
                for s in range(GB):
                    nc.gpsimd.memset(ka[s][KS:KA, :, :], 1.0).then_inc(consts, 1)
                pool.wait_ge(consts, GB)
                for s in range(2):
                    nc.gpsimd.memset(vst[s][:, :, :, HD0:HD0 + 1], 1.0).then_inc(consts, 1)
                    nc.gpsimd.memset(vst[s][:, :, :, HD0 + 1:32], 0.0).then_inc(consts, 1)

                def stage_v(par, b, k):
                    w = HG * HD0
                    src = G["v"][:, ds(2 * b + k // 2, 1), :, (k % 2) * w:(k % 2 + 1) * w]
                    nc.gpsimd.tensor_copy(vst[par][:, :, :, 0:HD0],
                                          src.rearrange("p o j (h d) -> p (o j) h d", h=HG)).then_inc(v_in, 1)

                stage_v(0, 0, 0)
                with pool.Fori(0, B) as b:
                    for k in range(GB):
                        pool.wait_ge(pv_done, STEPS * (b * GB + k))
                        pool.sem_inc(passed, 1)
                        stage_v((k + 1) % 2, *following(b, k))

            @block.scalar
            def _(act):
                with act.Fori(0, B) as b:
                    for k in range(GB):
                        g = b * GB + k
                        for n in range(STEPS):
                            act.wait_ge(pv_done, STEPS * g + max(n - 1, 0))
                            for ab in range(2):
                                act.wait_ge(st_ps, 2 * STEPS * g + 2 * n + ab + 1)
                                nc.scalar.activation(pt[n % 2][:, 2 * ab:2 * ab + 2, :].rearrange("p h t -> p (h t)"),
                                                     PB[ab][:, :], ACT.Exp, scale=HD0 ** -0.5).then_inc(p_ready, 1)
                            if n == TT + 1:
                                act.wait_ge(pv_done, STEPS * g + TT)
                                nc.scalar.activation(OT[:, ds(g, 1), 0:HALF].rearrange("p o t -> p (o t)"),
                                                     PB[2][:, 0:HALF], ACT.Copy).then_inc(o_out[0], 1)

            @block.vector
            def _(dve):
                V = nc.vector

                def maxima(par, g, when=None):
                    for u in range(MU):
                        dve.wait_ge(max_ps, MU * g + u + 1)
                        V.reduce_max(mx[par][:, u // 2, u % 2:u % 2 + 1], mbank[u % MB], X).then_inc(max_done, 1)
                    dve.wait_ge(max_done, MU * (g + 1))
                    V.reduce_max(mcol[par][:, :], mx[par][:, :, :], X).then_inc(m_ready, 1)

                def rows(par, g, old):
                    if old is not None:
                        dve.wait_ge(*old)
                    dve.wait_ge(m_rows, g + 1)
                    src = PB[3][0:HG * TT, 0:P]
                    V.tensor_scalar_mul(mrow[par][:, 0, :], src, -1.0).then_inc(row_step, 1)
                    dve.wait_ge(row_step, 3 * g + 1)
                    V.scalar_tensor_tensor(out=mrest[par][:, :], in0=src, scalar=-1.0, in1=mrow[par][:, 0, :],
                                           op0=ALU.mult, op1=ALU.subtract).then_inc(row_step, 1)
                    dve.wait_ge(row_step, 3 * g + 2)
                    V.tensor_copy(mrow[par][:, 1, :], mrest[par][:, :]).then_inc(row_step, 1)
                    dve.wait_ge(row_step, 3 * g + 3)
                    V.tensor_tensor(mrow[par][:, 2, :], mrest[par][:, :], mrow[par][:, 1, :],
                                    ALU.subtract).then_inc(row_ready, 1)

                maxima(0, 0)
                rows(0, 0, None)
                with dve.Fori(0, B) as b:
                    for k in range(GB):
                        g, par = b * GB + k, (k + 1) % 2
                        maxima(par, g + 1)
                        rows(par, g + 1, (shifted[(k - 1) % GB], 48 * (b + 1) if k else 48 * b))
                        dve.wait_ge(pv_done, STEPS * g + STEPS)
                        V.tensor_copy(OT[:, ds(g, 1), HALF:T].rearrange("p o t -> p (o t)"),
                                      PB[2][:, 0:HALF]).then_inc(o_out[1], 1)

            @block.tensor
            def _(pe):
                mm = nc.tensor.matmul

                def max_unit(slot, u):
                    h, it, jh = u // (2 * TT), u // 2 % TT, u % 2
                    mm(mbank[u % MB], qa[slot][0:KS, h, it * P:(it + 1) * P],
                       ka[slot][0:KS, h, jh * HALF:(jh + 1) * HALF], start=True, stop=True).then_inc(max_ps, 1)

                def max_rows(par, g):
                    pe.wait_ge(m_ready, g + 1)
                    nc.tensor.transpose(PB[3][0:HG * TT, 0:P], mcol[par][:, :], ident[:, :]).then_inc(m_rows, 1)

                def weighted(k, g, n):
                    ih, jt = n // TT, n % TT
                    if jt == 0:
                        pe.wait_ge(o_out[1 - ih], g + ih)
                    pe.wait_ge(p_ready, 2 * STEPS * g + 2 * n + 2)
                    for q in range(HG):
                        last = mm(PB[2][32 * q:32 * q + 32, 0:HALF], vst[k % 2][:, jt, q, :],
                                  pt[n % 2][:, q, :], start=(jt == 0), stop=(jt == TT - 1))
                    last.then_inc(pv_done, 1)

                pe.wait_ge(consts, GB + 4)
                pe.wait_ge(staged[0], DMAS)
                for u in range(MU):
                    if u >= MB:
                        pe.wait_ge(max_done, u - MB + 1)
                    max_unit(0, u)
                max_rows(0, 0)
                with pe.Fori(0, B) as b:
                    for k in range(GB):
                        g, nxt = b * GB + k, (k + 1) % GB
                        pe.wait_ge(shifted[k], 48 * (b + 1))
                        pe.wait_ge(v_in, g + 1)
                        units = iter(range(MU))

                        def maxima(count):
                            for u in itertools.islice(units, count):
                                pe.wait_ge(max_done, MU * (g + 1) + max(u - MB + 1, 0))
                                max_unit(nxt, u)

                        for n in range(STEPS):
                            ih, jt = n // TT, n % TT
                            for ab in range(2):
                                pe.wait_ge(p_ready, 2 * STEPS * g + (2 * n + ab - 1 if n else 0))
                                for q in (2 * ab, 2 * ab + 1):
                                    last = mm(PB[ab][:, (q % 2) * HALF:(q % 2 + 1) * HALF], ka[k][:, q, jt * P:(jt + 1) * P],
                                              qa[k][:, q, ih * HALF:(ih + 1) * HALF], start=True, stop=True)
                                last.then_inc(st_ps, 1)
                                if n == 0 and ab == 0:
                                    pe.wait_ge(staged[nxt], DMAS * (b + 1) if k < GB - 1 else DMAS * (b + 2))
                                    pe.wait_ge(row_ready, g + 1)
                                maxima(1)
                            maxima(1)
                            if n >= 1:
                                weighted(k, g, n - 1)
                            maxima(SHARE - 3)
                            if n == STEPS - 2:
                                max_rows((k + 1) % 2, g + 1)
                        weighted(k, g, STEPS - 1)


def stage_out0(nc, G, A):
    with ExitStack() as ctx:
        sb = lambda n, s, dt=F32: ctx.enter_context(nc.sbuf_tensor(n, s, dt))
        sem = lambda n: ctx.enter_context(nc.semaphore(n))
        PB, ident, OT = G["PB"], G["ident"], G["OT"]
        wout = sb("o_wout", [P, KD, D])
        bout = sb("o_bout", [P, KD])
        boutB = sb("o_boutB", [P, D])
        outT = sb("o_outT", [P, KD, N])
        dg = sb("o_dg", [P, 2, 2, H0])
        ot = sb("o_ot", [P, 2, D])
        og = sb("o_og", [P, 2, D])
        xt = sb("o_xt", [P, KD, HALF])
        x0 = sb("o_x0", [P, 2, D])
        csum = sb("o_csum", [P, KD, N // HALF])
        ld, t1_ps, ot_step, og_ready, t2_ps, outT_ready, x0_ps, x0_done, xt_ps, xt_done = (sem("o_" + n) for n in (
            "ld", "t1_ps", "ot_step", "og_ready", "t2_ps", "outT_ready", "x0_ps", "x0_done", "xt_ps", "xt_done"))
        x0_high, x0_low, xt_high, xt_low = (sem("o_" + n) for n in ("x0_high", "x0_low", "xt_high", "xt_low"))
        X0T, X0 = G["X0T"], G["X0"]
        TILES = B * TT

        with nc.Block() as block:
            @block.sync
            def _(sp):
                sp.dma_start(wout[:, :, :], A["woutT"].rearrange("(k p) n -> p k n", p=P)).then_inc(ld, 16)
                sp.dma_start(bout[:, :], A["bout"]).then_inc(ld, 16)
                sp.dma_start(boutB[:, :], A["boutB"]).then_inc(ld, 16)

            @block.tensor
            def _(pe):
                mm, tr = nc.tensor.matmul, nc.tensor.transpose
                pe.wait_ge(ld, 48)
                for i in range(TILES + 2):
                    if i < TILES:
                        if i >= 2:
                            pe.wait_ge(og_ready, i - 1)
                        b, it = i // TT, i % TT
                        for hg in range(4):
                            last = tr(PB[0][:, HALF * (i % 2) + hg * P:HALF * (i % 2) + (hg + 1) * P],
                                      OT[:, 4 * b + hg, it * P:(it + 1) * P], ident[:, :])
                        last.then_inc(t1_ps, 1)
                    if 1 <= i <= TILES:
                        t = i - 1
                        pe.wait_ge(og_ready, t + 1)
                        if t >= 2:
                            pe.wait_ge(outT_ready, t - 1)
                        for k in range(KD):
                            last = tr(PB[1][:, HALF * (t % 2) + k * P:HALF * (t % 2) + (k + 1) * P],
                                      og[:, t % 2, k * P:(k + 1) * P], ident[:, :])
                        last.then_inc(t2_ps, 1)
                    if i >= 2:
                        t = i - 2
                        pe.wait_ge(outT_ready, t + 1)
                        if t >= 2:
                            pe.wait_ge(x0_done, t - 1)
                        for k in range(KD):
                            last = mm(PB[2][:, HALF * (t % 2):HALF * (t % 2) + D], outT[:, k, t * P:(t + 1) * P],
                                      wout[:, k, :], start=(k == 0), stop=(k == KD - 1))
                        last.then_inc(x0_ps, 1)
                        if t % 4 == 3:
                            n = t // 4
                            for m in range(KD):
                                if n >= 1:
                                    pe.wait_ge(xt_done, KD * (n - 1) + m + 1)
                                for k in range(KD):
                                    last = mm(PB[3][:, m * HALF:(m + 1) * HALF], wout[:, k, m * P:(m + 1) * P],
                                              outT[:, k, n * HALF:(n + 1) * HALF], start=(k == 0), stop=(k == KD - 1))
                                last.then_inc(xt_ps, 1)

            def project(act, n):
                for m in range(KD):
                    act.wait_ge(xt_ps, KD * n + m + 1)
                    if n >= 1:
                        act.wait_ge(xt_low, KD * (n - 1) + m + 1)
                    nc.scalar.activation(xt[:, m, :], PB[3][:, m * HALF:(m + 1) * HALF], ACT.Identity,
                                         bias=bout[:, m:m + 1], accum_out=csum[:, m, n:n + 1]).then_inc(xt_done, 1)

            @block.scalar
            def _(act):
                act.wait_ge(ld, 48)
                for t in range(TILES):
                    act.wait_ge(t2_ps, t + 1)
                    nc.scalar.activation(outT[:, :, t * P:(t + 1) * P],
                                         PB[1][:, HALF * (t % 2):HALF * (t % 2) + D].rearrange("p (k t) -> p k t", k=KD),
                                         ACT.Copy).then_inc(outT_ready, 1)
                    if t % 4 == 0 and t >= 4:
                        project(act, t // 4 - 1)
                project(act, TILES // 4 - 1)

            @block.vector
            def _(dve):
                V = nc.vector
                dve.wait_ge(ld, 48)
                link = chain(dve, ot_step)

                def split_columns(n):
                    for m in range(KD):
                        dve.wait_ge(xt_done, KD * n + m + 1)
                        V.tensor_copy(X0T[0][:, m, n * HALF:(n + 1) * HALF], xt[:, m, :]).then_inc(xt_high, 1)

                for t in range(TILES + 1):
                    if t < TILES:
                        b, it, s = t // TT, t % TT, t % 2
                        dve.wait_ge(t1_ps, t + 1)
                        if t >= 2:
                            dve.wait_ge(t2_ps, t - 1)
                        heads = PB[0][:, HALF * s:HALF * s + HALF].rearrange("p (h r) -> p h r", r=32)
                        link(V.tensor_tensor(dg[:, s, 0, :], heads[:, :, HD0], G["gate"][:, t * H0:(t + 1) * H0], ALU.mult))
                        link(V.reciprocal(dg[:, s, 1, :], dg[:, s, 0, :]))
                        link(V.tensor_tensor(ot[:, s, :].rearrange("p (h d) -> p h d", d=HD0), heads[:, :, 0:HD0],
                                             dg[:, s, 1, :].unsqueeze(2).to_broadcast([P, H0, HD0]), ALU.mult))
                        V.scalar_tensor_tensor(out=og[:, s, :], in0=G["vsum"][:, b, :], scalar=G["fa"][:, it, b:b + 1],
                                               in1=ot[:, s, :], op0=ALU.mult, op1=ALU.add).then_inc(og_ready, 1)
                    if t >= 1:
                        r = t - 1
                        dve.wait_ge(x0_ps, r + 1)
                        if r >= 2:
                            dve.wait_ge(x0_low, r - 1)
                        V.tensor_tensor(x0[:, r % 2, :], PB[2][:, HALF * (r % 2):HALF * (r % 2) + D], boutB[:, :],
                                        ALU.add).then_inc(x0_done, 1)
                        dve.wait_ge(x0_done, r + 1)
                        V.tensor_copy(X0[0][:, r, :], x0[:, r % 2, :]).then_inc(x0_high, 1)
                        if r % 4 == 0 and r >= 4:
                            split_columns(r // 4 - 1)
                split_columns(TILES // 4 - 1)
                link(V.tensor_reduce(G["csum"][:, :, :], csum[:, :, :].rearrange("p k (b n) -> p k b n", b=B), X, ALU.add))
                link(V.tensor_scalar_mul(G["csum"][:, :, :], G["csum"][:, :, :], 0.5))

            @block.gpsimd
            def _(pool):
                V = nc.gpsimd
                for t in range(TILES):
                    pool.wait_ge(x0_high, t + 1)
                    V.tensor_tensor(X0[1][:, t, :], x0[:, t % 2, :], X0[0][:, t, :].bitcast(F32),
                                    ALU.subtract).then_inc(x0_low, 1)
                    if t % 4 == 1 and t >= 4 or t == TILES - 1:
                        n = t // 4 - (t < TILES - 1)
                        for m in range(KD):
                            ts = slice(n * HALF, (n + 1) * HALF)
                            pool.wait_ge(xt_high, KD * n + m + 1)
                            V.tensor_tensor(X0T[1][:, m, ts], xt[:, m, :], X0T[0][:, m, ts].bitcast(F32),
                                            ALU.subtract).then_inc(xt_low, 1)


def stage_moe(nc, G, A):
    with ExitStack() as ctx:
        sb = lambda n, s, dt=F32: ctx.enter_context(nc.sbuf_tensor(n, s, dt))
        sem = lambda n: ctx.enter_context(nc.semaphore("f_" + n))
        PB, ident, X0T, X0 = G["PB"], G["ident"], G["X0T"], G["X0"]
        TILES = B * TT
        NT = CS // P
        phi = sb("f_phi", [P, KD, CS])
        phis = [sb(f"f_phi_{c}", [P, KD, CS], F32R) for c in range(2)]
        wex = sb("f_wex", [P, CE, KD, D])
        bex = sb("f_bex", [P, NT, D])
        l1s = sb("f_l1s", [P, 2, CS])
        dl = sb("f_dl", [P, 2, CS])
        th = sb("f_th", [P, 2, CS])
        ths = [sb(f"f_th_{c}", [P, 2, CS], F32R) for c in range(2)]
        E = sb("f_E", [P, TILES, CS])
        ET = sb("f_ET", [P, 2, NT, P])
        slT = sb("f_slT", [P, B, KD, CS])
        ysb = sb("f_ysb", [P, NT, B, D])
        mc = sb("f_mc", [P, TILES])
        nmc = sb("f_nmc", [P, TILES])
        dc = sb("f_dc", [P, TILES])
        mrun = sb("f_mrun", [P, 2, TILES])
        arg = sb("f_arg", [P, 2, TILES])
        fac = sb("f_fac", [P, 2, TILES])
        dtmp = sb("f_dtmp", [P, 2, TILES])
        passed = G["passed"]
        ld_phi, w_in, init = sem("ld_phi"), sem("w_in"), sem("init")
        lg_ps, l1_sb, mx_done, neg_done, dl_done, e_done, th_done, sl_done = (sem(n) for n in (
            "lg_ps", "l1_sb", "mx_done", "neg_done", "dl_done", "e_done", "th_done", "sl_done"))
        sl_out, et_ps, et_out, y_ps, y_out, oc_ps, oc_out = (sem(n) for n in (
            "sl_out", "et_ps", "et_out", "y_ps", "y_out", "oc_ps", "oc_out"))
        run_step, run_arg, run_fac = sem("run_step"), sem("run_arg"), sem("run_fac")
        phi_high, phi_low, th_high, th_low = sem("phi_high"), sem("phi_low"), sem("th_high"), sem("th_low")
        LW = 48
        O, DEN = G["O"], G["den"]

        with nc.Block() as block:
            @block.sync
            def _(sp):
                sp.dma_start(phi[:, :, :], A["phi"][:, 0:CS].rearrange("(k p) s -> p k s", p=P)).then_inc(ld_phi, 16)
                with sp.Fori(0, CH) as c:
                    sp.wait_ge(phi_low, c + 1)
                    sp.sem_inc(passed, 1)
                    sp.dma_start(phi[:, :, :], A["phi"][:, ds((c + 1) * CS, CS)].rearrange("(k p) s -> p k s", p=P)).then_inc(ld_phi, 16)
                    sp.wait_ge(y_ps, NT * c)
                    sp.wait_ge(y_out, NT * c)
                    sp.sem_inc(passed, 1)
                    for k in range(KD):
                        sp.dma_start(wex[:, :, k, :], A["W"][ds(c * CE, CE), k * P:(k + 1) * P, :]
                                     .rearrange("n p e -> p n e")).then_inc(w_in, 16)
                    sp.dma_start(bex[:, :, :], A["bexp"][ds(c * CS, CS), :]
                                 .rearrange("(t p) e -> p t e", p=P)).then_inc(w_in, 16)

            @block.gpsimd
            def _(pool):
                nc.gpsimd.memset(O[:, :, :], 0.0).then_inc(init, 1)
                nc.gpsimd.memset(DEN[:, :], 0.0).then_inc(init, 1)
                nc.gpsimd.memset(mrun[:, 0, :], LOWEST).then_inc(init, 1)

            @block.tensor
            def _(pe):
                mm, tr = nc.tensor.matmul, nc.tensor.transpose
                with pe.Fori(0, CH) as c:
                    def dispatch(mt):
                        pe.wait_ge(th_low, TT * c + mt + 1)
                        for b in range(B):
                            for k in range(KD):
                                for n, (cx, ct) in enumerate(PRODUCTS):
                                    last = mm(PB[2 + b][:, k * HALF:(k + 1) * HALF], X0[cx][:, b * TT + mt, k * P:(k + 1) * P],
                                              ths[ct][:, mt % 2, :], start=(mt == n == 0),
                                              stop=(mt == TT - 1 and n == len(PRODUCTS) - 1))
                        last.then_inc(sl_done, 1)

                    def expo_rows(t):
                        for n in range(NT):
                            last = tr(PB[0][:, HALF * (t % 2) + n * P:HALF * (t % 2) + (n + 1) * P],
                                      E[:, t, n * P:(n + 1) * P], ident[:, :])
                        last.then_inc(et_ps, 1)

                    pe.wait_ge(phi_low, c + 1)
                    for mt in range(TT):
                        if mt < 2:
                            pe.wait_ge(et_out, TILES * c)
                            pe.wait_ge(oc_out, TILES * c)
                        else:
                            pe.wait_ge(e_done, TT * c + mt - 1)
                            pe.wait_ge(dl_done, TT * c + mt - 1)
                        for b in range(B):
                            for n, (cx, cp) in enumerate(PRODUCTS):
                                for k in range(KD):
                                    last = mm(PB[mt % 2][:, b * HALF:(b + 1) * HALF],
                                              X0T[cx][:, k, b * T + mt * P:b * T + (mt + 1) * P], phis[cp][:, k, :],
                                              start=(n == k == 0), stop=(n == len(PRODUCTS) - 1 and k == KD - 1))
                        last.then_inc(lg_ps, 1)
                        if mt == 0:
                            pe.wait_ge(y_out, NT * c)
                        elif mt >= 2:
                            dispatch(mt - 2)
                    dispatch(TT - 2)
                    dispatch(TT - 1)
                    pe.wait_ge(e_done, TT * c + TT)
                    pe.wait_ge(dl_done, TT * c + TT)
                    expo_rows(0)
                    expo_rows(1)
                    pe.wait_ge(sl_out, B * KD * (c + 1))
                    pe.wait_ge(w_in, LW * (c + 1))
                    for n in range(NT):
                        for b in range(B):
                            for k in range(KD):
                                for q in range(4):
                                    s0 = n * P + 32 * q
                                    last = mm(PB[2 + n // 2][32 * q:32 * q + 32, (n % 2) * HALF + b * D:(n % 2) * HALF + (b + 1) * D],
                                              slT[:, b, k, s0:s0 + 32], wex[:, 4 * n + q, k, :],
                                              start=(k == 0), stop=(k == KD - 1))
                        last.then_inc(y_ps, 1)
                    pe.wait_ge(y_out, NT * (c + 1))
                    for t in range(TILES):
                        pe.wait_ge(et_out, TILES * c + t + 1)
                        if t >= 2:
                            pe.wait_ge(oc_out, TILES * c + t - 1)
                        for n in range(NT):
                            last = mm(PB[1][:, HALF * (t % 2):HALF * (t % 2) + D], ET[:, t % 2, n, :],
                                      ysb[:, n, t // TT, :], start=(n == 0), stop=(n == NT - 1))
                        last.then_inc(oc_ps, 1)
                        if t + 2 < TILES:
                            expo_rows(t + 2)

            @block.scalar
            def _(act):
                S = nc.scalar.activation
                act.wait_ge(init, 3)
                with act.Fori(0, CH) as c:
                    for mt in range(TT):
                        s, a = mt % 2, TT * c + mt
                        act.wait_ge(lg_ps, a + 1)
                        act.wait_ge(dl_done, TT * c + max(mt - 1, 0))
                        S(l1s[:, s, :], PB[s][:, HALF:2 * HALF], ACT.Copy).then_inc(l1_sb, 1)
                        act.wait_ge(neg_done, a + 1)
                        act.wait_ge(dl_done, a + 1)
                        for b in range(B):
                            t = b * TT + mt
                            last = S(E[:, t, :], PB[s][:, b * HALF:(b + 1) * HALF], ACT.Exp, bias=nmc[:, t:t + 1],
                                     accum_out=dc[:, t:t + 1])
                        last.then_inc(e_done, 1)
                        act.wait_ge(th_low, TT * c + max(mt - 1, 0))
                        S(th[:, s, :], dl[:, s, :], ACT.Tanh, scale=0.5).then_inc(th_done, 1)
                    act.wait_ge(run_arg, c + 1)
                    S(fac[:, :, :], arg[:, :, :], ACT.Exp).then_inc(run_fac, 1)
                    act.wait_ge(sl_done, TT * (c + 1))
                    for b in range(B):
                        for k in range(KD):
                            S(slT[:, b, k, :], PB[2 + b][:, k * HALF:(k + 1) * HALF], ACT.Identity,
                              bias=G["csum"][:, k, b:b + 1], scale=0.5 - b).then_inc(sl_out, 1)
                    for t in range(TILES):
                        act.wait_ge(et_ps, TILES * c + t + 1)
                        act.wait_ge(oc_ps, TILES * c + max(t - 1, 0))
                        S(ET[:, t % 2, :, :].rearrange("p n m -> p (n m)"), PB[0][:, HALF * (t % 2):HALF * (t % 2) + HALF],
                          ACT.Copy).then_inc(et_out, 1)

            @block.vector
            def _(dve):
                V = nc.vector
                dve.wait_ge(init, 3)

                def split_phi(c):
                    dve.wait_ge(ld_phi, 16 * (c + 1))
                    V.tensor_copy(phis[0][:, :, :], phi[:, :, :]).then_inc(phi_high, 1)
                    dve.wait_ge(phi_high, c + 1)
                    V.tensor_tensor(phis[1][:, :, :], phi[:, :, :], phis[0][:, :, :].bitcast(F32), ALU.subtract).then_inc(phi_low, 1)

                split_phi(0)
                with dve.Fori(0, CH) as c:
                    def split_dispatch(mt):
                        s, a = mt % 2, TT * c + mt
                        dve.wait_ge(th_done, a + 1)
                        dve.wait_ge(sl_done, TT * c + max(mt - 1, 0))
                        V.tensor_copy(ths[0][:, s, :], th[:, s, :]).then_inc(th_high, 1)
                        dve.wait_ge(th_high, a + 1)
                        V.tensor_tensor(ths[1][:, s, :], th[:, s, :], ths[0][:, s, :].bitcast(F32), ALU.subtract).then_inc(th_low, 1)

                    for mt in range(TT):
                        s, a = mt % 2, TT * c + mt
                        dve.wait_ge(l1_sb, a + 1)
                        pair = mc[:, :].rearrange("p (b t) -> p b t", b=B)[:, :, mt]
                        npair = nmc[:, :].rearrange("p (b t) -> p b t", b=B)[:, :, mt]
                        V.reduce_max(pair, PB[s][:, :].rearrange("p (b n) -> p b n", b=B), X).then_inc(mx_done, 1)
                        dve.wait_ge(th_done, TT * c + max(mt - 1, 0))
                        V.tensor_tensor(dl[:, s, :], PB[s][:, 0:HALF], l1s[:, s, :], ALU.subtract).then_inc(dl_done, 1)
                        dve.wait_ge(mx_done, a + 1)
                        V.tensor_scalar_mul(npair, pair, -1.0).then_inc(neg_done, 1)
                        if mt >= 1:
                            split_dispatch(mt - 1)
                    split_dispatch(TT - 1)
                    split_phi(c + 1)
                    link = chain(dve, run_step, 7 * c)
                    link(V.tensor_tensor(mrun[:, 1, :], mrun[:, 0, :], mc[:, :], ALU.max))
                    link(V.tensor_tensor(arg[:, 0, :], mrun[:, 0, :], mrun[:, 1, :], ALU.subtract))
                    V.tensor_tensor(arg[:, 1, :], mc[:, :], mrun[:, 1, :], ALU.subtract).then_inc(run_arg, 1)
                    link(V.tensor_copy(mrun[:, 0, :], mrun[:, 1, :]))
                    dve.wait_ge(run_fac, c + 1)
                    link(V.tensor_tensor(dtmp[:, 0, :], DEN[:, :], fac[:, 0, :], ALU.mult))
                    link(V.tensor_tensor(dtmp[:, 1, :], dc[:, :], fac[:, 1, :], ALU.mult))
                    link(V.tensor_tensor(DEN[:, :], dtmp[:, 0, :], dtmp[:, 1, :], ALU.add))
                    link(V.tensor_tensor(O[:, :, :], O[:, :, :], fac[:, 0, :].unsqueeze(2).to_broadcast([P, TILES, D]),
                                         ALU.mult))
                    dve.wait_ge(w_in, LW * (c + 1))
                    for n in range(NT):
                        dve.wait_ge(y_ps, NT * c + n + 1)
                        V.tensor_tensor(ysb[:, n, :, :],
                                        PB[2 + n // 2][:, (n % 2) * HALF:(n % 2 + 1) * HALF].rearrange("p (b e) -> p b e", b=B),
                                        bex[:, n, :].unsqueeze(1).to_broadcast([P, B, D]), ALU.add).then_inc(y_out, 1)
                    for t in range(TILES):
                        dve.wait_ge(oc_ps, TILES * c + t + 1)
                        V.scalar_tensor_tensor(out=O[:, t, :], in0=PB[1][:, HALF * (t % 2):HALF * (t % 2) + D],
                                               scalar=fac[:, 1, t:t + 1], in1=O[:, t, :], op0=ALU.mult,
                                               op1=ALU.add).then_inc(oc_out, 1)
                    dve.wait_ge(oc_out, TILES * (c + 1))


def load_attention1(sp, G, A, l):
    sp.dma_start(G["wqkv1_raw"][:, :, :], A["wqkv1"][l].rearrange("(k p) n -> p k n", p=P)).then_inc(G["ld_att"], 16)
    sp.dma_start(G["wo"][:, :, :], A["wo"][l].rearrange("(k p) n -> p k n", p=P)).then_inc(G["ld_att"], 16)


def load_ffn1(sp, G, A, l):
    sp.dma_start(G["w1"][:, :, :], A["w1"][l].rearrange("(k p) n -> p k n", p=P)).then_inc(G["ld_ffn"], 16)
    sp.dma_start(G["w2"][:, :, :], A["w2"][l].rearrange("(k p) n -> p k n", p=P)).then_inc(G["ld_ffn"], 16)
    for name in ("lg", "lb", "b1", "b2"):
        sp.dma_start(G[name][:, :], A[name][l]).then_inc(G["ld_ffn"], 16)


LD_ATT, LD_FFN = 32, 96


def split_wqkv(nc, dve, G, l):
    V, raw, (high, low), done = nc.vector, G["wqkv1_raw"], G["wqkv1"], G["wqkv_split"]
    dve.wait_ge(G["ld_att"], LD_ATT * (l + 1))
    V.tensor_copy(low[:, :, :], raw[:, :, :]).then_inc(done, 1)
    dve.wait_ge(done, 3 * l + 1)
    V.tensor_tensor(low[:, :, :], raw[:, :, :], low[:, :, :].bitcast(F32), ALU.subtract).then_inc(done, 1)
    dve.wait_ge(done, 3 * l + 2)
    V.tensor_copy(high[:, :, :], raw[:, :, :]).then_inc(done, 1)


def stage_rotate(nc, G, A):
    with ExitStack() as ctx:
        sb = lambda n, s, dt=F32: ctx.enter_context(nc.sbuf_tensor(n, s, dt))
        sem = lambda n: ctx.enter_context(nc.semaphore("r_" + n))
        PB, ident, xr = G["PB"], G["ident"], G["xr"]
        TILES = B * TT
        x1T = sb("r_x1T", [P, KD, N])
        rden = sb("r_rden", [P, TILES])
        on = sb("r_on", [P, 2, D])
        step, on_ready, t_ps, x1_done, rot_ps, rot_out, zeroed = (sem(n) for n in (
            "step", "on_ready", "t_ps", "x1_done", "rot_ps", "rot_out", "zeroed"))
        with nc.Block() as block:
            @block.sync
            def _(sp):
                sp.dma_start(x1T[:, :, :], A["xT"].rearrange("(k p) n -> p k n", p=P)).then_inc(G["ld_x1"], 16)
                load_attention1(sp, G, A, 0)
                sp.dma_start(G["mask"][:, :], A["mask"]).then_inc(G["ld_tab"], 16)
                sp.dma_start(G["qks"][:, :, :, :], A["qks"]).then_inc(G["ld_tab"], 16)
                sp.wait_ge(x1_done, TILES)
                sp.dma_start(G["x1"].rearrange("(k p) n -> p k n", p=P), x1T[:, :, :]).then_inc(G["x1_out"], 16)
                sp.wait_ge(G["x1_out"], 16)

            @block.gpsimd
            def _(pool):
                nc.gpsimd.memset(xr[:, :, :, 0:1], 0.0).then_inc(zeroed, 1)

            @block.vector
            def _(dve):
                V = nc.vector
                link = chain(dve, step)
                link(V.reciprocal(rden[:, :], G["den"][:, :]))
                dve.wait_ge(G["ld_x1"], 16)
                for t in range(TILES + 1):
                    if t < TILES:
                        if t >= 2:
                            dve.wait_ge(t_ps, t - 1)
                        V.tensor_scalar_mul(on[:, t % 2, :], G["O"][:, t, :], rden[:, t:t + 1]).then_inc(on_ready, 1)
                    if t >= 1:
                        r = t - 1
                        dve.wait_ge(t_ps, r + 1)
                        V.tensor_tensor(x1T[:, :, r * P:(r + 1) * P],
                                        PB[0][:, HALF * (r % 2):HALF * (r % 2) + D].rearrange("p (k t) -> p k t", k=KD),
                                        x1T[:, :, r * P:(r + 1) * P], ALU.add).then_inc(x1_done, 1)
                split_wqkv(nc, dve, G, 0)

            @block.tensor
            def _(pe):
                for t in range(TILES):
                    pe.wait_ge(on_ready, t + 1)
                    if t >= 2:
                        pe.wait_ge(x1_done, t - 1)
                    for k in range(KD):
                        last = nc.tensor.transpose(PB[0][:, HALF * (t % 2) + k * P:HALF * (t % 2) + (k + 1) * P],
                                                   on[:, t % 2, k * P:(k + 1) * P], ident[:, :])
                    last.then_inc(t_ps, 1)
                for n in range(N // HALF):
                    pe.wait_ge(x1_done, 4 * n + 4)
                    for m in range(KD):
                        if n >= 1:
                            pe.wait_ge(rot_out, KD * (n - 1) + m + 1)
                        for k in range(KD):
                            last = nc.tensor.matmul(PB[1 + m][:, 0:HALF], G["rot"][:, k, m * P:(m + 1) * P],
                                                    x1T[:, k, n * HALF:(n + 1) * HALF], start=(k == 0), stop=(k == KD - 1))
                        last.then_inc(rot_ps, 1)

            @block.scalar
            def _(act):
                for n in range(N // HALF):
                    for m in range(KD):
                        act.wait_ge(rot_ps, KD * n + m + 1)
                        c0 = 1 + (n % 2) * HALF
                        nc.scalar.activation(xr[:, m, n // 2, c0:c0 + HALF], PB[1 + m][:, 0:HALF],
                                             ACT.Copy).then_inc(rot_out, 1)
                act.wait_ge(zeroed, 1)


def stage_attention1(nc, G, A, l):
    with ExitStack() as ctx:
        sb = lambda n, s, dt=F32: ctx.enter_context(nc.sbuf_tensor(f"w{l}_{n}", s, dt))
        sem = lambda n: G["layer_sem"](f"w_{n}")
        PB, ident, xr, mask = G["PB"], G["ident"], G["xr"], G["mask"]
        wqkv, wo = G["wqkv1"], G["wo"]
        tab = [sb(f"tab{i}", [P, NW, HD1]) for i in range(4)]
        qkr = sb("qkr", [P, NW, 2 * INNER])
        vsb = sb("vsb", [P, NW, INNER])
        ss = sb("ss", [P, NW, 2 * H1])
        nrm = sb("nrm", [P, NW, 2 * H1])
        rn = sb("rn", [P, NW, 2 * H1])
        cosp = sb("cosp", [P, 2 * INNER])
        sinp = sb("sinp", [P, 2 * INNER])
        turned = sb("turned", [P, 2, 2 * INNER])
        kT = sb("kT", [P, HP, T])
        qz = sb("qz", [P, 2, HP, 2, P])
        sm = sb("sm", [P, 2, H1, 2 * WIN])
        sq = sm[:, 1, 0:4, :].rearrange("p h n -> p (h n)")
        PT = sb("PT", [P, 2, 4, P])
        with nc.sbuf_tensor(f"w{l}_hst", [P, 2, KD, T], F32R) as hst:
            pass
        oT = sb("oT", [P, HP, T])
        st = sb("st", [P, 2, 4, H1])
        (ld_tab, tabs, zeroed, h_high, h_low, qk_ps, v_ps, qk_sb, v_sb, sq_done, ss_done, n_sqrt, n_step) = (sem(n) for n in (
            "ld_tab", "tabs", "zeroed", "h_high", "h_low", "qk_ps", "v_ps", "qk_sb", "v_sb", "sq_done", "ss_done", "n_sqrt", "n_step"))
        (qn_done, cos_done, sin_done, turn_done, tq_ps, tk_ps, qz_done, kT_done, s_ps, s_masked, m_done, e_done,
         d_done, p_done, pt_ps, pt_act, pt_dve, pv_ps, oT_done, wo_ps, wo_done) = (sem(n) for n in (
            "qn_done", "cos_done", "sin_done", "turn_done", "tq_ps", "tk_ps", "qz_done", "kT_done", "s_ps", "s_masked",
            "m_done", "e_done", "d_done", "p_done", "pt_ps", "pt_act", "pt_dve", "pv_ps", "oT_done", "wo_ps", "wo_done"))
        passed = G["passed"]
        C = HD1 // 2
        NN = NW // 2

        def keys(w):
            return slice(0, 2 * WIN) if w else slice(WIN, 2 * WIN)

        with nc.Block() as block:
            @block.sync
            def _(sp):
                for i in range(4):
                    sp.dma_start(tab[i][:, :, :], A["tables"][i].rearrange("(w p) d -> p w d", p=P)).then_inc(ld_tab, 16)
                load_ffn1(sp, G, A, l)

            @block.gpsimd
            def _(pool):
                V = nc.gpsimd
                for s in range(2):
                    V.memset(qz[64:128, s, :, 0, :], 0.0).then_inc(zeroed, 1)
                    V.memset(qz[0:64, s, :, 1, :], 0.0).then_inc(zeroed, 1)
                pool.wait_ge(zeroed, 4 * (l + 1))
                pool.wait_ge(ld_tab, 16 * 4 * (l + 1))
                pool.wait_ge(G["ld_tab"], 32)
                for i in range(4):
                    V.tensor_tensor(tab[i][:, :, :], tab[i][:, :, :],
                                    G["qks"][:, l, i, :].unsqueeze(1).to_broadcast([P, NW, HD1]), ALU.mult).then_inc(tabs, 1)
                pool.wait_ge(tabs, 4 * (l + 1))
                with pool.Fori(l * B, (l + 1) * B) as b:
                    def turn(w):
                        pool.wait_ge(qn_done, NW * b + w + 1)
                        pool.wait_ge(turn_done, NW * b + w)
                        for j in range(2):
                            V.tensor_tensor(
                                cosp[:, j * INNER:(j + 1) * INNER].rearrange("p (h d) -> p h d", d=HD1),
                                qkr[:, w, j * INNER:(j + 1) * INNER].rearrange("p (h d) -> p h d", d=HD1),
                                tab[2 * j][:, w, :].unsqueeze(1).to_broadcast([P, H1, HD1]), ALU.mult).then_inc(cos_done, 1)

                    def probabilities(w, j):
                        hs = slice(4 * j, 4 * j + 4)
                        pool.wait_ge(d_done, 2 * (NW * b + w) + j + 1)
                        V.tensor_tensor(sm[:, w % 2, hs, keys(w)], sm[:, w % 2, hs, keys(w)],
                                        st[:, w % 2, 3, hs].unsqueeze(2).to_broadcast([P, 4, 2 * WIN if w else WIN]),
                                        ALU.mult).then_inc(p_done, 1)

                    turn(0)
                    for i in range(NW + 2):
                        if i >= 2:
                            probabilities(i - 2, 1)
                        if i + 1 < NW:
                            turn(i + 1)
                        if 1 <= i <= NW:
                            probabilities(i - 1, 0)

            @block.tensor
            def _(pe):
                mm, tr = nc.tensor.matmul, nc.tensor.transpose
                pe.wait_ge(G["ld_att"], LD_ATT * (l + 1))
                pe.wait_ge(G["wqkv_split"], 3 * (l + 1))
                pe.wait_ge(zeroed, 4 * (l + 1))
                with pe.Fori(l * B, (l + 1) * B) as b:
                    pe.wait_ge(oT_done, NW * b)
                    pe.wait_ge(wo_done, 2 * KD * b)
                    pe.wait_ge(pt_act, 2 * NW * b)
                    pe.wait_ge(pt_dve, 2 * NW * b)
                    def project(out, w, j):
                        for n, (ch, cw) in enumerate(PRODUCTS):
                            for k in range(KD):
                                last = mm(out, hst[:, ch, k, w * P:(w + 1) * P], wqkv[cw][:, k, j * INNER:(j + 1) * INNER],
                                          start=(n == k == 0), stop=(n == len(PRODUCTS) - 1 and k == KD - 1))
                        return last

                    for w in range(NW):
                        pe.wait_ge(h_low, KD * (2 * b + w // NN + 1))
                        if w >= 2:
                            pe.wait_ge(sq_done, NW * b + w - 1)
                        for j in range(2):
                            last = project(PB[w % 2][:, j * HALF:(j + 1) * HALF], w, j)
                        last.then_inc(qk_ps, 1)
                        if w >= 2:
                            pe.wait_ge(v_sb, NW * b + w - 1)
                        project(PB[2][:, (w % 2) * HALF:(w % 2 + 1) * HALF], w, 2).then_inc(v_ps, 1)

                    def to_rows(w):
                        pe.wait_ge(turn_done, NW * b + w + 1)
                        if w == 0:
                            pe.wait_ge(sq_done, NW * (b + 1))
                        if w >= 3:
                            pe.wait_ge(oT_done, NW * b + w - 2)
                        if w >= 1:
                            pe.wait_ge(qz_done, NW * b + w)
                        for p in range(HP):
                            last = tr(PB[0][:, p * P:(p + 1) * P], turned[:, w % 2, p * P:(p + 1) * P], ident[:, :])
                        last.then_inc(tq_ps, 1)
                        if w >= 1:
                            pe.wait_ge(kT_done, NW * b + w)
                        for p in range(HP):
                            last = tr(PB[0][:, HALF + p * P:HALF + (p + 1) * P],
                                      turned[:, w % 2, INNER + p * P:INNER + (p + 1) * P], ident[:, :])
                        last.then_inc(tk_ps, 1)

                    def scores(w):
                        pe.wait_ge(qz_done, NW * b + w + 1)
                        pe.wait_ge(kT_done, NW * b + w + 1)
                        if w == 0:
                            pe.wait_ge(v_sb, NW * (b + 1))
                        k0 = (w - 1) * WIN if w else 0
                        for h in range(H1):
                            if h % 2 == 0 and w >= 1:
                                pe.wait_ge(s_masked, H1 * (NW * b + w - 1) + h + 2)
                            c0 = (h % 4) * 2 * WIN + keys(w).start
                            n = keys(w).stop - keys(w).start
                            mm(PB[1 + h // 4][:, c0:c0 + n], qz[:, w % 2, h // 2, h % 2, :],
                               kT[:, h // 2, k0:k0 + n], start=True, stop=True).then_inc(s_ps, 1)

                    def sums(w):
                        tiles = (0, 1) if w else (1,)

                        def prob_rows(p):
                            pe.wait_ge(p_done, 2 * (NW * b + w) + p // 2 + 1)
                            if p >= 2:
                                pe.wait_ge((pt_act, pt_dve)[p % 2], 2 * (NW * b + w) + 1)
                            elif w >= 1:
                                pe.wait_ge((pt_act, pt_dve)[p % 2], 2 * (NW * b + w))
                            for e in range(2):
                                for j in tiles:
                                    c0 = (p % 2) * HALF + (2 * e + j) * P
                                    last = tr(PB[3][:, c0:c0 + P], sm[:, w % 2, 2 * p + e, j * P:(j + 1) * P], ident[:, :])
                            last.then_inc(pt_ps, 1)

                        def weighted(p):
                            pe.wait_ge((pt_act, pt_dve)[p % 2], 2 * (NW * b + w) + p // 2 + 1)
                            for j in tiles:
                                for e in range(2):
                                    h = 2 * p + e
                                    last = mm(PB[0][64 * e:64 * e + 64, p * P:(p + 1) * P],
                                              vsb[:, w - 1 + j, h * HD1:(h + 1) * HD1], PT[:, p % 2, 2 * e + j, :],
                                              start=(j == tiles[0]), stop=(j == 1))
                            last.then_inc(pv_ps, 1)

                        prob_rows(0)
                        prob_rows(1)
                        pe.wait_ge(qz_done, NW * b + min(w + 3, NW))
                        weighted(0)
                        prob_rows(2)
                        weighted(1)
                        prob_rows(3)
                        weighted(2)
                        weighted(3)

                    for i in range(NW + 2):
                        if 1 <= i <= NW:
                            scores(i - 1)
                        if i < NW:
                            to_rows(i)
                        if i >= 2:
                            sums(i - 2)
                        if i in (NW // 2 + 2, NW + 1):
                            hf = 0 if i < NW else 1
                            pe.wait_ge(oT_done, NW * b + (NW // 2) * (hf + 1))
                            pe.wait_ge(s_masked, H1 * (NW * b + min(i, NW)))
                            for m in range(KD):
                                for p in range(HP):
                                    last = mm(PB[1][:, m * HALF:(m + 1) * HALF], wo[:, p, m * P:(m + 1) * P],
                                              oT[:, p, hf * HALF:(hf + 1) * HALF], start=(p == 0), stop=(p == HP - 1))
                                last.then_inc(wo_ps, 1)
                            if i < NW:
                                pe.wait_ge(wo_done, 2 * KD * b + KD)

            @block.scalar
            def _(act):
                S = nc.scalar.activation
                with act.Fori(l * B, (l + 1) * B) as b:
                    act.wait_ge(wo_done, 2 * KD * b)
                    for w in range(NW):
                        act.wait_ge(qk_ps, NW * b + w + 1)
                        S(qkr[:, w, :], PB[w % 2][:, :], ACT.Copy).then_inc(qk_sb, 1)
                        act.wait_ge(ss_done, NW * b + w)
                        S(sq[:, :], PB[w % 2][:, :], ACT.Square).then_inc(sq_done, 1)
                        act.wait_ge(v_ps, NW * b + w + 1)
                        S(vsb[:, w, :], PB[2][:, (w % 2) * HALF:(w % 2 + 1) * HALF], ACT.Copy).then_inc(v_sb, 1)
                        if w % NN == NN - 1:
                            act.wait_ge(ss_done, NW * b + w + 1)
                            S(nrm[:, w + 1 - NN:w + 1, :], ss[:, w + 1 - NN:w + 1, :], ACT.Sqrt).then_inc(n_sqrt, 1)
                    def exponentials(w, hs):
                        for h in hs:
                            if h % 4 == 0:
                                act.wait_ge(m_done, 2 * (NW * b + w) + h // 4 + 1)
                            last = S(sm[:, w % 2, h, keys(w)], sm[:, w % 2, h, keys(w)], ACT.Exp,
                                     bias=st[:, w % 2, 1, h:h + 1], scale=QK_SCALE, accum_out=st[:, w % 2, 2, h:h + 1])
                            if h % 4 == 3:
                                last.then_inc(e_done, 1)

                    def prob_rows(w, p):
                        act.wait_ge(pt_ps, HP * (NW * b + w) + p + 1)
                        if p or w:
                            act.wait_ge(pv_ps, HP * (NW * b + w) + p - 1)
                        c0 = slice(0, 4) if w else slice(1, 4, 2)
                        S(PT[:, 0, c0, :], PB[3][:, 0:HALF].rearrange("p (a t) -> p a t", t=P)[:, c0, :],
                          ACT.Copy).then_inc(pt_act, 1)

                    for i in range(NW + 2):
                        if 1 <= i <= NW:
                            exponentials(i - 1, range(0, 2))
                        if i < NW:
                            act.wait_ge(tq_ps, NW * b + i + 1)
                            for e in range(2):
                                last = S(qz[64 * e:64 * e + 64, i % 2, :, e, :],
                                         PB[0][64 * e:64 * e + 64, 0:HALF].rearrange("p (a t) -> p a t", a=HP), ACT.Copy)
                            last.then_inc(qz_done, 1)
                        if i >= 2:
                            prob_rows(i - 2, 0)
                        if 1 <= i <= NW:
                            exponentials(i - 1, range(2, 4))
                        if i < NW:
                            act.wait_ge(tk_ps, NW * b + i + 1)
                            S(kT[:, :, i * WIN:(i + 1) * WIN], PB[0][:, HALF:2 * HALF].rearrange("p (a t) -> p a t", a=HP),
                              ACT.Copy).then_inc(kT_done, 1)
                        if 1 <= i <= NW:
                            exponentials(i - 1, range(4, 6))
                        if i >= 2:
                            prob_rows(i - 2, 2)
                        if 1 <= i <= NW:
                            exponentials(i - 1, range(6, 8))
                        if i >= 2:
                            w = i - 2
                            act.wait_ge(pv_ps, HP * (NW * b + w + 1))
                            S(oT[:, :, w * WIN:(w + 1) * WIN], PB[0][:, 0:HALF].rearrange("p (a t) -> p a t", a=HP),
                              ACT.Copy).then_inc(oT_done, 1)

            @block.vector
            def _(dve):
                V = nc.vector
                with dve.Fori(l * B, (l + 1) * B) as b:
                    dve.wait_ge(wo_done, 2 * KD * b)
                    for half in range(2):
                        t0, tn = half * (T // 2), T // 2
                        for k in range(KD):
                            c0 = t0 + (1 if k == 0 else 0)
                            src = xr[:, k, ds(b - l * B, 1), c0:c0 + tn].rearrange("p o t -> p (o t)")
                            V.tensor_copy(hst[:, 0, k, t0:t0 + tn], src).then_inc(h_high, 1)
                        for k in range(KD):
                            c0 = t0 + (1 if k == 0 else 0)
                            src = xr[:, k, ds(b - l * B, 1), c0:c0 + tn].rearrange("p o t -> p (o t)")
                            dve.wait_ge(h_high, KD * (2 * b + half) + k + 1)
                            V.tensor_tensor(hst[:, 1, k, t0:t0 + tn], src, hst[:, 0, k, t0:t0 + tn].bitcast(F32),
                                            ALU.subtract).then_inc(h_low, 1)
                    def products(w):
                        dve.wait_ge(qk_sb, NW * b + w + 1)
                        V.tensor_tensor(qkr[:, w, :].rearrange("p (h d) -> p h d", d=HD1),
                                        qkr[:, w, :].rearrange("p (h d) -> p h d", d=HD1),
                                        rn[:, w, :].unsqueeze(2).to_broadcast([P, 2 * H1, HD1]), ALU.mult).then_inc(qn_done, 1)
                        dve.wait_ge(qn_done, NW * b + w + 1)
                        dve.wait_ge(tabs, 4 * (l + 1))
                        for j in range(2):
                            src = qkr[:, w, j * INNER:(j + 1) * INNER].rearrange("p (h d) -> p h d", d=HD1)
                            dst = sinp[:, j * INNER:(j + 1) * INNER].rearrange("p (h d) -> p h d", d=HD1)
                            for r in range(2):
                                a, z = slice(r * C, (r + 1) * C), slice((1 - r) * C, (2 - r) * C)
                                last = V.tensor_tensor(dst[:, :, a], src[:, :, z],
                                                       tab[2 * j + 1][:, w, a].unsqueeze(1).to_broadcast([P, H1, C]), ALU.mult)
                        last.then_inc(sin_done, 1)

                    def turn(w):
                        dve.wait_ge(sin_done, NW * b + w + 1)
                        dve.wait_ge(cos_done, 2 * (NW * b + w + 1))
                        if w >= 2:
                            dve.wait_ge(tk_ps, NW * b + w - 1)
                        V.tensor_tensor(turned[:, w % 2, :], cosp[:, :], sinp[:, :], ALU.add).then_inc(turn_done, 1)
                        dve.wait_ge(turn_done, NW * b + w + 1)

                    def maxima(w):
                        s = w % 2
                        if w >= 2:
                            dve.wait_ge(pt_ps, HP * (NW * b + w - 1))
                        for h in range(H1):
                            if h % 2 == 0:
                                dve.wait_ge(s_ps, H1 * (NW * b + w) + h + 2)
                                dve.sem_inc(passed, 1)
                            c0 = (h % 4) * 2 * WIN
                            V.tensor_tensor_reduce(sm[:, s, h, keys(w)], PB[1 + h // 4][:, c0:c0 + 2 * WIN][:, keys(w)],
                                                   mask[:, keys(w)], 1.0, 0.0, ALU.add, ALU.max,
                                                   st[:, s, 0, h:h + 1]).then_inc(s_masked, 1)
                            if h % 4 == 3:
                                hs = slice(h - 3, h + 1)
                                dve.wait_ge(s_masked, H1 * (NW * b + w) + h + 1)
                                V.tensor_scalar_mul(st[:, s, 1, hs], st[:, s, 0, hs], -QK_SCALE).then_inc(m_done, 1)

                    def inverse_sums(w, j):
                        hs = slice(4 * j, 4 * j + 4)
                        dve.wait_ge(e_done, 2 * (NW * b + w) + j + 1)
                        V.reciprocal(st[:, w % 2, 3, hs], st[:, w % 2, 2, hs]).then_inc(d_done, 1)

                    def prob_rows(w, p):
                        dve.wait_ge(pt_ps, HP * (NW * b + w) + p + 1)
                        if p > 1 or w:
                            dve.wait_ge(pv_ps, HP * (NW * b + w) + p - 1)
                        c0 = slice(0, 4) if w else slice(1, 4, 2)
                        V.tensor_copy(PT[:, 1, c0, :],
                                      PB[3][:, HALF:2 * HALF].rearrange("p (a t) -> p a t", t=P)[:, c0, :]).then_inc(pt_dve, 1)

                    dve.wait_ge(G["ld_tab"], 32)
                    for w in range(NW):
                        dve.wait_ge(sq_done, NW * b + w + 1)
                        V.reduce_sum(ss[:, w, :], sq[:, :].rearrange("p (h d) -> p h d", d=HD1), X).then_inc(ss_done, 1)
                        if w % NN == NN - 1:
                            half, hs = w // NN, slice(w + 1 - NN, w + 1)
                            dve.wait_ge(n_sqrt, 2 * b + half + 1)
                            V.tensor_scalar_max(nrm[:, hs, :], nrm[:, hs, :], 1e-12).then_inc(n_step, 1)
                            dve.wait_ge(n_step, 4 * b + 2 * half + 1)
                            V.reciprocal(rn[:, hs, :], nrm[:, hs, :]).then_inc(n_step, 1)
                            dve.wait_ge(n_step, 4 * b + 2 * half + 2)
                        if w == NN:
                            products(0)
                            turn(0)
                    for i in range(NW + 2):
                        if i >= 2:
                            inverse_sums(i - 2, 1)
                        if 1 <= i <= NW:
                            maxima(i - 1)
                        if i + 1 < NW:
                            products(i + 1)
                        if i >= 2:
                            prob_rows(i - 2, 1)
                        if 1 <= i <= NW:
                            inverse_sums(i - 1, 0)
                        if i >= 2:
                            prob_rows(i - 2, 3)
                        if i + 1 < NW:
                            turn(i + 1)
                        if i in (NW // 2 + 2, NW + 1):
                            hf = 0 if i < NW else 1
                            for m in range(KD):
                                dve.wait_ge(wo_ps, KD * (2 * b + hf) + m + 1)
                                xs = xr[:, m, ds(b - l * B, 1), 1 + hf * HALF:1 + (hf + 1) * HALF].rearrange("p o t -> p (o t)")
                                V.tensor_tensor(xs, PB[1][:, m * HALF:(m + 1) * HALF], xs, ALU.add).then_inc(wo_done, 1)


def stage_ffn1(nc, G, A, l, out):
    with ExitStack() as ctx:
        sb = lambda n, s, dt=F32: ctx.enter_context(nc.sbuf_tensor(f"m{l}_{n}", s, dt))
        sem = lambda n: G["layer_sem"](f"m_{n}")
        PB, xr = G["PB"], G["xr"]
        w1, w2, lg, lb, b1, b2 = (G[n] for n in ("w1", "w2", "lg", "lb", "b1", "b2"))
        w1s = [sb(f"w1_{c}", [P, KD, 2 * HIDP], F32R) for c in range(2)]
        w2s = [sb(f"w2_{c}", [P, FT, D], F32R) for c in range(2)]
        mean = sb("mean", [P, P])
        eps = sb("eps", [P, 1])
        xc = sb("xc", [P, KD, HALF])
        sq = sb("sq", [P, KD, HALF])
        sd = sb("sd", [P, HALF])
        rs = sb("rs", [P, HALF])
        xn = sb("xn", [P, KD, HALF])
        hn = sb("hn", [P, KD, HALF])
        hns = [sb(f"hn_{c}", [P, 2, KD, HALF], F32R) for c in range(2)]
        gl = sb("gl", [P, 2, HALF])
        hid = sb("hid", [P, 2, HALF])
        hids = [sb(f"hid_{c}", [P, FT, HALF], F32R) for c in range(2)]
        consts, mu_ps, xc_done, sq_done, var_ps, sd_done, rs_done, xn_done, hn_done, hn_high, hn_low = (sem(n) for n in (
            "consts", "mu_ps", "xc_done", "sq_done", "var_ps", "sd_done", "rs_done", "xn_done", "hn_done", "hn_high", "hn_low"))
        g_ps, a_ps, gl_done, hid_done, hid_high, hid_low, y_ps, y_done = (sem(n) for n in (
            "g_ps", "a_ps", "gl_done", "hid_done", "hid_high", "hid_low", "y_ps", "y_done"))
        w1_high, w1_low, w2_high, w2_low = (sem(n) for n in ("w1_high", "w1_low", "w2_high", "w2_low"))
        stored, ld_half = sem("stored"), [sem(f"ld_half{hf}") for hf in range(T // HALF)]
        NH = T // HALF
        UNITS = NH * B
        NORMS = UNITS + 1
        BANK_MU, BANK_VAR = PB[1][:, 0:HALF], PB[1][:, HALF:2 * HALF]
        QW = HALF // 2

        def norm_of(b, hf):
            return NH * b + hf + l

        def following(b, hf):
            return (b, hf + 1) if hf + 1 < NH else ((2 * l + 1) * B - 1 - b, 0)

        def tokens(b):
            return ds(b - l * B, 1)

        def shifted(b, k, hf):
            c0 = hf * HALF + (1 if k == 0 else 0)
            return xr[:, k, tokens(b), c0:c0 + HALF].rearrange("p o t -> p (o t)")

        def w1_tile(w, f):
            return w[:, :, :].rearrange("p k (c n) -> p k c n", c=2)[:, :, :, f * P:(f + 1) * P]

        final = l + 1 == LAYERS
        x1T = sb("x1T", [P, KD, NH, HALF]) if final else None

        def half_of(b, hf):
            return ds((b - l * B) * T + hf * HALF, HALF)

        with nc.Block() as block:
            @block.sync
            def _(sp):
                if not final:
                    load_attention1(sp, G, A, l + 1)
                    return
                with sp.Fori(l * B, (l + 1) * B) as b:
                    for hf in range(NH):
                        if hf == 0:
                            sp.wait_ge(stored, 16 * NH * (b - l * B))
                        sp.sem_inc(G["passed"], 1)
                        sp.dma_start(x1T[:, :, hf, :], G["x1"][:, half_of(b, hf)].rearrange("(k p) n -> p k n", p=P)
                                     ).then_inc(ld_half[hf], 16)
                    for hf in range(NH):
                        sp.wait_ge(G["x1_ready"], KD * (NH * (b - l * B) + hf + 1))
                        sp.sem_inc(G["passed"], 1)
                        sp.dma_start(out[:, half_of(b, hf)].rearrange("(k p) n -> p k n", p=P), x1T[:, :, hf, :]
                                     ).then_inc(stored, 16)
                sp.wait_ge(stored, 16 * UNITS)

            @block.gpsimd
            def _(pool):
                V = nc.gpsimd
                V.memset(mean[:, :], 1.0 / D).then_inc(consts, 1)
                V.memset(eps[:, :], LN_EPS).then_inc(consts, 1)
                pool.wait_ge(G["ld_ffn"], LD_FFN * (l + 1))

                def normalise(i, n):
                    pool.wait_ge(rs_done, 2 * (i + 1))
                    for k in range(KD):
                        V.tensor_tensor(xn[:, k, :], xc[:, k, :], rs[:, :], ALU.mult).then_inc(xn_done, 1)
                    for k in range(KD):
                        pool.wait_ge(hn_high, KD * i + k + 1)
                        V.tensor_tensor(hns[1][:, n % 2, k, :], hn[:, k, :], hns[0][:, n % 2, k, :].bitcast(F32),
                                        ALU.subtract).then_inc(hn_low, 1)

                pool.wait_ge(w2_high, l + 1)
                V.tensor_tensor(w2s[1][:, :, :], w2[:, :, :], w2s[0][:, :, :].bitcast(F32), ALU.subtract).then_inc(w2_low, 1)
                normalise(norm_of(l * B, 0), 0)
                with pool.Fori(l * B, (l + 1) * B) as b:
                    for hf in range(NH):
                        normalise(norm_of(b, hf) + 1, hf + 1)
                        if final:
                            pool.wait_ge(ld_half[hf], 16 * (b - l * B + 1))
                            for m in range(KD):
                                pool.wait_ge(y_done, KD * (NH * b + hf) + m + 1)
                                xs = xr[:, m, tokens(b), 1 + hf * HALF:1 + (hf + 1) * HALF].rearrange("p o t -> p (o t)")
                                V.tensor_tensor(x1T[:, m, hf, :], x1T[:, m, hf, :], xs, ALU.add).then_inc(G["x1_ready"], 1)

            @block.tensor
            def _(pe):
                mm = nc.tensor.matmul
                pe.wait_ge(consts, 2 * (l + 1))

                def means(b, hf):
                    for k in range(KD):
                        last = mm(BANK_MU, mean[:, :], shifted(b, k, hf), start=(k == 0), stop=(k == KD - 1))
                    last.then_inc(mu_ps, 1)

                def variances(i):
                    pe.wait_ge(sq_done, KD * (i + 1))
                    for k in range(KD):
                        last = mm(BANK_VAR, mean[:, :], sq[:, k, :], start=(k == 0), stop=(k == KD - 1))
                    last.then_inc(var_ps, 1)

                means(l * B, 0)
                variances(norm_of(l * B, 0))
                pe.wait_ge(w1_low, FT * (l + 1))
                pe.wait_ge(w2_low, l + 1)
                with pe.Fori(l * B, (l + 1) * B) as b:
                    for hf in range(NH):
                        i, u0 = norm_of(b, hf), FT * (NH * b + hf)
                        pe.wait_ge(hn_low, KD * (i + 1))
                        for f in range(FT):
                            if f == 0:
                                pe.wait_ge(xc_done, KD * (i + 1))
                                if hf + 1 == NH:
                                    pe.wait_ge(y_done, KD * (NH * b + 1))
                                    pe.sem_inc(G["passed"], 1)
                                means(*following(b, hf))
                            for part, (col, ready) in enumerate(((HIDP, g_ps), (0, a_ps))):
                                pe.wait_ge(hid_done, u0 + f - 1 if f or hf else u0)
                                for n, (cw, ch) in enumerate(PRODUCTS):
                                    for k in range(KD):
                                        last = mm(PB[2 + f % 2][:, part * HALF:(part + 1) * HALF],
                                                  w1s[cw][:, k, col + f * P:col + (f + 1) * P], hns[ch][:, hf, k, :],
                                                  start=(n == k == 0), stop=(n == len(PRODUCTS) - 1 and k == KD - 1))
                                last.then_inc(ready, 1)
                            if f == 2:
                                pe.wait_ge(sd_done, i + 1)
                                variances(i + 1)
                        pe.wait_ge(y_done, KD * (NH * b + hf))
                        for tiles in (range(FT - 1), range(FT - 1, FT)):
                            pe.wait_ge(hid_low, u0 + tiles[-1] + 1)
                            for m in range(KD):
                                for f in tiles:
                                    for n, (cw, ch) in enumerate(PRODUCTS):
                                        last = mm(PB[0][:, m * HALF:(m + 1) * HALF], w2s[cw][:, f, m * P:(m + 1) * P],
                                                  hids[ch][:, f, :], start=(f == n == 0),
                                                  stop=(f == FT - 1 and n == len(PRODUCTS) - 1))
                                if tiles[-1] == FT - 1:
                                    last.then_inc(y_ps, 1)

            @block.scalar
            def _(act):
                S = nc.scalar.activation
                act.wait_ge(consts, 2 * (l + 1))
                act.wait_ge(G["ld_ffn"], LD_FFN * (l + 1))

                def squares(i):
                    for k in range(KD):
                        act.wait_ge(xc_done, KD * i + k + 1)
                        if i is not first:
                            act.wait_ge(var_ps, i)
                        S(sq[:, k, :], xc[:, k, :], ACT.Square).then_inc(sq_done, 1)

                def deviation(i):
                    act.wait_ge(var_ps, i + 1)
                    act.wait_ge(rs_done, 2 * i)
                    S(sd[:, :], BANK_VAR, ACT.Sqrt, bias=eps[:, 0:1]).then_inc(sd_done, 1)

                def scaled(i):
                    for k in range(KD):
                        act.wait_ge(xn_done, KD * i + k + 1)
                        act.wait_ge(hn_low, KD * i)
                        S(hn[:, k, :], xn[:, k, :], ACT.Identity, bias=lb[:, k:k + 1],
                          scale=lg[:, k:k + 1]).then_inc(hn_done, 1)

                first = norm_of(l * B, 0)
                squares(first)
                deviation(first)
                scaled(first)
                with act.Fori(l * B, (l + 1) * B) as b:
                    for hf in range(NH):
                        i = norm_of(b, hf) + 1
                        squares(i)
                        for f in range(FT):
                            u = FT * (NH * b + hf) + f
                            act.wait_ge(g_ps, u + 1)
                            act.wait_ge(hid_done, u - 1 if f or hf else u)
                            S(gl[:, f % 2, :], PB[2 + f % 2][:, 0:HALF], ACT.Gelu, bias=b1[:, FT + f:FT + f + 1]).then_inc(gl_done, 1)
                            if f == 2:
                                deviation(i)
                        scaled(i)

            @block.vector
            def _(dve):
                V = nc.vector
                dve.wait_ge(G["ld_ffn"], LD_FFN * (l + 1))

                def centred(b, hf, i):
                    dve.wait_ge(mu_ps, i + 1)
                    dve.wait_ge(xn_done, KD * i)
                    dve.wait_ge(sq_done, KD * i)
                    dve.sem_inc(G["passed"], 1)
                    for k in range(KD):
                        V.tensor_tensor(xc[:, k, :], shifted(b, k, hf), BANK_MU, ALU.subtract).then_inc(xc_done, 1)

                def inverse(i, q):
                    dve.wait_ge(sd_done, i + 1)
                    dve.wait_ge(xn_done, KD * i)
                    V.reciprocal(rs[:, q * QW:(q + 1) * QW], sd[:, q * QW:(q + 1) * QW]).then_inc(rs_done, 1)

                def split_w1(f):
                    V.tensor_copy(w1_tile(w1s[0], f), w1_tile(w1, f)).then_inc(w1_high, 1)

                def high(i, n):
                    for k in range(KD):
                        dve.wait_ge(hn_done, KD * i + k + 1)
                        V.tensor_copy(hns[0][:, n % 2, k, :], hn[:, k, :]).then_inc(hn_high, 1)

                first = norm_of(l * B, 0)
                V.tensor_copy(w2s[0][:, :, :], w2[:, :, :]).then_inc(w2_high, 1)
                for f in range(FT):
                    split_w1(f)
                    if f == 1:
                        centred(l * B, 0, first)
                for f in range(FT):
                    dve.wait_ge(w1_high, FT * l + f + 1)
                    V.tensor_tensor(w1_tile(w1s[1], f), w1_tile(w1, f), w1_tile(w1s[0], f).bitcast(F32),
                                    ALU.subtract).then_inc(w1_low, 1)
                    if f == 1:
                        for q in range(2):
                            inverse(first, q)
                high(first, 0)
                if l + 1 < LAYERS:
                    split_wqkv(nc, dve, G, l + 1)
                with dve.Fori(l * B, (l + 1) * B) as b:
                    for hf in range(NH):
                        i = norm_of(b, hf) + 1
                        centred(*following(b, hf), i)
                        for f in range(FT):
                            u, s = FT * (NH * b + hf) + f, f % 2
                            dve.wait_ge(gl_done, u + 1)
                            dve.wait_ge(a_ps, u + 1)
                            V.scalar_tensor_tensor(out=hid[:, s, :], in0=PB[2 + s][:, HALF:2 * HALF], scalar=b1[:, f:f + 1],
                                                   in1=gl[:, s, :], op0=ALU.add, op1=ALU.mult).then_inc(hid_done, 1)
                            dve.wait_ge(hid_done, u + 1)
                            V.tensor_copy(hids[0][:, f, :], hid[:, s, :]).then_inc(hid_high, 1)
                            dve.wait_ge(hid_high, u + 1)
                            V.tensor_tensor(hids[1][:, f, :], hid[:, s, :], hids[0][:, f, :].bitcast(F32),
                                            ALU.subtract).then_inc(hid_low, 1)
                            if f in (3, 4):
                                inverse(i, f - 3)
                        high(i, hf + 1)
                        for m in range(KD):
                            dve.wait_ge(y_ps, KD * (NH * b + hf) + m + 1)
                            xs = xr[:, m, tokens(b), 1 + hf * HALF:1 + (hf + 1) * HALF].rearrange("p o t -> p (o t)")
                            V.scalar_tensor_tensor(out=xs, in0=PB[0][:, m * HALF:(m + 1) * HALF], scalar=b2[:, m:m + 1],
                                                   in1=xs, op0=ALU.add, op1=ALU.add).then_inc(y_done, 1)


def program(nc, A, out):
    with ExitStack() as top:
        def sb(n, s, dt=F32, ctx=top, side="left"):
            return ctx.enter_context(nc.sbuf_tensor(n, s, dt, side=side))

        G = {"PB": [top.enter_context(nc.psum_tensor(f"bank{i}", [P, 2 * HALF], F32)) for i in range(4)],
             "x1": nc.dram_tensor("x1", [D, N], F32, kind="Internal").ap(),
             "scr": nc.dram_tensor("qk_parts", [2, 3, D, N], BF16, kind="Internal").ap()}
        for n in ("ld_x1", "ld_att", "ld_ffn", "ld_tab", "passed", "wqkv_split", "x1_ready", "x1_out"):
            G[n] = top.enter_context(nc.semaphore("g_" + n))
        G["early_sems"] = []

        def early_sem(n):
            G["early_sems"].append(nc.alloc_semaphore(n))
            return G["early_sems"][-1]

        G["early_sem"] = early_sem
        layer_sems = {}

        def layer_sem(n):
            if n not in layer_sems:
                layer_sems[n] = top.enter_context(nc.semaphore(n))
            return layer_sems[n]

        G["layer_sem"] = layer_sem
        G["ident"] = sb("ident", [P, P])
        G["rot"] = sb("rot", [P, KD, D])
        G["csum"] = sb("csum", [P, KD, B])
        heads, values, mixed, moe = ExitStack(), ExitStack(), ExitStack(), ExitStack()
        G["gate"] = sb("gate", [P, B * TT * H0], ctx=heads, side="right")
        G["fa"] = sb("fa", [P, TT, B], ctx=heads, side="right")
        G["vsum"] = sb("vsum", [P, B, D], ctx=heads, side="right")
        G["v"] = sb("v", [P, 2 * B, TT, P], ctx=values)
        stage_project(nc, G, A)
        G["OT"] = sb("OT", [P, 2 * HG, T], ctx=heads, side="right")
        stage_attention0(nc, G, A)
        values.close()
        G["X0T"] = [sb(f"X0T_{c}", [P, KD, N], F32R, ctx=mixed) for c in range(2)]
        G["X0"] = [sb(f"X0_{c}", [P, B * TT, D], F32R, ctx=mixed) for c in range(2)]
        stage_out0(nc, G, A)
        heads.close()
        G["O"] = sb("O", [P, B * TT, D], ctx=moe, side="right")
        G["den"] = sb("den", [P, B * TT], ctx=moe, side="right")
        stage_moe(nc, G, A)
        mixed.close()
        G["xr"] = sb("xr", [P, KD, B, 1 + T])
        with ExitStack() as place:
            G["wqkv1_raw"] = sb("wqkv1_raw", [P, KD, 3 * INNER], ctx=place)
        G["wqkv1"] = [sb(f"wqkv1_{c}", [P, KD, 3 * INNER], F32R) for c in range(2)]
        G["wo"] = sb("wo", [P, HP, D])
        G["mask"] = sb("mask", [P, 2 * WIN])
        G["qks"] = sb("qks", [P, LAYERS, 4, HD1])
        G["w1"] = sb("w1", [P, KD, 2 * HIDP])
        G["w2"] = sb("w2", [P, FT, D])
        G["lg"], G["lb"], G["b2"] = (sb(n, [P, KD]) for n in ("lg", "lb", "b2"))
        G["b1"] = sb("b1", [P, 2 * FT])
        stage_rotate(nc, G, A)
        moe.close()
        for l in range(LAYERS):
            stage_attention1(nc, G, A, l)
            stage_ffn1(nc, G, A, l, out)


def constants():
    f = np.float32
    c = {}
    inv = f(10000.0) ** np.repeat(np.arange(0, D, 2, dtype=f) / f(D), 2)
    c["peT"] = np.sin(np.arange(T, dtype=f)[:, None] / inv[None, :]).astype(f).T
    half = np.arange(0, HD1, 2, dtype=f)
    t = np.arange(T, dtype=f)
    freqs = t[:, None] * (f(1.0) / f(10000.0) ** (half / f(HD1)))[None, :]
    freqs = np.concatenate([freqs, freqs], -1)
    scale = ((half + f(0.4 * HD1)) / f(1.4 * HD1))[None, :] ** ((t - T // 2) / f(WIN // 2))[:, None]
    scale = np.concatenate([scale, scale], -1)
    cos, sin = np.cos(freqs), np.sin(freqs)
    sin = np.concatenate([-sin[:, :HD1 // 2], sin[:, HD1 // 2:]], -1)
    c["tables"] = np.stack([cos * scale, sin * scale, cos / scale, sin / scale]).astype(f)
    i, j = np.arange(WIN)[:, None], np.arange(WIN)[None, :]
    c["mask"] = np.concatenate([np.where(j >= i, 0.0, MASKED), np.where(j <= i, 0.0, MASKED)], 1).astype(f)
    c["ident"] = np.eye(P, dtype=f)
    ham = np.zeros((4, 4, 4))
    for k, terms in enumerate((((0, 0, 1), (1, 1, -1), (2, 2, -1), (3, 3, -1)), ((0, 1, 1), (1, 0, 1), (2, 3, 1), (3, 2, -1)),
                               ((0, 2, 1), (1, 3, -1), (2, 0, 1), (3, 1, 1)), ((0, 3, 1), (1, 2, 1), (2, 1, -1), (3, 0, 1)))):
        for a, b, s in terms:
            ham[k, a, b] = s
    conj = np.array([1.0, -1.0, -1.0, -1.0])
    c["sgn"] = np.einsum("iak,kjb,b->abij", ham, ham, conj).reshape(16, 16).astype(f)
    return c


def kernel(**inputs):
    import concourse.bacc as _bacc
    from concourse.bass_utils import run_bass_kernel_spmd as _run

    I = {n: np.asarray(v) for n, v in inputs.items()}
    c0, f1 = "L0_cond_", "L1_ffn_"
    col = lambda v: v.reshape(-1, P).T
    rep = lambda v, n: np.broadcast_to(v, (n,) + v.shape)
    pad = lambda a, n: np.pad(a, [(0, 0)] * (a.ndim - 1) + [(0, n - a.shape[-1])])
    cond, qr = I["cond_256"], I["L1_cond_q_right"]
    w1, b1 = I[f1 + "w1"], I[f1 + "b1"]
    phi = I["L0_ffn_phi"].reshape(D, SLOTS)
    w1 = np.concatenate([pad(w1[..., :HID], HIDP), pad(w1[..., HID:], HIDP)], -1)
    b1 = np.concatenate([pad(b1[..., :HID], HIDP), pad(b1[..., HID:], HIDP)], -1)
    qs, ks = I[f1 + "q_scale"], I[f1 + "k_scale"]
    swap = lambda v: np.concatenate([v[:, HD1 // 2:], v[:, :HD1 // 2]], -1)
    rows = [0] * 4 + [1] * 12
    arrays = {
        **constants(),
        "xT": I["x"].reshape(N, D).T,
        "wqkv0T": I[c0 + "Wqkv"].T, "bqk": col(I[c0 + "bqkv"][:2 * D]), "bvB": rep(I[c0 + "bqkv"][2 * D:], P),
        "wc1xT": I[c0 + "Wc1"][:, :D].T, "wc1cT": I[c0 + "Wc1"][:, D:].T, "bc1": col(I[c0 + "bc1"]),
        "wc2T": I[c0 + "Wc2"].T, "bc2B": rep(I[c0 + "bc2"], P),
        "csT": cond.T, "we1T": I[c0 + "We1"].T, "be1": col(I[c0 + "be1"]), "we2T": I[c0 + "We2"].T,
        "rows2": rep(np.stack([I[c0 + "be2"], I[c0 + "ln_g"], I[c0 + "ln_b"]]), B),
        "woutT": I[c0 + "Wout"].T, "bout": col(I[c0 + "bout"]), "boutB": rep(I[c0 + "bout"], P),
        "phi": np.concatenate([phi, phi[:, :CS]], 1), "W": I["L0_ffn_W"], "bexp": np.repeat(I["L0_ffn_b"], NP_, 0),
        "ql": cond[rows], "qr": np.tile(qr, (4, 1)), "gate": rep(I["L1_cond_spectral_gate"].reshape(64), 16),
        "qall": rep(np.concatenate([cond, qr], 0), 16),
        "wqkv1": I[f1 + "wqkv"], "wo": I[f1 + "wo"], "w1": w1,
        "w2": np.pad(I[f1 + "w2"], [(0, 0), (0, HIDP - HID), (0, 0)]),
        "lg": np.stack([col(v) for v in I[f1 + "ln_g"]]), "lb": np.stack([col(v) for v in I[f1 + "ln_b"]]),
        "b1": np.stack([col(v) for v in b1]), "b2": np.stack([col(v) for v in I[f1 + "b2"]]),
        "qks": rep(np.stack([qs, swap(qs), ks, swap(ks)], 1), P),
    }
    arrays = {f"in_{n}": np.ascontiguousarray(a) for n, a in arrays.items()}
    nc = _bacc.Bacc("TRN2", target_bir_lowering=False, num_devices=1)
    A = {n[3:]: nc.dram_tensor(n, a.shape, mybir.dt.from_np(a.dtype), kind="ExternalInput").ap() for n, a in arrays.items()}
    out = nc.dram_tensor("out_T", (D, N), F32, kind="ExternalOutput").ap()
    program(nc, A, out)
    r = _run(nc, [arrays], core_ids=[0])
    return np.ascontiguousarray(r.results[0]["out_T"].T).reshape(B, T, D)
```

```python
import itertools
from contextlib import ExitStack

import numpy as np

import concourse.bass as bass
from concourse import mybir

F32 = mybir.dt.float32
F32R = mybir.dt.float32r
BF16 = mybir.dt.bfloat16
ACT = mybir.ActivationFunctionType
ALU = mybir.AluOpType
X = mybir.AxisListType.X
ds = bass.ds

P = 128
B, T, D = 2, 1024, 256
N = B * T
KD = D // P
TT = T // P
HALF = 512
H0, HD0 = 16, 16
HG = 4
GB = H0 // HG
KS = 6 * HD0
KA = KS + 3
Q_PART = (0, 0, 1, 1, 0, 2)
K_PART = (0, 1, 0, 1, 2, 0)
COUPLING = 0.3 * 0.7
COH_EPS = 1e-8
CD = 64
NE, NP_ = 64, 32
SLOTS = NE * NP_
CH = 4
CS = SLOTS // CH
CE = NE // CH
LAYERS = 2
H1, HD1 = 8, 64
INNER = H1 * HD1
HP = H1 // 2
WIN = 128
NW = T // WIN
HID = 682
FT = -(-HID // P)
HIDP = FT * P
QK_SCALE = 8.0
LN_EPS = 1e-5
PRODUCTS = ((0, 0), (0, 1), (1, 0))
MASKED = -1e30
LOWEST = -3e38


def chain(eng, sem, start=0):
    n = [0]

    def link(ins):
        n[0] += 1
        ins.then_inc(sem, 1)
        eng.wait_ge(sem, start + n[0])

    link.count = n
    return link


def stage_project(nc, G, A):
    with ExitStack() as ctx:
        sb = lambda n, s, dt=F32: ctx.enter_context(nc.sbuf_tensor(n, s, dt))
        sem = G["early_sem"]
        PB = G["PB"]
        xT = sb("p_xT", [P, KD, N])
        wqkv = sb("p_wqkv", [P, KD, 3 * D])
        wc1x = sb("p_wc1x", [P, KD, D])
        wc2 = sb("p_wc2", [P, KD, 32])
        zT = sb("p_zT", [P, HALF])
        we2 = sb("p_we2", [P, KD, D])
        peT = sb("p_peT", [P, KD, T])
        wc1c = sb("p_wc1c", [CD, D])
        we1 = sb("p_we1", [CD, D])
        csT = sb("p_csT", [CD, B])
        bqk = sb("p_bqk", [P, 4])
        bvB = sb("p_bvB", [P, D])
        bc1 = sb("p_bc1", [P, KD])
        be1 = sb("p_be1", [P, KD])
        bc2B = sb("p_bc2B", [P, H0])
        rows2 = sb("p_rows2", [B, 3, D])
        ql = sb("p_ql", [16, 64])
        qr = sb("p_qr", [16, 64])
        gate = sb("p_gate", [16, 64])
        qall = sb("p_qall", [16, 6, 64])
        sgn = sb("p_sgn", [16, 16])
        parts = sb("p_parts", [P, 4, 3, HALF], BF16)
        rest = sb("p_rest", [P, 4, HALF])
        c1T = sb("p_c1T", [P, KD, N])
        cbias = sb("p_cbias", [P, KD, B])
        h1T = sb("p_h1T", [P, KD, B])
        fpw = sb("p_fpw", [B, 4, D])
        fst = sb("p_fst", [B, 8])
        fpT = sb("p_fpT", [P, KD, B])
        faw = sb("p_faw", [B, 3, T])
        zt = sb("p_zt", [P, 3, B * TT * H0])
        xsum = sb("p_xsum", [P, KD, B])
        xsB = sb("p_xsB", [P, KD, B, P])
        qsq = sb("p_qsq", [16, 6, 64])
        qn = sb("p_qn", [16, 2, 64])
        qsd = sb("p_qsd", [16, 2, 64])
        qpr = sb("p_qpr", [16, 4, 64])
        pp2 = sb("p_pp2", [16, 2, 64])
        mco = sb("p_mco", [P, 16])
        ones = sb("p_ones", [P, P])
        eps5 = sb("p_eps5", [B, 1])

        ld_small, ld_w, ld_c1, ld_pe = sem("ld_small"), sem("ld_w"), sem("ld_c1"), sem("ld_pe")
        ld_x = [sem(f"ld_x{b}") for b in range(B)]
        consts = sem("consts")
        dve_step, act_step = sem("dve_step"), sem("act_step")
        cond_ps, h1_ready, fp_ps, ln_var, ln_sd, fp_ready = (sem(n) for n in (
            "cond_ps", "h1_ready", "fp_ps", "ln_var", "ln_sd", "fp_ready"))
        fpT_ps, fpT_ready, fa_ps, fa_max, fa_exp, fa_ready, faT_ps = (sem(n) for n in (
            "fpT_ps", "fpT_ready", "fa_ps", "fa_max", "fa_exp", "fa_ready", "faT_ps"))
        q_norm, q_sd, pp_ready, mco_ps = sem("q_norm"), sem("q_sd"), sem("pp_ready"), sem("mco_ps")
        cb_ready = sem("cb_ready")
        qk_ps, qk_p1, qk_rest, qk_p2, qk_p3 = (sem(n) for n in ("qk_ps", "qk_p1", "qk_rest", "qk_p2", "qk_p3"))
        qk_stored = [sem(f"qk_stored{i}") for i in range(4)]
        v_ps, v_done, c1_ps, c1_done, z_ps, z_clip, z_exp = (sem(n) for n in (
            "v_ps", "v_done", "c1_ps", "c1_done", "z_ps", "z_clip", "z_exp"))
        xs_ready, vs_ps, zT_ps, zT_out = sem("xs_ready"), sem("vs_ps"), sem("zT_ps"), sem("zT_out")
        AT_HIDDEN, AT_FIELD, AT_NORM = 4, 8, 11
        UNITS = [(b, hf, m) for b in range(B) for hf in range(T // HALF) for m in range(4)]
        small = [(wc1c, A["wc1cT"]), (we1, A["we1T"]), (csT, A["csT"]), (be1, A["be1"]), (bc1, A["bc1"]),
                 (rows2, A["rows2"]), (ql, A["ql"]), (qr, A["qr"]), (gate, A["gate"]), (qall, A["qall"]),
                 (sgn, A["sgn"]), (G["ident"], A["ident"]), (bqk, A["bqk"]), (bvB, A["bvB"]), (bc2B, A["bc2B"])]
        NSMALL = 16 * (len(small) + 2)
        kp = lambda a: a.rearrange("(k p) n -> p k n", p=P)
        scr = G["scr"]
        ring = lambda u: PB[(u % 4) // 2][:, HALF * (u % 2):HALF * (u % 2) + HALF]
        misc = lambda r, a, b: PB[3][0:r, HALF + a:HALF + b]

        with nc.Block() as block:
            @block.sync
            def _(sp):
                sp.dma_start(wqkv[:, :, :], kp(A["wqkv0T"])).then_inc(ld_w, 16)
                for dst, src in small:
                    sp.dma_start(dst[:], src).then_inc(ld_small, 16)
                sp.dma_start(we2[:, :, :], kp(A["we2T"])).then_inc(ld_small, 16)
                sp.dma_start(wc2[:, :, 0:H0], kp(A["wc2T"])).then_inc(ld_small, 16)
                for u, (b, hf, m) in enumerate(UNITS):
                    sp.wait_ge(qk_p3, u + 1)
                    t0 = b * T + hf * HALF
                    dst = scr[m // 2, :, (m % 2) * P:(m % 2) * P + P, t0:t0 + HALF].rearrange("c p t -> p c t")
                    sp.dma_start(dst, parts[:, u % 4, :, :]).then_inc(qk_stored[u % 4], 16)
                for s in qk_stored:
                    sp.wait_ge(s, 16 * len(UNITS) // 4)
                for k in range(GB - 1):
                    load_heads(sp, G, k, 0, k)

            @block.gpsimd
            def _(pool):
                nc.gpsimd.memset(ones[:, :], 1.0).then_inc(consts, 1)
                nc.gpsimd.memset(eps5[:, :], LN_EPS).then_inc(consts, 1)
                nc.gpsimd.memset(wc2[:, :, H0:32], 0.0).then_inc(consts, 1)
                for u in range(len(UNITS)):
                    pool.wait_ge(qk_p2, u + 1)
                    nc.gpsimd.tensor_tensor(parts[:, u % 4, 2, :], rest[:, u % 4, :], parts[:, u % 4, 1, :],
                                            ALU.subtract).then_inc(qk_p3, 1)

            @block.scalar
            def _(act):
                for b in range(B):
                    act.dma_start(xT[:, :, b * T:(b + 1) * T], kp(A["xT"])[:, :, b * T:(b + 1) * T]).then_inc(ld_x[b], 16)
                act.dma_start(wc1x[:, :, :], kp(A["wc1xT"])).then_inc(ld_c1, 16)
                act.dma_start(peT[:, :, :], kp(A["peT"])).then_inc(ld_pe, 16)
                act.wait_ge(ld_small, NSMALL)
                act.wait_ge(consts, 3)

                def second(u):
                    act.wait_ge(qk_rest, u + 1)
                    nc.scalar.activation(parts[:, u % 4, 1, :], rest[:, u % 4, :], ACT.Copy).then_inc(qk_p2, 1)

                for u, (b, hf, m) in enumerate(UNITS):
                    s = u % 4
                    act.wait_ge(qk_ps, u + 1)
                    if u >= 4:
                        act.wait_ge(qk_stored[s], 16 * (u // 4))
                    nc.scalar.activation(parts[:, s, 0, :], ring(u), ACT.Identity,
                                         bias=bqk[:, m:m + 1]).then_inc(qk_p1, 1)
                    if u >= 1:
                        second(u - 1)
                    if u == AT_HIDDEN + 1:
                        act.wait_ge(cb_ready, KD)
                        for k in range(KD):
                            nc.scalar.activation(h1T[:, k, :], misc(P, 4 + 2 * k, 6 + 2 * k), ACT.Relu,
                                                 bias=be1[:, k:k + 1]).then_inc(h1_ready, 1)
                        act.wait_ge(q_norm, 1)
                        nc.scalar.activation(qsd[:, :, :], qn[:, :, :], ACT.Sqrt).then_inc(q_sd, 1)
                    if u == AT_NORM:
                        act.wait_ge(ln_var, 1)
                        nc.scalar.activation(fst[:, 4:5], fst[:, 3:4], ACT.Sqrt, bias=eps5[:, 0:1]).then_inc(ln_sd, 1)
                second(len(UNITS) - 1)
                for v in range(KD * N // HALF):
                    e, n = v % KD, v // KD
                    act.wait_ge(c1_ps, v + 1)
                    nc.scalar.activation(c1T[:, e, n * HALF:(n + 1) * HALF], ring(v), ACT.Tanh,
                                         bias=cbias[:, e, n // 2:n // 2 + 1]).then_inc(c1_done, 1)
                    if v == 3:
                        act.wait_ge(fa_max, 1)
                        nc.scalar.activation(faw[:, 1, :], faw[:, 0, :], ACT.Exp, bias=fst[:, 6:7],
                                             accum_out=fst[:, 7:8]).then_inc(fa_exp, 1)
                act.wait_ge(z_clip, 1)
                nc.scalar.activation(zt[:, 2, :], zt[:, 1, :], ACT.Exp).then_inc(z_exp, 1)

            @block.vector
            def _(dve):
                link = chain(dve, dve_step)
                V = nc.vector

                def quaternion_norms():
                    dve.wait_ge(ld_small, NSMALL)
                    dve.wait_ge(consts, 3)
                    link(V.tensor_tensor(qsq[:, :, :], qall[:, :, :], qall[:, :, :], ALU.mult))
                    link(V.tensor_reduce(qn[:, 0, :], qsq[:, 0:2, :].rearrange("p r d -> p d r"), X, ALU.add))
                    link(V.tensor_reduce(qn[:, 1, :], qsq[:, 2:6, :].rearrange("p r d -> p d r"), X, ALU.add))
                    V.tensor_scalar_add(qn[:, :, :], qn[:, :, :], 1e-8).then_inc(q_norm, 1)

                def condition_bias():
                    dve.wait_ge(cond_ps, 1)
                    for k in range(KD):
                        V.tensor_scalar_add(cbias[:, k, :], misc(P, 2 * k, 2 * k + 2), bc1[:, k:k + 1]).then_inc(cb_ready, 1)

                def quaternion_products():
                    dve.wait_ge(q_sd, 1)
                    link(V.tensor_tensor(qpr[:, 0, :], qsd[:, 0, :], qsd[:, 1, :], ALU.mult))
                    link(V.reciprocal(qpr[:, 1, :], qpr[:, 0, :]))
                    link(V.tensor_tensor(qpr[:, 2, :], ql[:, :], qr[:, :], ALU.mult))
                    link(V.tensor_tensor(qpr[:, 3, :], qpr[:, 2, :], gate[:, :], ALU.mult))
                    for r in range(2):
                        V.tensor_tensor(pp2[:, r, :], qpr[:, 3, :], qpr[:, 1, :], ALU.mult).then_inc(pp_ready, 1)

                def field_norm():
                    dve.wait_ge(fp_ps, 1)
                    link(V.tensor_tensor(fpw[:, 0, :], misc(B, 16, 16 + D), rows2[:, 0, :], ALU.add))
                    link(V.reduce_sum(fst[:, 0:1], fpw[:, 0, :], X))
                    link(V.tensor_scalar_mul(fst[:, 1:2], fst[:, 0:1], 1.0 / D))
                    link(V.tensor_scalar(fpw[:, 1, :], fpw[:, 0, :], fst[:, 1:2], None, ALU.subtract))
                    link(V.tensor_tensor(fpw[:, 2, :], fpw[:, 1, :], fpw[:, 1, :], ALU.mult))
                    link(V.reduce_sum(fst[:, 2:3], fpw[:, 2, :], X))
                    V.tensor_scalar_mul(fst[:, 3:4], fst[:, 2:3], 1.0 / D).then_inc(ln_var, 1)

                def field_scaled():
                    dve.wait_ge(ln_sd, 1)
                    link(V.reciprocal(fst[:, 5:6], fst[:, 4:5]))
                    link(V.scalar_tensor_tensor(out=fpw[:, 3, :], in0=fpw[:, 1, :], scalar=fst[:, 5:6],
                                                in1=rows2[:, 1, :], op0=ALU.mult, op1=ALU.mult))
                    V.tensor_tensor(fpw[:, 0, :], fpw[:, 3, :], rows2[:, 2, :], ALU.add).then_inc(fp_ready, 1)

                def rotation():
                    dve.wait_ge(mco_ps, 1)
                    link(V.tensor_copy(mco[:, :], misc(P, 304, 320)))
                    for i in range(4):
                        for j in range(4):
                            r = slice(64 * (j % 2), 64 * (j % 2) + 64)
                            V.tensor_scalar_mul(G["rot"][r, j // 2, 64 * i:64 * i + 64], G["ident"][r, r],
                                                mco[r, 4 * i + j:4 * i + j + 1])

                beside = {AT_HIDDEN: (quaternion_norms, condition_bias), AT_FIELD - 1: (quaternion_products,),
                          AT_FIELD + 1: (field_norm,), AT_NORM + 1: (rotation, field_scaled)}
                dve.wait_ge(ld_small, NSMALL)
                for u, (b, hf, m) in enumerate(UNITS):
                    dve.wait_ge(qk_p1, u + 1)
                    if u >= 4:
                        dve.wait_ge(qk_p3, u - 3)
                    V.scalar_tensor_tensor(out=rest[:, u % 4, :], in0=ring(u), scalar=bqk[:, m:m + 1],
                                           in1=parts[:, u % 4, 0, :], op0=ALU.add,
                                           op1=ALU.subtract).then_inc(qk_rest, 1)
                    for work in beside.get(u, ()):
                        work()
                dve.wait_ge(fpT_ps, 1)
                V.tensor_copy(fpT[:, :, :], misc(P, 288, 292).rearrange("p (k b) -> p k b", b=B)).then_inc(fpT_ready, 1)
                for tt in range(B * TT):
                    b, jt = tt // TT, tt % TT
                    dve.wait_ge(v_ps, tt + 1)
                    V.tensor_tensor(G["v"][:, 2 * b:2 * b + 2, jt, :],
                                    PB[2][:, HALF * (tt % 2):HALF * (tt % 2) + D].rearrange("p (m d) -> p m d", m=2),
                                    bvB[:, :].rearrange("p (m d) -> p m d", m=2), ALU.add).then_inc(v_done, 1)
                dve.wait_ge(fa_ps, 1)
                link2 = chain(dve, act_step)
                link2(V.tensor_copy(faw[:, 0, :], PB[2][0:B, 0:T]))
                link2(V.reduce_max(fst[:, 0:1], faw[:, 0, :], X))
                V.tensor_scalar_mul(fst[:, 6:7], fst[:, 0:1], -1.0).then_inc(fa_max, 1)
                for k in range(KD):
                    link(V.reduce_sum(xsum[:, k, :], xT[:, k, :].rearrange("p (b t) -> p b t", b=B), X))
                for k in range(KD):
                    for b in range(B):
                        V.tensor_scalar_mul(xsB[:, k, b, :], ones[:, :], xsum[:, k, b:b + 1]).then_inc(xs_ready, 1)
                dve.wait_ge(fa_exp, 1)
                link2(V.reciprocal(fst[:, 1:2], fst[:, 7:8]))
                V.tensor_scalar(faw[:, 2, :], faw[:, 1, :], fst[:, 1:2], COUPLING, ALU.mult, ALU.mult).then_inc(fa_ready, 1)
                dve.wait_ge(vs_ps, 1)
                for b in range(B):
                    V.scalar_tensor_tensor(out=G["vsum"][:, b, :], in0=bvB[:, :], scalar=float(T),
                                           in1=PB[2][:, b * D:(b + 1) * D], op0=ALU.mult, op1=ALU.add)
                dve.wait_ge(zT_ps, 1)
                V.tensor_copy(zT[:, :], PB[3][:, 0:HALF]).then_inc(zT_out, 1)
                dve.wait_ge(faT_ps, 1)
                V.tensor_copy(G["fa"][:, :, :], misc(P, 320, 320 + B * TT).rearrange("p (t b) -> p t b", b=B))
                dve.wait_ge(z_ps, 1)
                link2(V.tensor_tensor(zt[:, 0, :].rearrange("p (n j h) -> p n j h", j=HALF // P, h=H0),
                                      PB[2][:, HALF:2 * HALF].rearrange("p (j n h) -> p n j h", n=N // HALF, h=32)[:, :, :, 0:H0],
                                      bc2B[:, :].unsqueeze(1).unsqueeze(1).to_broadcast([P, N // HALF, HALF // P, H0]), ALU.add))
                V.tensor_scalar(zt[:, 1, :], zt[:, 0, :], -87.0, -1.0, ALU.max, ALU.mult).then_inc(z_clip, 1)
                dve.wait_ge(z_exp, 1)
                c = 1.0 / (1.0 - COUPLING)
                link2(V.tensor_scalar(G["gate"][:, :], zt[:, 2, :], COH_EPS * c, (1.0 + COH_EPS) * c, ALU.mult, ALU.add))

            @block.tensor
            def _(pe):
                mm, tr, ident = nc.tensor.matmul, nc.tensor.transpose, G["ident"]

                def condition():
                    pe.wait_ge(ld_small, NSMALL)
                    for k in range(KD):
                        mm(misc(P, 2 * k, 2 * k + 2), wc1c[:, k * P:(k + 1) * P], csT[:, :], start=True, stop=True)
                        last = mm(misc(P, 4 + 2 * k, 6 + 2 * k), we1[:, k * P:(k + 1) * P], csT[:, :], start=True, stop=True)
                    last.then_inc(cond_ps, 1)

                def field():
                    pe.wait_ge(h1_ready, KD)
                    pe.wait_ge(pp_ready, 2)
                    mm(misc(P, 304, 320), pp2[:, :, :].rearrange("p r d -> p (r d)"), sgn[:, :], start=True,
                       stop=True).then_inc(mco_ps, 1)
                    for k in range(KD):
                        last = mm(misc(B, 16, 16 + D), h1T[:, k, :], we2[:, k, :], start=(k == 0), stop=(k == KD - 1))
                    last.then_inc(fp_ps, 1)

                beside = {AT_HIDDEN - 1: condition, AT_FIELD: field}
                pe.wait_ge(ld_w, 16)
                for u, (b, hf, m) in enumerate(UNITS):
                    if hf == m == 0:
                        pe.wait_ge(ld_x[b], 16)
                    if u >= 4:
                        pe.wait_ge(qk_rest, u - 3)
                    t0 = b * T + hf * HALF
                    for k in range(KD):
                        last = mm(ring(u), wqkv[:, k, m * P:(m + 1) * P], xT[:, k, t0:t0 + HALF],
                                  start=(k == 0), stop=(k == KD - 1))
                    last.then_inc(qk_ps, 1)
                    if u in beside:
                        beside[u]()
                for tt in range(B * TT):
                    if tt >= 2:
                        pe.wait_ge(v_done, tt - 1)
                    for k in range(KD):
                        last = mm(PB[2][:, HALF * (tt % 2):HALF * (tt % 2) + D], xT[:, k, tt * P:(tt + 1) * P],
                                  wqkv[:, k, 2 * D:3 * D], start=(k == 0), stop=(k == KD - 1))
                    last.then_inc(v_ps, 1)
                    if tt == 1:
                        pe.wait_ge(fp_ready, 1)
                        pe.wait_ge(mco_ps, 1)
                        for k in range(KD):
                            last = tr(misc(P, 288 + 2 * k, 290 + 2 * k), fpw[:, 0, k * P:(k + 1) * P], ident[0:B, 0:B])
                        last.then_inc(fpT_ps, 1)
                pe.wait_ge(fpT_ready, 1)
                pe.wait_ge(ld_pe, 16)
                pe.wait_ge(v_done, B * TT)
                for n in range(T // HALF):
                    for k in range(KD):
                        last = mm(PB[2][0:B, n * HALF:(n + 1) * HALF], fpT[:, k, :], peT[:, k, n * HALF:(n + 1) * HALF],
                                  start=(k == 0), stop=(k == KD - 1))
                last.then_inc(fa_ps, 1)
                pe.wait_ge(qk_rest, len(UNITS))
                pe.wait_ge(ld_c1, 16)
                for v in range(KD * N // HALF):
                    e, n = v % KD, v // KD
                    if v >= 4:
                        pe.wait_ge(c1_done, v - 3)
                    for k in range(KD):
                        last = mm(ring(v), wc1x[:, k, e * P:(e + 1) * P], xT[:, k, n * HALF:(n + 1) * HALF],
                                  start=(k == 0), stop=(k == KD - 1))
                    last.then_inc(c1_ps, 1)
                pe.wait_ge(xs_ready, KD * B)
                for b in range(B):
                    for k in range(KD):
                        last = mm(PB[2][:, b * D:(b + 1) * D], xsB[:, k, b, :], wqkv[:, k, 2 * D:3 * D],
                                  start=(k == 0), stop=(k == KD - 1))
                last.then_inc(vs_ps, 1)
                pe.wait_ge(fa_ready, 1)
                for it in range(TT):
                    last = tr(misc(P, 320 + 2 * it, 322 + 2 * it), faw[:, 2, it * P:(it + 1) * P], ident[0:B, 0:B])
                last.then_inc(faT_ps, 1)
                pe.wait_ge(c1_done, KD * N // HALF)
                pe.wait_ge(consts, 3)
                for k in range(KD):
                    for n in range(N // HALF):
                        last = mm(PB[3][32 * n:32 * n + 32, 0:HALF], wc2[:, k, :], c1T[:, k, n * HALF:(n + 1) * HALF],
                                  start=(k == 0), stop=(k == KD - 1))
                last.then_inc(zT_ps, 1)
                pe.wait_ge(zT_out, 1)
                for j in range(HALF // P):
                    last = tr(PB[2][:, HALF + j * P:HALF + (j + 1) * P], zT[:, j * P:(j + 1) * P], ident[:, :])
                last.then_inc(z_ps, 1)


def load_heads(sp, G, slot, b, k):
    r0 = k * HG * HD0
    for s, (dst, which) in enumerate(((G["qa"], Q_PART), (G["ka"], K_PART))):
        for c, part in enumerate(which):
            src = G["scr"][s, part, r0:r0 + HG * HD0, ds(b * T, T)].rearrange("(h p) t -> p h t", p=HD0)
            sp.dma_start(dst[slot][c * HD0:(c + 1) * HD0, :, :], src).then_inc(G["staged"][slot], 16)


def stage_attention0(nc, G, A):
    with ExitStack() as ctx:
        sb = lambda n, s, dt=F32: ctx.enter_context(nc.sbuf_tensor(n, s, dt))
        sem = lambda n: ctx.enter_context(nc.semaphore(n))
        PB, scr, ident = G["PB"], G["scr"], G["ident"]
        qa, ka, staged = G["qa"], G["ka"], G["staged"]
        vst = [sb(f"a_vst{s}", [P, TT, HG, 32]) for s in range(2)]
        pt = [sb(f"a_pt{s}", [P, HG, HALF]) for s in range(2)]
        mx = [sb(f"a_mx{s}", [P, HG * TT, 2]) for s in range(2)]
        mcol = [sb(f"a_mcol{s}", [P, HG * TT]) for s in range(2)]
        mrow = [sb(f"a_mrow{s}", [HG * TT, 3, P], BF16) for s in range(2)]
        mrest = [sb(f"a_mrest{s}", [HG * TT, P]) for s in range(2)]
        passed = G["passed"]
        consts = sem("a_consts")
        FIRST = 0
        shifted = [sem(f"a_shifted{s}") for s in range(GB)]
        v_in, st_ps, p_ready, pv_done = sem("a_v_in"), sem("a_st_ps"), sem("a_p_ready"), sem("a_pv_done")
        o_out = [sem("a_o_out0"), sem("a_o_out1")]
        max_ps, max_done, m_ready, m_rows, row_step, row_ready = (sem(n) for n in (
            "a_max_ps", "a_max_done", "a_m_ready", "a_m_rows", "a_row_step", "a_row_ready"))
        STEPS = 2 * TT
        MU = HG * TT * 2
        EARLY = TT * HG // 2
        PLAN = [4] * 12 + [2, 5, 5, 4]
        ROWS_AT = 12
        assert sum(PLAN) == MU and sum(PLAN[ROWS_AT:]) == EARLY
        DMAS = 16 * len(Q_PART) * 2
        OT = G["OT"]

        mbanks = (PB[3][:, 0:HALF], PB[3][:, HALF:T], PB[2][:, HALF:T])
        MB = len(mbanks)
        mbank = lambda u: mbanks[(u + 1) % MB if u >= 2 else 2 - u]

        def following(b, k):
            return (b, k + 1) if k + 1 < GB else (1 - b, 0)

        with nc.Block() as block:
            @block.sync
            def _(sp):
                def shift_rows(slot, par, count):
                    sp.wait_ge(row_ready, count)
                    for c in range(3):
                        sp.dma_start(qa[slot][KS + c:KS + c + 1, :, :], mrow[par][:, c, :]).then_inc(shifted[slot], 16)

                shift_rows(0, 0, 1)
                with sp.Fori(0, B) as b:
                    for k in range(GB):
                        sp.wait_ge(pv_done, STEPS * (b * GB + k))
                        sp.sem_inc(passed, 1)
                        b3, k3 = (b, GB - 1) if k == 0 else (1 - b, k - 1)
                        load_heads(sp, G, k3, b3, k3)
                        shift_rows((k + 1) % GB, (k + 1) % 2, b * GB + k + 2)
                for s in range(GB):
                    sp.wait_ge(staged[s], DMAS * (B + (s < GB - 1)))
                    sp.wait_ge(shifted[s], 48 * (B + (s == 0)))

            @block.gpsimd
            def _(pool):
                nc.clear_and_free_semaphores(G["early_sems"])
                for s in range(GB):
                    nc.gpsimd.memset(ka[s][KS:KA, :, :], 1.0).then_inc(consts, 1)
                pool.wait_ge(consts, GB)
                for s in range(2):
                    nc.gpsimd.memset(vst[s][:, :, :, HD0:HD0 + 1], 1.0).then_inc(consts, 1)
                    nc.gpsimd.memset(vst[s][:, :, :, HD0 + 1:32], 0.0).then_inc(consts, 1)

                def stage_v(par, b, k):
                    w = HG * HD0
                    src = G["v"][:, ds(2 * b + k // 2, 1), :, (k % 2) * w:(k % 2 + 1) * w]
                    nc.gpsimd.tensor_copy(vst[par][:, :, :, 0:HD0],
                                          src.rearrange("p o j (h d) -> p (o j) h d", h=HG)).then_inc(v_in, 1)

                stage_v(0, 0, 0)
                with pool.Fori(0, B) as b:
                    for k in range(GB):
                        pool.wait_ge(pv_done, STEPS * (b * GB + k))
                        pool.sem_inc(passed, 1)
                        stage_v((k + 1) % 2, *following(b, k))

            @block.scalar
            def _(act):
                with act.Fori(0, B) as b:
                    for k in range(GB):
                        g = b * GB + k
                        for n in range(STEPS):
                            act.wait_ge(pv_done, STEPS * g + max(n - 1, 0))
                            for ab in range(2):
                                act.wait_ge(st_ps, 2 * STEPS * g + 2 * n + ab + 1)
                                nc.scalar.activation(pt[n % 2][:, 2 * ab:2 * ab + 2, :].rearrange("p h t -> p (h t)"),
                                                     PB[ab][:, :], ACT.Exp, scale=HD0 ** -0.5).then_inc(p_ready, 1)
                            if n == TT:
                                act.wait_ge(pv_done, STEPS * g + TT)
                                nc.scalar.activation(OT[:, ds(g, 1), 0:HALF].rearrange("p o t -> p (o t)"),
                                                     PB[2][:, 0:HALF], ACT.Copy).then_inc(o_out[0], 1)

            @block.vector
            def _(dve):
                V = nc.vector

                def maxima(par, g, units):
                    for u in units:
                        dve.wait_ge(max_ps, MU * g + u + 1)
                        V.reduce_max(mx[par][:, u // 2, u % 2:u % 2 + 1], mbank(u), X).then_inc(max_done, 1)

                def columns(par, g):
                    dve.wait_ge(max_done, MU * (g + 1))
                    V.reduce_max(mcol[par][:, :], mx[par][:, :, :], X).then_inc(m_ready, 1)

                def rows(par, g, old):
                    if old is not None:
                        dve.wait_ge(*old)
                    dve.wait_ge(m_rows, g + 1)
                    src = PB[3][0:HG * TT, 0:P]
                    V.tensor_scalar_mul(mrow[par][:, 0, :], src, -1.0).then_inc(row_step, 1)
                    dve.wait_ge(row_step, 3 * g + 1)
                    V.scalar_tensor_tensor(out=mrest[par][:, :], in0=src, scalar=-1.0, in1=mrow[par][:, 0, :],
                                           op0=ALU.mult, op1=ALU.subtract).then_inc(row_step, 1)
                    dve.wait_ge(row_step, 3 * g + 2)
                    V.tensor_copy(mrow[par][:, 1, :], mrest[par][:, :]).then_inc(row_step, 1)
                    dve.wait_ge(row_step, 3 * g + 3)
                    V.tensor_tensor(mrow[par][:, 2, :], mrest[par][:, :], mrow[par][:, 1, :],
                                    ALU.subtract).then_inc(row_ready, 1)

                maxima(0, 0, range(MU))
                columns(0, 0)
                rows(0, 0, None)
                maxima(1, 1, range(EARLY))
                with dve.Fori(0, B) as b:
                    for k in range(GB):
                        g, par = b * GB + k, (k + 1) % 2
                        maxima(par, g + 1, range(EARLY, MU))
                        columns(par, g + 1)
                        maxima(k % 2, g + 2, range(2))
                        rows(par, g + 1, (shifted[(k - 1) % GB], 48 * (b + 1) if k else 48 * b))
                        maxima(k % 2, g + 2, range(2, EARLY))
                        dve.wait_ge(pv_done, STEPS * g + STEPS)
                        V.tensor_copy(OT[:, ds(g, 1), HALF:T].rearrange("p o t -> p (o t)"),
                                      PB[2][:, 0:HALF]).then_inc(o_out[1], 1)

            @block.tensor
            def _(pe):
                mm = nc.tensor.matmul

                def max_unit(slot, g, u):
                    if u >= MB:
                        pe.wait_ge(max_done, MU * g + (u - MB + 1 if u > MB else 2))
                    elif g is not FIRST:
                        pe.wait_ge(max_done, MU * g - (2 if u == 0 else 0))
                        if u == 2:
                            pe.wait_ge(row_ready, g)
                    h, it, jh = u // (2 * TT), u // 2 % TT, u % 2
                    mm(mbank(u), qa[slot][0:KS, h, it * P:(it + 1) * P],
                       ka[slot][0:KS, h, jh * HALF:(jh + 1) * HALF], start=True, stop=True).then_inc(max_ps, 1)

                def max_rows(par, g):
                    pe.wait_ge(m_ready, g + 1)
                    nc.tensor.transpose(PB[3][0:HG * TT, 0:P], mcol[par][:, :], ident[:, :]).then_inc(m_rows, 1)

                def weighted(k, g, n):
                    ih, jt = n // TT, n % TT
                    if jt == 0:
                        pe.wait_ge(o_out[1 - ih], g + ih)
                    pe.wait_ge(p_ready, 2 * STEPS * g + 2 * n + 2)
                    for q in range(HG):
                        last = mm(PB[2][32 * q:32 * q + 32, 0:HALF], vst[k % 2][:, jt, q, :],
                                  pt[n % 2][:, q, :], start=(jt == 0), stop=(jt == TT - 1))
                    last.then_inc(pv_done, 1)

                pe.wait_ge(staged[0], DMAS)
                for u in range(MU):
                    max_unit(0, FIRST, u)
                max_rows(0, 0)
                pe.wait_ge(staged[1], DMAS)
                for u in range(EARLY):
                    max_unit(1, 1, u)
                pe.wait_ge(consts, GB + 4)
                with pe.Fori(0, B) as b:
                    for k in range(GB):
                        g = b * GB + k
                        pe.wait_ge(shifted[k], 48 * (b + 1))
                        pe.wait_ge(v_in, g + 1)
                        units = iter([(1, u) for u in range(EARLY, MU)] + [(2, u) for u in range(EARLY)])

                        def maxima(count):
                            for ahead, u in itertools.islice(units, count):
                                slot = (k + ahead) % GB
                                if (ahead, u) in ((1, EARLY), (2, 0)):
                                    pe.wait_ge(staged[slot], DMAS * (b + 1) if k + ahead < GB else DMAS * (b + 2))
                                max_unit(slot, g + ahead, u)

                        for n in range(STEPS):
                            ih, jt = n // TT, n % TT
                            for ab in range(2):
                                pe.wait_ge(p_ready, 2 * STEPS * g + (2 * n + ab - 1 if n else 0))
                                for q in (2 * ab, 2 * ab + 1):
                                    last = mm(PB[ab][:, (q % 2) * HALF:(q % 2 + 1) * HALF], ka[k][:, q, jt * P:(jt + 1) * P],
                                              qa[k][:, q, ih * HALF:(ih + 1) * HALF], start=True, stop=True)
                                last.then_inc(st_ps, 1)
                                if n != ROWS_AT + 1 or ab == 1:
                                    maxima(1)
                            if n == ROWS_AT:
                                max_rows((k + 1) % 2, g + 1)
                            rest = PLAN[n] - (1 if n == ROWS_AT + 1 else 2)
                            maxima(max(rest - 2, 0))
                            if n >= 1:
                                weighted(k, g, n - 1)
                            maxima(min(rest, 2))
                        weighted(k, g, STEPS - 1)


def load_phi(sp, G, A, c):
    sp.dma_start(G["phi"][:, :, :], A["phi"][:, ds(c * CS, CS)].rearrange("(k p) s -> p k s", p=P)).then_inc(G["ld_phi"], 16)


def split_phi(nc, pool, G, c):
    V, phi, (high, low) = nc.gpsimd, G["phi"], G["phis"]
    pool.wait_ge(G["ld_phi"], 16 * (c + 1))
    pool.sem_inc(G["passed"], 1)
    V.tensor_copy(high[:, :, :], phi[:, :, :]).then_inc(G["phi_high"], 1)
    pool.wait_ge(G["phi_high"], c + 1)
    V.tensor_tensor(low[:, :, :], phi[:, :, :], high[:, :, :].bitcast(F32), ALU.subtract).then_inc(G["phi_low"], 1)


def stage_out0(nc, G, A):
    with ExitStack() as ctx:
        sb = lambda n, s, dt=F32: ctx.enter_context(nc.sbuf_tensor(n, s, dt))
        sem = lambda n: ctx.enter_context(nc.semaphore(n))
        PB, ident, OT = G["PB"], G["ident"], G["OT"]
        wout = sb("o_wout", [P, KD, D])
        bout = sb("o_bout", [P, KD])
        boutB = sb("o_boutB", [P, D])
        outT = sb("o_outT", [P, KD, N])
        dg = sb("o_dg", [P, 2, 2, H0])
        ot = sb("o_ot", [P, 2, D])
        og = sb("o_og", [P, 2, D])
        xt = sb("o_xt", [P, KD, HALF])
        x0 = sb("o_x0", [P, 2, D])
        csum = sb("o_csum", [P, KD, N // HALF])
        ld, t1_ps, ot_step, og_ready, t2_ps, outT_ready, x0_ps, x0_done, xt_ps, xt_done = (sem("o_" + n) for n in (
            "ld", "t1_ps", "ot_step", "og_ready", "t2_ps", "outT_ready", "x0_ps", "x0_done", "xt_ps", "xt_done"))
        x0_high, x0_low, xt_high, xt_low = (sem("o_" + n) for n in ("x0_high", "x0_low", "xt_high", "xt_low"))
        X0T, X0 = G["X0T"], G["X0"]
        TILES = B * TT

        with nc.Block() as block:
            @block.sync
            def _(sp):
                sp.dma_start(wout[:, :, :], A["woutT"].rearrange("(k p) n -> p k n", p=P)).then_inc(ld, 16)
                sp.dma_start(bout[:, :], A["bout"]).then_inc(ld, 16)
                sp.dma_start(boutB[:, :], A["boutB"]).then_inc(ld, 16)
                load_phi(sp, G, A, 0)

            @block.tensor
            def _(pe):
                mm, tr = nc.tensor.matmul, nc.tensor.transpose
                pe.wait_ge(ld, 48)
                for i in range(TILES + 3):
                    if i < TILES:
                        if i >= 2:
                            pe.wait_ge(og_ready, i - 1)
                        b, it = i // TT, i % TT
                        for hg in range(4):
                            last = tr(PB[0][:, HALF * (i % 2) + hg * P:HALF * (i % 2) + (hg + 1) * P],
                                      OT[:, 4 * b + hg, it * P:(it + 1) * P], ident[:, :])
                        last.then_inc(t1_ps, 1)
                    if 2 <= i < TILES + 2:
                        t = i - 2
                        pe.wait_ge(og_ready, t + 1)
                        if t >= 2:
                            pe.wait_ge(outT_ready, t - 1)
                        for k in range(KD):
                            last = tr(PB[1][:, HALF * (t % 2) + k * P:HALF * (t % 2) + (k + 1) * P],
                                      og[:, t % 2, k * P:(k + 1) * P], ident[:, :])
                        last.then_inc(t2_ps, 1)
                    if i >= 3:
                        t = i - 3
                        pe.wait_ge(outT_ready, t + 1)
                        if t >= 2:
                            pe.wait_ge(x0_done, t - 1)
                        for k in range(KD):
                            last = mm(PB[2][:, HALF * (t % 2):HALF * (t % 2) + D], outT[:, k, t * P:(t + 1) * P],
                                      wout[:, k, :], start=(k == 0), stop=(k == KD - 1))
                        last.then_inc(x0_ps, 1)
                        if t % 4 == 3:
                            n = t // 4
                            for m in range(KD):
                                if n >= 1:
                                    pe.wait_ge(xt_done, KD * (n - 1) + m + 1)
                                for k in range(KD):
                                    last = mm(PB[3][:, m * HALF:(m + 1) * HALF], wout[:, k, m * P:(m + 1) * P],
                                              outT[:, k, n * HALF:(n + 1) * HALF], start=(k == 0), stop=(k == KD - 1))
                                last.then_inc(xt_ps, 1)

            def project(act, n):
                for m in range(KD):
                    act.wait_ge(xt_ps, KD * n + m + 1)
                    if n >= 1:
                        act.wait_ge(xt_low, KD * (n - 1) + m + 1)
                    nc.scalar.activation(xt[:, m, :], PB[3][:, m * HALF:(m + 1) * HALF], ACT.Identity,
                                         bias=bout[:, m:m + 1], accum_out=csum[:, m, n:n + 1]).then_inc(xt_done, 1)

            @block.scalar
            def _(act):
                act.wait_ge(ld, 48)
                for t in range(TILES):
                    act.wait_ge(t2_ps, t + 1)
                    nc.scalar.activation(outT[:, :, t * P:(t + 1) * P],
                                         PB[1][:, HALF * (t % 2):HALF * (t % 2) + D].rearrange("p (k t) -> p k t", k=KD),
                                         ACT.Copy).then_inc(outT_ready, 1)
                    if t % 4 == 0 and t >= 4:
                        project(act, t // 4 - 1)
                project(act, TILES // 4 - 1)

            @block.vector
            def _(dve):
                V = nc.vector
                dve.wait_ge(ld, 48)
                link = chain(dve, ot_step)

                def split_columns(n):
                    for m in range(KD):
                        dve.wait_ge(xt_done, KD * n + m + 1)
                        V.tensor_copy(X0T[0][:, m, n * HALF:(n + 1) * HALF], xt[:, m, :]).then_inc(xt_high, 1)

                for t in range(TILES + 2):
                    if t < TILES:
                        b, it, s = t // TT, t % TT, t % 2
                        dve.wait_ge(t1_ps, t + 1)
                        if t >= 2:
                            dve.wait_ge(t2_ps, t - 1)
                        heads = PB[0][:, HALF * s:HALF * s + HALF].rearrange("p (h r) -> p h r", r=32)
                        link(V.tensor_tensor(dg[:, s, 0, :], heads[:, :, HD0], G["gate"][:, t * H0:(t + 1) * H0], ALU.mult))
                        link(V.reciprocal(dg[:, s, 1, :], dg[:, s, 0, :]))
                        link(V.tensor_tensor(ot[:, s, :].rearrange("p (h d) -> p h d", d=HD0), heads[:, :, 0:HD0],
                                             dg[:, s, 1, :].unsqueeze(2).to_broadcast([P, H0, HD0]), ALU.mult))
                        V.scalar_tensor_tensor(out=og[:, s, :], in0=G["vsum"][:, b, :], scalar=G["fa"][:, it, b:b + 1],
                                               in1=ot[:, s, :], op0=ALU.mult, op1=ALU.add).then_inc(og_ready, 1)
                    if t >= 2:
                        r = t - 2
                        dve.wait_ge(x0_ps, r + 1)
                        if r >= 2:
                            dve.wait_ge(x0_low, r - 1)
                        V.tensor_tensor(x0[:, r % 2, :], PB[2][:, HALF * (r % 2):HALF * (r % 2) + D], boutB[:, :],
                                        ALU.add).then_inc(x0_done, 1)
                        dve.wait_ge(x0_done, r + 1)
                        V.tensor_copy(X0[0][:, r, :], x0[:, r % 2, :]).then_inc(x0_high, 1)
                        if r % 4 == 0 and r >= 4:
                            split_columns(r // 4 - 1)
                split_columns(TILES // 4 - 1)
                link(V.tensor_reduce(G["csum"][:, :, :], csum[:, :, :].rearrange("p k (b n) -> p k b n", b=B), X, ALU.add))
                link(V.tensor_scalar_mul(G["csum"][:, :, :], G["csum"][:, :, :], 0.5))

            @block.gpsimd
            def _(pool):
                V = nc.gpsimd
                split_phi(nc, pool, G, 0)
                for t in range(TILES):
                    pool.wait_ge(x0_high, t + 1)
                    V.tensor_tensor(X0[1][:, t, :], x0[:, t % 2, :], X0[0][:, t, :].bitcast(F32),
                                    ALU.subtract).then_inc(x0_low, 1)
                    if t % 4 == 1 and t >= 4 or t == TILES - 1:
                        n = t // 4 - (t < TILES - 1)
                        for m in range(KD):
                            ts = slice(n * HALF, (n + 1) * HALF)
                            pool.wait_ge(xt_high, KD * n + m + 1)
                            V.tensor_tensor(X0T[1][:, m, ts], xt[:, m, :], X0T[0][:, m, ts].bitcast(F32),
                                            ALU.subtract).then_inc(xt_low, 1)


def stage_moe(nc, G, A):
    with ExitStack() as ctx:
        sb = lambda n, s, dt=F32: ctx.enter_context(nc.sbuf_tensor(n, s, dt))
        sem = lambda n: ctx.enter_context(nc.semaphore("f_" + n))
        PB, ident, X0T, X0 = G["PB"], G["ident"], G["X0T"], G["X0"]
        TILES = B * TT
        NT = CS // P
        phis, phi_low = G["phis"], G["phi_low"]
        wex = sb("f_wex", [P, CE, KD, D])
        bex = sb("f_bex", [P, NT, D])
        with ExitStack() as dispatching:
            own = lambda n, s, dt=F32: dispatching.enter_context(nc.sbuf_tensor(n, s, dt))
            l1s = own("f_l1s", [P, 2, CS])
            dl = own("f_dl", [P, 2, CS])
            th = own("f_th", [P, 2, CS])
            ths = [own(f"f_th_{c}", [P, 2, CS], F32R) for c in range(2)]
        y = sb("f_y", [P, 2, B, D])
        ys = [sb(f"f_y_{c}", [P, NT, B, D], F32R) for c in range(2)]
        E = sb("f_E", [P, TILES, CS])
        ETs = [sb(f"f_ET_{c}", [P, 2, NT, P], F32R) for c in range(2)]
        slT = sb("f_slT", [P, B, KD, CS])
        mc = sb("f_mc", [P, TILES])
        nmc = sb("f_nmc", [P, TILES])
        dc = sb("f_dc", [P, TILES])
        mrun = sb("f_mrun", [P, 2, TILES])
        arg = sb("f_arg", [P, 2, TILES])
        fac = sb("f_fac", [P, 2, TILES])
        dtmp = sb("f_dtmp", [P, 2, TILES])
        passed = G["passed"]
        w_in, init = sem("w_in"), sem("init")
        lg_ps, l1_sb, mx_done, neg_done, dl_done, e_done, th_done, sl_done = (sem(n) for n in (
            "lg_ps", "l1_sb", "mx_done", "neg_done", "dl_done", "e_done", "th_done", "sl_done"))
        sl_out, et_ps, et_out, y_ps, y_out, oc_ps, oc_out = (sem(n) for n in (
            "sl_out", "et_ps", "et_out", "y_ps", "y_out", "oc_ps", "oc_out"))
        run_step, run_arg, run_fac = sem("run_step"), sem("run_arg"), sem("run_fac")
        et_low, y_high, y_low, sl_out2, o_scaled = sem("et_low"), sem("y_high"), sem("y_low"), sem("sl_out2"), sem("o_scaled")
        th_high, th_low, sl_first = sem("th_high"), sem("th_low"), sem("sl_first")
        LW = 48
        O, DEN = G["O"], G["den"]
        AHEAD = 3

        def logit_bank(mt):
            return PB[2 + mt] if mt < 2 else PB[mt % 2]

        with nc.Block() as block:
            @block.sync
            def _(sp):
                with sp.Fori(0, CH) as c:
                    sp.wait_ge(phi_low, c + 1)
                    sp.sem_inc(passed, 1)
                    load_phi(sp, G, A, c + 1)
                    sp.wait_ge(y_ps, NT * c)
                    sp.wait_ge(y_out, NT * c)
                    sp.sem_inc(passed, 1)
                    for k in range(KD):
                        sp.dma_start(wex[:, :, k, :], A["W"][ds(c * CE, CE), k * P:(k + 1) * P, :]
                                     .rearrange("n p e -> p n e")).then_inc(w_in, 16)
                    sp.dma_start(bex[:, :, :], A["bexp"][ds(c * CS, CS), :]
                                 .rearrange("(t p) e -> p t e", p=P)).then_inc(w_in, 16)

            @block.gpsimd
            def _(pool):
                nc.gpsimd.memset(O[:, :, :], 0.0).then_inc(init, 1)
                nc.gpsimd.memset(DEN[:, :], 0.0).then_inc(init, 1)
                nc.gpsimd.memset(mrun[:, 0, :], LOWEST).then_inc(init, 1)
                V = nc.gpsimd

                pool.wait_ge(init, 3)
                with pool.Fori(0, CH) as c:
                    pool.wait_ge(run_fac, c + 1)
                    pool.wait_ge(oc_out, TILES * c)
                    for i in range(4):
                        ts = slice(i * TILES // 4, (i + 1) * TILES // 4)
                        V.tensor_tensor(O[:, ts, :], O[:, ts, :], fac[:, 0, ts].unsqueeze(2).to_broadcast([P, TILES // 4, D]),
                                        ALU.mult).then_inc(o_scaled, 1)
                    split_phi(nc, pool, G, c + 1)

            @block.tensor
            def _(pe):
                mm, tr = nc.tensor.matmul, nc.tensor.transpose
                with pe.Fori(0, CH) as c:
                    def dispatch(mt):
                        pe.wait_ge(th_low, TT * c + mt + 1)
                        for b in range(B):
                            for k in range(KD):
                                for n, (cx, ct) in enumerate(PRODUCTS):
                                    last = mm(PB[2 + b][:, k * HALF:(k + 1) * HALF], X0[cx][:, b * TT + mt, k * P:(k + 1) * P],
                                              ths[ct][:, mt % 2, :], start=(mt == n == 0),
                                              stop=(mt == TT - 1 and n == len(PRODUCTS) - 1))
                            if mt == TT - 1 and b == 0:
                                last.then_inc(sl_first, 1)
                        last.then_inc(sl_done, 1)

                    def expo_rows(t):
                        for n in range(NT):
                            last = tr(PB[0][:, HALF * (t % 2) + n * P:HALF * (t % 2) + (n + 1) * P],
                                      E[:, t, n * P:(n + 1) * P], ident[:, :])
                        last.then_inc(et_ps, 1)

                    pe.wait_ge(phi_low, c + 1)
                    for mt in range(TT):
                        if mt < 2:
                            pe.wait_ge(y_out, NT * c)
                        elif mt < 4:
                            pe.wait_ge(et_low, TILES * c)
                            pe.wait_ge(oc_out, TILES * c)
                        else:
                            pe.wait_ge(e_done, TT * c + mt - 1)
                            pe.wait_ge(dl_done, TT * c + mt - 1)
                        for b in range(B):
                            for n, (cx, cp) in enumerate(PRODUCTS):
                                for k in range(KD):
                                    last = mm(logit_bank(mt)[:, b * HALF:(b + 1) * HALF],
                                              X0T[cx][:, k, b * T + mt * P:b * T + (mt + 1) * P], phis[cp][:, k, :],
                                              start=(n == k == 0), stop=(n == len(PRODUCTS) - 1 and k == KD - 1))
                        last.then_inc(lg_ps, 1)
                        if mt == AHEAD:
                            pe.wait_ge(e_done, TT * c + 2)
                            pe.wait_ge(dl_done, TT * c + 2)
                        if mt >= AHEAD:
                            dispatch(mt - AHEAD)
                    for mt in range(TT - AHEAD, TT):
                        dispatch(mt)
                    pe.wait_ge(e_done, TT * c + TT)
                    pe.wait_ge(dl_done, TT * c + TT)
                    expo_rows(0)
                    expo_rows(1)
                    pe.wait_ge(w_in, LW * (c + 1))
                    pe.wait_ge(sl_out, 3 * c + 2)
                    for n in range(NT):
                        for b in range(B):
                            if n == 0 and b == 1:
                                pe.wait_ge(sl_out, 3 * c + 3)
                                pe.wait_ge(sl_out2, c + 1)
                            for k in range(KD):
                                for q in range(4):
                                    s0 = n * P + 32 * q
                                    last = mm(PB[2 + n // 2][32 * q:32 * q + 32, (n % 2) * HALF + b * D:(n % 2) * HALF + (b + 1) * D],
                                              slT[:, b, k, s0:s0 + 32], wex[:, 4 * n + q, k, :],
                                              start=(k == 0), stop=(k == KD - 1))
                        last.then_inc(y_ps, 1)
                    for t in range(TILES):
                        pe.wait_ge(et_low, TILES * c + t + 1)
                        if t >= 2:
                            pe.wait_ge(oc_out, TILES * c + t - 1)
                        for n in range(NT):
                            if t == 0:
                                pe.wait_ge(y_low, NT * c + n + 1)
                            for i, (ce, cy) in enumerate(PRODUCTS):
                                last = mm(PB[1][:, HALF * (t % 2):HALF * (t % 2) + D], ETs[ce][:, t % 2, n, :],
                                          ys[cy][:, n, t // TT, :], start=(n == i == 0),
                                          stop=(n == NT - 1 and i == len(PRODUCTS) - 1))
                        last.then_inc(oc_ps, 1)
                        if t + 2 < TILES:
                            pe.wait_ge(et_low, TILES * c + t + 1)
                            expo_rows(t + 2)

            @block.scalar
            def _(act):
                S = nc.scalar.activation
                act.wait_ge(init, 3)
                with act.Fori(0, CH) as c:
                    def second_logits(mt):
                        act.wait_ge(lg_ps, TT * c + mt + 1)
                        act.wait_ge(dl_done, TT * c + max(mt - 1, 0))
                        S(l1s[:, mt % 2, :], logit_bank(mt)[:, HALF:2 * HALF], ACT.Copy).then_inc(l1_sb, 1)

                    second_logits(0)
                    for mt in range(TT):
                        s, a = mt % 2, TT * c + mt
                        if mt + 1 < TT:
                            second_logits(mt + 1)
                        act.wait_ge(neg_done, a + 1)
                        act.wait_ge(dl_done, a + 1)
                        for b in range(B):
                            t = b * TT + mt
                            last = S(E[:, t, :], logit_bank(mt)[:, b * HALF:(b + 1) * HALF], ACT.Exp, bias=nmc[:, t:t + 1],
                                     accum_out=dc[:, t:t + 1])
                        last.then_inc(e_done, 1)
                        act.wait_ge(th_low, TT * c + max(mt - 1, 0))
                        S(th[:, s, :], dl[:, s, :], ACT.Tanh, scale=0.5).then_inc(th_done, 1)
                    act.wait_ge(sl_first, c + 1)
                    for k in range(KD):
                        S(slT[:, 0, k, :], PB[2][:, k * HALF:(k + 1) * HALF], ACT.Identity,
                          bias=G["csum"][:, k, 0:1], scale=0.5).then_inc(sl_out, 1)
                    act.wait_ge(sl_done, TT * (c + 1))
                    S(slT[:, 1, 1, :], PB[3][:, HALF:2 * HALF], ACT.Identity,
                      bias=G["csum"][:, 1, 1:2], scale=-0.5).then_inc(sl_out, 1)
                    act.wait_ge(run_arg, c + 1)
                    S(fac[:, :, :], arg[:, :, :], ACT.Exp).then_inc(run_fac, 1)
                    for t in range(TILES):
                        act.wait_ge(et_ps, TILES * c + t + 1)
                        act.wait_ge(oc_ps, TILES * c + max(t - 1, 0))
                        S(ETs[0][:, t % 2, :, :].rearrange("p n m -> p (n m)"), PB[0][:, HALF * (t % 2):HALF * (t % 2) + HALF],
                          ACT.Copy).then_inc(et_out, 1)

            @block.vector
            def _(dve):
                V = nc.vector
                dve.wait_ge(init, 3)

                with dve.Fori(0, CH) as c:
                    def split_dispatch(mt):
                        s, a = mt % 2, TT * c + mt
                        dve.wait_ge(th_done, a + 1)
                        dve.wait_ge(sl_done, TT * c + max(mt - 1, 0))
                        V.tensor_copy(ths[0][:, s, :], th[:, s, :]).then_inc(th_high, 1)
                        dve.wait_ge(th_high, a + 1)
                        V.tensor_tensor(ths[1][:, s, :], th[:, s, :], ths[0][:, s, :].bitcast(F32), ALU.subtract).then_inc(th_low, 1)

                    for mt in range(TT):
                        s, a = mt % 2, TT * c + mt
                        dve.wait_ge(l1_sb, a + 1)
                        pair = mc[:, :].rearrange("p (b t) -> p b t", b=B)[:, :, mt]
                        npair = nmc[:, :].rearrange("p (b t) -> p b t", b=B)[:, :, mt]
                        V.reduce_max(pair, logit_bank(mt)[:, :].rearrange("p (b n) -> p b n", b=B), X).then_inc(mx_done, 1)
                        dve.wait_ge(th_done, TT * c + max(mt - 1, 0))
                        V.tensor_tensor(dl[:, s, :], logit_bank(mt)[:, 0:HALF], l1s[:, s, :], ALU.subtract).then_inc(dl_done, 1)
                        dve.wait_ge(mx_done, a + 1)
                        V.tensor_scalar_mul(npair, pair, -1.0).then_inc(neg_done, 1)
                        if mt >= 1:
                            split_dispatch(mt - 1)
                    split_dispatch(TT - 1)
                    dve.wait_ge(sl_done, TT * (c + 1))
                    V.tensor_scalar(slT[:, 1, 0, :], PB[3][:, 0:HALF], -0.5, G["csum"][:, 0, 1:2],
                                    ALU.mult, ALU.add).then_inc(sl_out2, 1)
                    link = chain(dve, run_step, 6 * c)
                    link(V.tensor_tensor(mrun[:, 1, :], mrun[:, 0, :], mc[:, :], ALU.max))
                    link(V.tensor_tensor(arg[:, 0, :], mrun[:, 0, :], mrun[:, 1, :], ALU.subtract))
                    V.tensor_tensor(arg[:, 1, :], mc[:, :], mrun[:, 1, :], ALU.subtract).then_inc(run_arg, 1)
                    link(V.tensor_copy(mrun[:, 0, :], mrun[:, 1, :]))
                    dve.wait_ge(run_fac, c + 1)
                    link(V.tensor_tensor(dtmp[:, 0, :], DEN[:, :], fac[:, 0, :], ALU.mult))
                    link(V.tensor_tensor(dtmp[:, 1, :], dc[:, :], fac[:, 1, :], ALU.mult))
                    link(V.tensor_tensor(DEN[:, :], dtmp[:, 0, :], dtmp[:, 1, :], ALU.add))
                    def split_rows(t):
                        dve.wait_ge(et_out, TILES * c + t + 1)
                        V.tensor_tensor(ETs[1][:, t % 2, :, :].rearrange("p n m -> p (n m)"),
                                        PB[0][:, HALF * (t % 2):HALF * (t % 2) + HALF],
                                        ETs[0][:, t % 2, :, :].bitcast(F32).rearrange("p n m -> p (n m)"),
                                        ALU.subtract).then_inc(et_low, 1)

                    dve.wait_ge(w_in, LW * (c + 1))
                    for n in range(NT):
                        dve.wait_ge(y_ps, NT * c + n + 1)
                        V.tensor_tensor(y[:, n % 2, :, :],
                                        PB[2 + n // 2][:, (n % 2) * HALF:(n % 2 + 1) * HALF].rearrange("p (b e) -> p b e", b=B),
                                        bex[:, n, :].unsqueeze(1).to_broadcast([P, B, D]), ALU.add).then_inc(y_out, 1)
                        dve.wait_ge(y_out, NT * c + n + 1)
                        V.tensor_copy(ys[0][:, n, :, :], y[:, n % 2, :, :]).then_inc(y_high, 1)
                        dve.wait_ge(y_high, NT * c + n + 1)
                        V.tensor_tensor(ys[1][:, n, :, :], y[:, n % 2, :, :], ys[0][:, n, :, :].bitcast(F32),
                                        ALU.subtract).then_inc(y_low, 1)
                        if n < 2:
                            split_rows(n)

                    for t in range(TILES):
                        if t % (TILES // 4) == 0:
                            dve.wait_ge(o_scaled, 4 * c + t // (TILES // 4) + 1)
                        dve.wait_ge(oc_ps, TILES * c + t + 1)
                        V.scalar_tensor_tensor(out=O[:, t, :], in0=PB[1][:, HALF * (t % 2):HALF * (t % 2) + D],
                                               scalar=fac[:, 1, t:t + 1], in1=O[:, t, :], op0=ALU.mult,
                                               op1=ALU.add).then_inc(oc_out, 1)
                        if t + 2 < TILES:
                            split_rows(t + 2)
                    dve.wait_ge(oc_out, TILES * (c + 1))


def load_attention1(sp, G, A, l):
    sp.dma_start(G["wqkv1_raw"][:, :, :], A["wqkv1"][l].rearrange("(k p) n -> p k n", p=P)).then_inc(G["ld_att"], 16)
    sp.dma_start(G["wo"][:, :, :], A["wo"][l].rearrange("(k p) n -> p k n", p=P)).then_inc(G["ld_att"], 16)


def load_ffn1(sp, G, A, l):
    sp.dma_start(G["w1"][:, :, :], A["w1"][l].rearrange("(k p) n -> p k n", p=P)).then_inc(G["ld_ffn"], 16)
    sp.dma_start(G["w2"][:, :, :], A["w2"][l].rearrange("(k p) n -> p k n", p=P)).then_inc(G["ld_ffn"], 16)
    for name in ("lg", "lb", "b1", "b2"):
        sp.dma_start(G[name][:, :], A[name][l]).then_inc(G["ld_ffn"], 16)


LD_ATT, LD_FFN = 32, 96


def copy_wqkv(nc, act, G, l):
    act.wait_ge(G["ld_att"], LD_ATT * (l + 1))
    for k in range(KD):
        nc.scalar.activation(G["wqkv1"][1][:, k, :], G["wqkv1_raw"][:, k, :], ACT.Copy).then_inc(G["wqkv_copy"], 1)


def split_wqkv(nc, pool, G, l):
    low = G["wqkv1"][1]
    for k in range(KD):
        pool.wait_ge(G["wqkv_copy"], KD * l + k + 1)
        nc.gpsimd.tensor_tensor(low[:, k, :], G["wqkv1_raw"][:, k, :], low[:, k, :].bitcast(F32),
                                ALU.subtract).then_inc(G["wqkv_low"], 1)


def round_wqkv(nc, act, G, l):
    for k in range(KD):
        act.wait_ge(G["wqkv_low"], KD * l + k + 1)
        nc.scalar.activation(G["wqkv1"][0][:, k, :], G["wqkv1_raw"][:, k, :], ACT.Copy).then_inc(G["wqkv_high"], 1)


def stage_rotate(nc, G, A):
    with ExitStack() as ctx:
        sb = lambda n, s, dt=F32: ctx.enter_context(nc.sbuf_tensor(n, s, dt))
        sem = lambda n: ctx.enter_context(nc.semaphore("r_" + n))
        PB, ident, xr = G["PB"], G["ident"], G["xr"]
        TILES = B * TT
        x1T = sb("r_x1T", [P, KD, N])
        rden = sb("r_rden", [P, TILES])
        on = sb("r_on", [P, 2, D])
        step, on_ready, t_ps, x1_done, rot_ps, rot_out, zeroed = (sem(n) for n in (
            "step", "on_ready", "t_ps", "x1_done", "rot_ps", "rot_out", "zeroed"))
        ld_x = [sem(f"ld_x{n}") for n in range(N // HALF)]
        with nc.Block() as block:
            @block.sync
            def _(sp):
                for n in range(N // HALF):
                    ts = slice(n * HALF, (n + 1) * HALF)
                    sp.dma_start(x1T[:, :, ts], A["xT"].rearrange("(k p) n -> p k n", p=P)[:, :, ts]).then_inc(ld_x[n], 16)
                load_attention1(sp, G, A, 0)
                sp.dma_start(G["mask"][:, :], A["mask"]).then_inc(G["ld_tab"], 16)
                sp.dma_start(G["qks"][:, :, :, :], A["qks"]).then_inc(G["ld_tab"], 16)
                for n in range(N // HALF):
                    ts = slice(n * HALF, (n + 1) * HALF)
                    sp.wait_ge(x1_done, 4 * n + 4)
                    sp.dma_start(G["x1"].rearrange("(k p) n -> p k n", p=P)[:, :, ts], x1T[:, :, ts]).then_inc(G["x1_out"], 16)
                sp.wait_ge(G["x1_out"], 16 * (N // HALF))

            @block.gpsimd
            def _(pool):
                nc.gpsimd.memset(xr[:, :, :, 0:1], 0.0).then_inc(zeroed, 1)
                split_wqkv(nc, pool, G, 0)

            @block.vector
            def _(dve):
                V = nc.vector
                link = chain(dve, step)
                link(V.reciprocal(rden[:, :], G["den"][:, :]))
                for t in range(TILES + 1):
                    if t < TILES:
                        if t >= 2:
                            dve.wait_ge(t_ps, t - 1)
                        V.tensor_scalar_mul(on[:, t % 2, :], G["O"][:, t, :], rden[:, t:t + 1]).then_inc(on_ready, 1)
                    if t >= 1:
                        r = t - 1
                        if r * P % HALF == 0:
                            dve.wait_ge(ld_x[r * P // HALF], 16)
                        dve.wait_ge(t_ps, r + 1)
                        V.tensor_tensor(x1T[:, :, r * P:(r + 1) * P],
                                        PB[0][:, HALF * (r % 2):HALF * (r % 2) + D].rearrange("p (k t) -> p k t", k=KD),
                                        x1T[:, :, r * P:(r + 1) * P], ALU.add).then_inc(x1_done, 1)

            @block.tensor
            def _(pe):
                def rotate(n):
                    pe.wait_ge(x1_done, 4 * n + 4)
                    for m in range(KD):
                        if n >= 1:
                            pe.wait_ge(rot_out, KD * (n - 1) + m + 1)
                        for k in range(KD):
                            last = nc.tensor.matmul(PB[1 + m][:, 0:HALF], G["rot"][:, k, m * P:(m + 1) * P],
                                                    x1T[:, k, n * HALF:(n + 1) * HALF], start=(k == 0), stop=(k == KD - 1))
                        last.then_inc(rot_ps, 1)

                for t in range(TILES):
                    pe.wait_ge(on_ready, t + 1)
                    if t >= 2:
                        pe.wait_ge(x1_done, t - 1)
                    for k in range(KD):
                        last = nc.tensor.transpose(PB[0][:, HALF * (t % 2) + k * P:HALF * (t % 2) + (k + 1) * P],
                                                   on[:, t % 2, k * P:(k + 1) * P], ident[:, :])
                    last.then_inc(t_ps, 1)
                    if t % 4 == 1 and t >= 4:
                        rotate(t // 4 - 1)
                rotate(TILES // 4 - 1)

            @block.scalar
            def _(act):
                for n in range(N // HALF):
                    if n == 1:
                        copy_wqkv(nc, act, G, 0)
                    if n == 3:
                        round_wqkv(nc, act, G, 0)
                    for m in range(KD):
                        act.wait_ge(rot_ps, KD * n + m + 1)
                        c0 = 1 + (n % 2) * HALF
                        nc.scalar.activation(xr[:, m, n // 2, c0:c0 + HALF], PB[1 + m][:, 0:HALF],
                                             ACT.Copy).then_inc(rot_out, 1)
                act.wait_ge(zeroed, 1)


def stage_attention1(nc, G, A, l):
    with ExitStack() as ctx:
        sb = lambda n, s, dt=F32: ctx.enter_context(nc.sbuf_tensor(f"w{l}_{n}", s, dt))
        sem = lambda n: G["layer_sem"](f"w_{n}")
        PB, ident, xr, mask = G["PB"], G["ident"], G["xr"], G["mask"]
        wqkv, wo = G["wqkv1"], G["wo"]
        tab = [sb(f"tab{i}", [P, NW, HD1]) for i in range(4)]
        qkr = sb("qkr", [P, NW, 2 * INNER])
        vsb = sb("vsb", [P, NW, INNER])
        ss = sb("ss", [P, NW, 2 * H1])
        nrm = sb("nrm", [P, NW, 2 * H1])
        rn = sb("rn", [P, NW, 2 * H1])
        cosp = sb("cosp", [P, 2 * INNER])
        sinp = sb("sinp", [P, 2 * INNER])
        turned = sb("turned", [P, 2, 2 * INNER])
        kT = sb("kT", [P, HP, T])
        qz = sb("qz", [P, 2, HP, 2, P])
        sm = sb("sm", [P, 2, H1, 2 * WIN])
        sq = sm[:, 1, 0:4, :].rearrange("p h n -> p (h n)")
        PT = sb("PT", [P, 2, 4, P])
        with nc.sbuf_tensor(f"w{l}_hst", [P, 2, KD, T], F32R) as hst:
            pass
        oT = sb("oT", [P, HP, T])
        st = sb("st", [P, 2, 4, H1])
        (ld_tab, tabs, zeroed, h_high, h_low, qk_ps, v_ps, qk_sb, v_sb, sq_done, ss_done, n_sqrt, n_step) = (sem(n) for n in (
            "ld_tab", "tabs", "zeroed", "h_high", "h_low", "qk_ps", "v_ps", "qk_sb", "v_sb", "sq_done", "ss_done", "n_sqrt", "n_step"))
        (qn_done, cos_done, sin_done, turn_done, tq_ps, tk_ps, qz_done, kT_done, s_ps, s_masked, m_done, e_done,
         d_done, p_done, pt_ps, pt_act, pt_dve, pv_ps, oT_done, wo_ps, wo_done) = (sem(n) for n in (
            "qn_done", "cos_done", "sin_done", "turn_done", "tq_ps", "tk_ps", "qz_done", "kT_done", "s_ps", "s_masked",
            "m_done", "e_done", "d_done", "p_done", "pt_ps", "pt_act", "pt_dve", "pv_ps", "oT_done", "wo_ps", "wo_done"))
        passed = G["passed"]
        C = HD1 // 2
        NN = NW // 2

        def keys(w):
            return slice(0, 2 * WIN) if w else slice(WIN, 2 * WIN)

        with nc.Block() as block:
            @block.sync
            def _(sp):
                for i in range(4):
                    sp.dma_start(tab[i][:, :, :], A["tables"][i].rearrange("(w p) d -> p w d", p=P)).then_inc(ld_tab, 16)
                load_ffn1(sp, G, A, l)

            @block.gpsimd
            def _(pool):
                V = nc.gpsimd
                for s in range(2):
                    V.memset(qz[64:128, s, :, 0, :], 0.0).then_inc(zeroed, 1)
                    V.memset(qz[0:64, s, :, 1, :], 0.0).then_inc(zeroed, 1)
                pool.wait_ge(zeroed, 4 * (l + 1))
                pool.wait_ge(ld_tab, 16 * 4 * (l + 1))
                pool.wait_ge(G["ld_tab"], 32)
                for i in range(4):
                    V.tensor_tensor(tab[i][:, :, :], tab[i][:, :, :],
                                    G["qks"][:, l, i, :].unsqueeze(1).to_broadcast([P, NW, HD1]), ALU.mult).then_inc(tabs, 1)
                pool.wait_ge(tabs, 4 * (l + 1))
                with pool.Fori(l * B, (l + 1) * B) as b:
                    def turn(w):
                        pool.wait_ge(qn_done, NW * b + w + 1)
                        pool.wait_ge(turn_done, NW * b + w)
                        for j in range(2):
                            V.tensor_tensor(
                                cosp[:, j * INNER:(j + 1) * INNER].rearrange("p (h d) -> p h d", d=HD1),
                                qkr[:, w, j * INNER:(j + 1) * INNER].rearrange("p (h d) -> p h d", d=HD1),
                                tab[2 * j][:, w, :].unsqueeze(1).to_broadcast([P, H1, HD1]), ALU.mult).then_inc(cos_done, 1)

                    def probabilities(w, j):
                        hs = slice(4 * j, 4 * j + 4)
                        pool.wait_ge(d_done, 2 * (NW * b + w) + j + 1)
                        V.tensor_tensor(sm[:, w % 2, hs, keys(w)], sm[:, w % 2, hs, keys(w)],
                                        st[:, w % 2, 3, hs].unsqueeze(2).to_broadcast([P, 4, 2 * WIN if w else WIN]),
                                        ALU.mult).then_inc(p_done, 1)

                    turn(0)
                    turn(1)
                    for i in range(NW + 2):
                        if i >= 2:
                            probabilities(i - 2, 1)
                        if i < NW - 2:
                            turn(i + 2)
                        if 1 <= i <= NW:
                            probabilities(i - 1, 0)

            @block.tensor
            def _(pe):
                mm, tr = nc.tensor.matmul, nc.tensor.transpose
                pe.wait_ge(G["ld_att"], LD_ATT * (l + 1))
                pe.wait_ge(G["wqkv_high"], KD * (l + 1))
                pe.wait_ge(zeroed, 4 * (l + 1))
                with pe.Fori(l * B, (l + 1) * B) as b:
                    pe.wait_ge(oT_done, NW * b)
                    pe.wait_ge(wo_done, 2 * KD * b)
                    pe.wait_ge(pt_act, 2 * NW * b)
                    pe.wait_ge(pt_dve, 2 * NW * b)
                    def project(out, w, j):
                        for n, (ch, cw) in enumerate(PRODUCTS):
                            for k in range(KD):
                                last = mm(out, hst[:, ch, k, w * P:(w + 1) * P], wqkv[cw][:, k, j * INNER:(j + 1) * INNER],
                                          start=(n == k == 0), stop=(n == len(PRODUCTS) - 1 and k == KD - 1))
                        return last

                    for w in range(NW):
                        pe.wait_ge(h_low, KD * (4 * b + w // 2 + 1))
                        if w >= 2:
                            pe.wait_ge(sq_done, NW * b + w - 1)
                        for j in range(2):
                            last = project(PB[w % 2][:, j * HALF:(j + 1) * HALF], w, j)
                        last.then_inc(qk_ps, 1)
                        if w >= 2:
                            pe.wait_ge(v_sb, NW * b + w - 1)
                        project(PB[2][:, (w % 2) * HALF:(w % 2 + 1) * HALF], w, 2).then_inc(v_ps, 1)

                    def query_rows(w):
                        pe.wait_ge(turn_done, NW * b + w + 1)
                        if w == 0:
                            pe.wait_ge(sq_done, NW * (b + 1))
                        if w >= 3:
                            pe.wait_ge(oT_done, NW * b + w - 2)
                        if w >= 1:
                            pe.wait_ge(qz_done, NW * b + w)
                        for p in range(HP):
                            last = tr(PB[0][:, p * P:(p + 1) * P], turned[:, w % 2, p * P:(p + 1) * P], ident[:, :])
                        last.then_inc(tq_ps, 1)

                    def key_rows(w):
                        if w >= 1:
                            pe.wait_ge(kT_done, NW * b + w)
                        for p in range(HP):
                            last = tr(PB[0][:, HALF + p * P:HALF + (p + 1) * P],
                                      turned[:, w % 2, INNER + p * P:INNER + (p + 1) * P], ident[:, :])
                        last.then_inc(tk_ps, 1)

                    def scores(w, heads):
                        pe.wait_ge(qz_done, NW * b + w + 1)
                        pe.wait_ge(kT_done, NW * b + w + 1)
                        if w == 0:
                            pe.wait_ge(v_sb, NW * (b + 1))
                        k0 = (w - 1) * WIN if w else 0
                        for h in heads:
                            if h % 2 == 0 and w >= 1:
                                pe.wait_ge(s_masked, H1 * (NW * b + w - 1) + h + 2)
                            c0 = (h % 4) * 2 * WIN + keys(w).start
                            n = keys(w).stop - keys(w).start
                            mm(PB[1 + h // 4][:, c0:c0 + n], qz[:, w % 2, h // 2, h % 2, :],
                               kT[:, h // 2, k0:k0 + n], start=True, stop=True).then_inc(s_ps, 1)

                    def tiles(w):
                        return (0, 1) if w else (1,)

                    def prob_rows(w, p):
                        pe.wait_ge(p_done, 2 * (NW * b + w) + p // 2 + 1)
                        if p >= 2:
                            pe.wait_ge((pt_act, pt_dve)[p % 2], 2 * (NW * b + w) + 1)
                        elif w >= 1:
                            pe.wait_ge((pt_act, pt_dve)[p % 2], 2 * (NW * b + w))
                        for e in range(2):
                            for j in tiles(w):
                                c0 = (p % 2) * HALF + (2 * e + j) * P
                                last = tr(PB[3][:, c0:c0 + P], sm[:, w % 2, 2 * p + e, j * P:(j + 1) * P], ident[:, :])
                        last.then_inc(pt_ps, 1)

                    def weighted(w, p):
                        pe.wait_ge((pt_act, pt_dve)[p % 2], 2 * (NW * b + w) + p // 2 + 1)
                        if p == 0:
                            pe.wait_ge(qz_done, NW * b + min(w + 3, NW))
                        for j in tiles(w):
                            for e in range(2):
                                h = 2 * p + e
                                last = mm(PB[0][64 * e:64 * e + 64, p * P:(p + 1) * P],
                                          vsb[:, w - 1 + j, h * HD1:(h + 1) * HD1], PT[:, p % 2, 2 * e + j, :],
                                          start=(j == tiles(w)[0]), stop=(j == 1))
                        last.then_inc(pv_ps, 1)

                    for i in range(NW + 2):
                        if 1 <= i <= NW:
                            scores(i - 1, range(2))
                        if i < NW:
                            query_rows(i)
                        if 1 <= i <= NW:
                            scores(i - 1, range(2, H1 - 2))
                        if i >= 2:
                            prob_rows(i - 2, 0)
                            prob_rows(i - 2, 1)
                        if i < NW:
                            key_rows(i)
                        if i >= 2:
                            weighted(i - 2, 0)
                            prob_rows(i - 2, 2)
                            weighted(i - 2, 1)
                            prob_rows(i - 2, 3)
                        if 1 <= i <= NW:
                            scores(i - 1, range(H1 - 2, H1))
                        if i >= 2:
                            weighted(i - 2, 2)
                            weighted(i - 2, 3)
                        if i in (NW // 2 + 2, NW + 1):
                            hf = 0 if i < NW else 1
                            pe.wait_ge(oT_done, NW * b + (NW // 2) * (hf + 1))
                            pe.wait_ge(s_masked, H1 * (NW * b + min(i, NW)))
                            for m in range(KD):
                                for p in range(HP):
                                    last = mm(PB[1][:, m * HALF:(m + 1) * HALF], wo[:, p, m * P:(m + 1) * P],
                                              oT[:, p, hf * HALF:(hf + 1) * HALF], start=(p == 0), stop=(p == HP - 1))
                                last.then_inc(wo_ps, 1)
                            if i < NW:
                                pe.wait_ge(wo_done, 2 * KD * b + KD)

            @block.scalar
            def _(act):
                S = nc.scalar.activation
                with act.Fori(l * B, (l + 1) * B) as b:
                    def norms(half):
                        hs = slice(half * NN, (half + 1) * NN)
                        act.wait_ge(ss_done, NW * b + hs.stop)
                        S(nrm[:, hs, :], ss[:, hs, :], ACT.Sqrt).then_inc(n_sqrt, 1)

                    act.wait_ge(wo_done, 2 * KD * b)
                    for w in range(NW):
                        act.wait_ge(qk_ps, NW * b + w + 1)
                        S(qkr[:, w, :], PB[w % 2][:, :], ACT.Copy).then_inc(qk_sb, 1)
                        act.wait_ge(ss_done, NW * b + w)
                        S(sq[:, :], PB[w % 2][:, :], ACT.Square).then_inc(sq_done, 1)
                        act.wait_ge(v_ps, NW * b + w + 1)
                        S(vsb[:, w, :], PB[2][:, (w % 2) * HALF:(w % 2 + 1) * HALF], ACT.Copy).then_inc(v_sb, 1)
                        if w == NN - 1:
                            norms(0)
                    def exponentials(w, hs):
                        for h in hs:
                            if h % 2 == 0:
                                act.wait_ge(m_done, HP * (NW * b + w) + h // 2 + 1)
                            last = S(sm[:, w % 2, h, keys(w)], sm[:, w % 2, h, keys(w)], ACT.Exp,
                                     bias=st[:, w % 2, 1, h:h + 1], scale=QK_SCALE, accum_out=st[:, w % 2, 2, h:h + 1])
                            if h % 4 == 3:
                                last.then_inc(e_done, 1)

                    def prob_rows(w, p):
                        act.wait_ge(pt_ps, HP * (NW * b + w) + p + 1)
                        if p or w:
                            act.wait_ge(pv_ps, HP * (NW * b + w) + p - 1)
                        c0 = slice(0, 4) if w else slice(1, 4, 2)
                        S(PT[:, 0, c0, :], PB[3][:, 0:HALF].rearrange("p (a t) -> p a t", t=P)[:, c0, :],
                          ACT.Copy).then_inc(pt_act, 1)

                    def queries(w):
                        act.wait_ge(tq_ps, NW * b + w + 1)
                        for e in range(2):
                            last = S(qz[64 * e:64 * e + 64, w % 2, :, e, :],
                                     PB[0][64 * e:64 * e + 64, 0:HALF].rearrange("p (a t) -> p a t", a=HP), ACT.Copy)
                        last.then_inc(qz_done, 1)

                    def keys_of(w):
                        act.wait_ge(tk_ps, NW * b + w + 1)
                        S(kT[:, :, w * WIN:(w + 1) * WIN], PB[0][:, HALF:2 * HALF].rearrange("p (a t) -> p a t", a=HP),
                          ACT.Copy).then_inc(kT_done, 1)

                    queries(0)
                    keys_of(0)
                    norms(1)
                    queries(1)
                    keys_of(1)
                    for i in range(1, NW + 2):
                        if 2 <= i < NW:
                            queries(i)
                        if 1 <= i <= NW:
                            exponentials(i - 1, range(0, 2))
                        if i >= 2:
                            prob_rows(i - 2, 0)
                        if 1 <= i <= NW:
                            exponentials(i - 1, range(2, 4))
                        if 2 <= i < NW:
                            keys_of(i)
                        if i >= 2:
                            prob_rows(i - 2, 2)
                        if 1 <= i <= NW:
                            exponentials(i - 1, range(4, 6))
                        if i >= 2:
                            w = i - 2
                            act.wait_ge(pv_ps, HP * (NW * b + w + 1))
                            S(oT[:, :, w * WIN:(w + 1) * WIN], PB[0][:, 0:HALF].rearrange("p (a t) -> p a t", a=HP),
                              ACT.Copy).then_inc(oT_done, 1)
                        if 1 <= i <= NW:
                            exponentials(i - 1, range(6, 8))

            @block.vector
            def _(dve):
                V = nc.vector
                with dve.Fori(l * B, (l + 1) * B) as b:
                    dve.wait_ge(wo_done, 2 * KD * b)
                    for quarter in range(4):
                        t0, tn = quarter * (T // 4), T // 4
                        for k in range(KD):
                            c0 = t0 + (1 if k == 0 else 0)
                            src = xr[:, k, ds(b - l * B, 1), c0:c0 + tn].rearrange("p o t -> p (o t)")
                            V.tensor_copy(hst[:, 0, k, t0:t0 + tn], src).then_inc(h_high, 1)
                        for k in range(KD):
                            c0 = t0 + (1 if k == 0 else 0)
                            src = xr[:, k, ds(b - l * B, 1), c0:c0 + tn].rearrange("p o t -> p (o t)")
                            dve.wait_ge(h_high, KD * (4 * b + quarter) + k + 1)
                            V.tensor_tensor(hst[:, 1, k, t0:t0 + tn], src, hst[:, 0, k, t0:t0 + tn].bitcast(F32),
                                            ALU.subtract).then_inc(h_low, 1)
                    def normalised(w):
                        dve.wait_ge(qk_sb, NW * b + w + 1)
                        V.tensor_tensor(qkr[:, w, :].rearrange("p (h d) -> p h d", d=HD1),
                                        qkr[:, w, :].rearrange("p (h d) -> p h d", d=HD1),
                                        rn[:, w, :].unsqueeze(2).to_broadcast([P, 2 * H1, HD1]), ALU.mult).then_inc(qn_done, 1)

                    def sines(w):
                        dve.wait_ge(qn_done, NW * b + w + 1)
                        dve.wait_ge(tabs, 4 * (l + 1))
                        for j in range(2):
                            src = qkr[:, w, j * INNER:(j + 1) * INNER].rearrange("p (h d) -> p h d", d=HD1)
                            dst = sinp[:, j * INNER:(j + 1) * INNER].rearrange("p (h d) -> p h d", d=HD1)
                            for r in range(2):
                                a, z = slice(r * C, (r + 1) * C), slice((1 - r) * C, (2 - r) * C)
                                last = V.tensor_tensor(dst[:, :, a], src[:, :, z],
                                                       tab[2 * j + 1][:, w, a].unsqueeze(1).to_broadcast([P, H1, C]), ALU.mult)
                        last.then_inc(sin_done, 1)

                    def turn(w):
                        dve.wait_ge(sin_done, NW * b + w + 1)
                        dve.wait_ge(cos_done, 2 * (NW * b + w + 1))
                        if w >= 2:
                            dve.wait_ge(tk_ps, NW * b + w - 1)
                        V.tensor_tensor(turned[:, w % 2, :], cosp[:, :], sinp[:, :], ALU.add).then_inc(turn_done, 1)
                        dve.wait_ge(turn_done, NW * b + w + 1)

                    def maxima(w, heads):
                        s = w % 2
                        if w >= 2:
                            dve.wait_ge(pt_ps, HP * (NW * b + w - 1))
                        for h in heads:
                            if h % 2 == 0:
                                dve.wait_ge(s_ps, H1 * (NW * b + w) + h + 2)
                                dve.sem_inc(passed, 1)
                            c0 = (h % 4) * 2 * WIN
                            V.tensor_tensor_reduce(sm[:, s, h, keys(w)], PB[1 + h // 4][:, c0:c0 + 2 * WIN][:, keys(w)],
                                                   mask[:, keys(w)], 1.0, 0.0, ALU.add, ALU.max,
                                                   st[:, s, 0, h:h + 1]).then_inc(s_masked, 1)
                            if h % 2 == 1:
                                hs = slice(h - 1, h + 1)
                                dve.wait_ge(s_masked, H1 * (NW * b + w) + h + 1)
                                V.tensor_scalar_mul(st[:, s, 1, hs], st[:, s, 0, hs], -QK_SCALE).then_inc(m_done, 1)

                    def inverse_sums(w, j):
                        hs = slice(4 * j, 4 * j + 4)
                        dve.wait_ge(e_done, 2 * (NW * b + w) + j + 1)
                        V.reciprocal(st[:, w % 2, 3, hs], st[:, w % 2, 2, hs]).then_inc(d_done, 1)

                    def prob_rows(w, p):
                        dve.wait_ge(pt_ps, HP * (NW * b + w) + p + 1)
                        if p > 1 or w:
                            dve.wait_ge(pv_ps, HP * (NW * b + w) + p - 1)
                        c0 = slice(0, 4) if w else slice(1, 4, 2)
                        V.tensor_copy(PT[:, 1, c0, :],
                                      PB[3][:, HALF:2 * HALF].rearrange("p (a t) -> p a t", t=P)[:, c0, :]).then_inc(pt_dve, 1)

                    def inverse_norms(half):
                        hs = slice(half * NN, (half + 1) * NN)
                        dve.wait_ge(n_sqrt, 2 * b + half + 1)
                        V.tensor_scalar_max(nrm[:, hs, :], nrm[:, hs, :], 1e-12).then_inc(n_step, 1)
                        dve.wait_ge(n_step, 4 * b + 2 * half + 1)
                        V.reciprocal(rn[:, hs, :], nrm[:, hs, :]).then_inc(n_step, 1)
                        dve.wait_ge(n_step, 4 * b + 2 * half + 2)

                    dve.wait_ge(G["ld_tab"], 32)
                    for w in range(NW):
                        dve.wait_ge(sq_done, NW * b + w + 1)
                        V.reduce_sum(ss[:, w, :], sq[:, :].rearrange("p (h d) -> p h d", d=HD1), X).then_inc(ss_done, 1)
                        if w == NN - 1:
                            inverse_norms(0)
                        if w == NN:
                            normalised(0)
                            sines(0)
                        if w == NN + 1:
                            turn(0)
                            normalised(1)
                        if w == NN + 2:
                            sines(1)
                            turn(1)
                    for i in range(NW + 2):
                        if 1 <= i <= NW:
                            maxima(i - 1, range(2))
                        if i >= 2:
                            inverse_sums(i - 2, 1)
                        if 1 <= i <= NW:
                            maxima(i - 1, range(2, H1 - 2))
                        if i >= 2:
                            prob_rows(i - 2, 1)
                        if 1 <= i < NW - 1:
                            turn(i + 1)
                        if i < NW - 2:
                            normalised(i + 2)
                        if i >= 2:
                            prob_rows(i - 2, 3)
                        if 1 <= i <= NW:
                            inverse_sums(i - 1, 0)
                        if 1 <= i <= NW:
                            maxima(i - 1, range(H1 - 2, H1))
                        if i < NW - 2:
                            sines(i + 2)
                        if i == 0:
                            inverse_norms(1)
                        if i in (NW // 2 + 2, NW + 1):
                            hf = 0 if i < NW else 1
                            for m in range(KD):
                                dve.wait_ge(wo_ps, KD * (2 * b + hf) + m + 1)
                                xs = xr[:, m, ds(b - l * B, 1), 1 + hf * HALF:1 + (hf + 1) * HALF].rearrange("p o t -> p (o t)")
                                V.tensor_tensor(xs, PB[1][:, m * HALF:(m + 1) * HALF], xs, ALU.add).then_inc(wo_done, 1)


def stage_ffn1(nc, G, A, l, out):
    with ExitStack() as ctx:
        sb = lambda n, s, dt=F32: ctx.enter_context(nc.sbuf_tensor(f"m{l}_{n}", s, dt))
        sem = lambda n: G["layer_sem"](f"m_{n}")
        PB, xr = G["PB"], G["xr"]
        w1, w2, lg, lb, b1, b2 = (G[n] for n in ("w1", "w2", "lg", "lb", "b1", "b2"))
        w1s = [sb(f"w1_{c}", [P, KD, 2 * HIDP], F32R) for c in range(2)]
        w2s = [sb(f"w2_{c}", [P, FT, D], F32R) for c in range(2)]
        mean = sb("mean", [P, P])
        eps = sb("eps", [P, 1])
        xc = sb("xc", [P, KD, HALF])
        sq = sb("sq", [P, KD, HALF])
        xsum = sb("xsum", [P, HALF])
        sqsum = sb("sqsum", [P, HALF])
        sd = sb("sd", [P, HALF])
        rs = sb("rs", [P, HALF])
        xn = sb("xn", [P, KD, HALF])
        hn = sb("hn", [P, KD, HALF])
        hns = [sb(f"hn_{c}", [P, 2, KD, HALF], F32R) for c in range(2)]
        gl = sb("gl", [P, 2, HALF])
        hid = sb("hid", [P, 2, HALF])
        hids = [sb(f"hid_{c}", [P, FT, HALF], F32R) for c in range(2)]
        consts, mu_ps, xc_done, sq_done, var_ps, sd_done, rs_done, xn_done, hn_done, hn_high, hn_low = (sem(n) for n in (
            "consts", "mu_ps", "xc_done", "sq_done", "var_ps", "sd_done", "rs_done", "xn_done", "hn_done", "hn_high", "hn_low"))
        g_ps, a_ps, gl_done, hid_done, hid_high, hid_low, y_ps, y_done = (sem(n) for n in (
            "g_ps", "a_ps", "gl_done", "hid_done", "hid_high", "hid_low", "y_ps", "y_done"))
        w1_high, w1_low, w2_high, w2_low, xsum_done, sqsum_done = (sem(n) for n in (
            "w1_high", "w1_low", "w2_high", "w2_low", "xsum_done", "sqsum_done"))
        stored, ld_half = sem("stored"), [sem(f"ld_half{hf}") for hf in range(T // HALF)]
        NH = T // HALF
        UNITS = NH * B
        NORMS = UNITS + 1
        BANK_MU, BANK_VAR = PB[1][:, 0:HALF], PB[1][:, HALF:2 * HALF]
        QW = HALF // 2

        def norm_of(b, hf):
            return NH * b + hf + l

        def following(b, hf):
            return (b, hf + 1) if hf + 1 < NH else ((2 * l + 1) * B - 1 - b, 0)

        def tokens(b):
            return ds(b - l * B, 1)

        def shifted(b, k, hf):
            c0 = hf * HALF + (1 if k == 0 else 0)
            return xr[:, k, tokens(b), c0:c0 + HALF].rearrange("p o t -> p (o t)")

        def w1_tile(w, f):
            return w[:, :, :].rearrange("p k (c n) -> p k c n", c=2)[:, :, :, f * P:(f + 1) * P]

        final = l + 1 == LAYERS
        x1T = sb("x1T", [P, KD, NH, HALF]) if final else None

        def half_of(b, hf):
            return ds((b - l * B) * T + hf * HALF, HALF)

        with nc.Block() as block:
            @block.sync
            def _(sp):
                if not final:
                    load_attention1(sp, G, A, l + 1)
                    return
                with sp.Fori(l * B, (l + 1) * B) as b:
                    for hf in range(NH):
                        if hf == 0:
                            sp.wait_ge(stored, 16 * NH * (b - l * B))
                        sp.sem_inc(G["passed"], 1)
                        sp.dma_start(x1T[:, :, hf, :], G["x1"][:, half_of(b, hf)].rearrange("(k p) n -> p k n", p=P)
                                     ).then_inc(ld_half[hf], 16)
                    for hf in range(NH):
                        sp.wait_ge(G["x1_ready"], KD * (NH * (b - l * B) + hf + 1))
                        sp.sem_inc(G["passed"], 1)
                        sp.dma_start(out[:, half_of(b, hf)].rearrange("(k p) n -> p k n", p=P), x1T[:, :, hf, :]
                                     ).then_inc(stored, 16)
                sp.wait_ge(stored, 16 * UNITS)

            @block.gpsimd
            def _(pool):
                V = nc.gpsimd
                V.memset(mean[:, :], 1.0 / D).then_inc(consts, 1)
                V.memset(eps[:, :], LN_EPS).then_inc(consts, 1)
                pool.wait_ge(G["ld_ffn"], LD_FFN * (l + 1))

                def normalise(i, n):
                    pool.wait_ge(rs_done, 2 * (i + 1))
                    for k in range(KD):
                        V.tensor_tensor(xn[:, k, :], xc[:, k, :], rs[:, :], ALU.mult).then_inc(xn_done, 1)
                    for k in range(KD):
                        pool.wait_ge(hn_high, KD * i + k + 1)
                        V.tensor_tensor(hns[1][:, n % 2, k, :], hn[:, k, :], hns[0][:, n % 2, k, :].bitcast(F32),
                                        ALU.subtract).then_inc(hn_low, 1)

                V.tensor_copy(w2s[0][:, :, :], w2[:, :, :]).then_inc(w2_high, 1)
                pool.wait_ge(w2_high, l + 1)
                V.tensor_tensor(w2s[1][:, :, :], w2[:, :, :], w2s[0][:, :, :].bitcast(F32), ALU.subtract).then_inc(w2_low, 1)
                if not final:
                    split_wqkv(nc, pool, G, l + 1)
                with pool.Fori(l * B, (l + 1) * B) as b:
                    for hf in range(NH):
                        i = norm_of(b, hf) + 1
                        normalise(i, hf + 1)
                        if final:
                            pool.wait_ge(ld_half[hf], 16 * (b - l * B + 1))
                            for m in range(KD):
                                pool.wait_ge(y_done, KD * (NH * b + hf) + m + 1)
                                xs = xr[:, m, tokens(b), 1 + hf * HALF:1 + (hf + 1) * HALF].rearrange("p o t -> p (o t)")
                                V.tensor_tensor(x1T[:, m, hf, :], x1T[:, m, hf, :], xs, ALU.add).then_inc(G["x1_ready"], 1)

            @block.tensor
            def _(pe):
                mm = nc.tensor.matmul
                pe.wait_ge(consts, 2 * (l + 1))

                def means(i):
                    pe.wait_ge(xsum_done, i + 1)
                    mm(BANK_MU, mean[:, :], xsum[:, :], start=True, stop=True).then_inc(mu_ps, 1)

                def variances(i):
                    pe.wait_ge(sqsum_done, i + 1)
                    mm(BANK_VAR, mean[:, :], sqsum[:, :], start=True, stop=True).then_inc(var_ps, 1)

                means(norm_of(l * B, 0))
                variances(norm_of(l * B, 0))
                with pe.Fori(l * B, (l + 1) * B) as b:
                    for hf in range(NH):
                        i, u0 = norm_of(b, hf), FT * (NH * b + hf)
                        pe.wait_ge(hn_low, KD * (i + 1))
                        for f in range(FT):
                            pe.wait_ge(w1_low, FT * l + f + 1)
                            if f == 1:
                                pe.wait_ge(xc_done, KD * (i + 1))
                                means(i + 1)
                            for part, (col, ready) in enumerate(((HIDP, g_ps), (0, a_ps))):
                                pe.wait_ge(hid_done, u0 + f - 1 if f or hf else u0)
                                for n, (cw, ch) in enumerate(PRODUCTS):
                                    for k in range(KD):
                                        last = mm(PB[2 + f % 2][:, part * HALF:(part + 1) * HALF],
                                                  w1s[cw][:, k, col + f * P:col + (f + 1) * P], hns[ch][:, hf, k, :],
                                                  start=(n == k == 0), stop=(n == len(PRODUCTS) - 1 and k == KD - 1))
                                last.then_inc(ready, 1)
                            if f == 3:
                                pe.wait_ge(sd_done, i + 1)
                                variances(i + 1)
                        pe.wait_ge(w2_low, l + 1)
                        pe.wait_ge(y_done, KD * (NH * b + hf))
                        for tiles in (range(FT - 1), range(FT - 1, FT)):
                            pe.wait_ge(hid_low, u0 + tiles[-1] + 1)
                            for m in range(KD):
                                for f in tiles:
                                    for n, (cw, ch) in enumerate(PRODUCTS):
                                        last = mm(PB[0][:, m * HALF:(m + 1) * HALF], w2s[cw][:, f, m * P:(m + 1) * P],
                                                  hids[ch][:, f, :], start=(f == n == 0),
                                                  stop=(f == FT - 1 and n == len(PRODUCTS) - 1))
                                if tiles[-1] == FT - 1:
                                    last.then_inc(y_ps, 1)

            @block.scalar
            def _(act):
                S = nc.scalar.activation
                act.wait_ge(consts, 2 * (l + 1))
                act.wait_ge(G["ld_ffn"], LD_FFN * (l + 1))

                def squares(i):
                    for k in range(KD):
                        act.wait_ge(xc_done, KD * i + k + 1)
                        if i is not first:
                            act.wait_ge(sqsum_done, i)
                        S(sq[:, k, :], xc[:, k, :], ACT.Square).then_inc(sq_done, 1)

                def deviation(i):
                    act.wait_ge(var_ps, i + 1)
                    act.wait_ge(rs_done, 2 * i)
                    S(sd[:, :], BANK_VAR, ACT.Sqrt, bias=eps[:, 0:1]).then_inc(sd_done, 1)

                def scaled(i):
                    for k in range(KD):
                        act.wait_ge(xn_done, KD * i + k + 1)
                        act.wait_ge(hn_low, KD * i)
                        S(hn[:, k, :], xn[:, k, :], ACT.Identity, bias=lb[:, k:k + 1],
                          scale=lg[:, k:k + 1]).then_inc(hn_done, 1)

                def high_w1(f):
                    S(w1_tile(w1s[0], f), w1_tile(w1, f), ACT.Copy).then_inc(w1_high, 1)

                first = norm_of(l * B, 0)
                for f in range(2):
                    high_w1(f)
                squares(first)
                for f in range(2, FT):
                    high_w1(f)
                deviation(first)
                scaled(first)
                if not final:
                    copy_wqkv(nc, act, G, l + 1)
                    round_wqkv(nc, act, G, l + 1)
                with act.Fori(l * B, (l + 1) * B) as b:
                    for hf in range(NH):
                        i = norm_of(b, hf) + 1
                        for f in range(FT):
                            u = FT * (NH * b + hf) + f
                            act.wait_ge(g_ps, u + 1)
                            act.wait_ge(hid_done, u - 1 if f or hf else u)
                            S(gl[:, f % 2, :], PB[2 + f % 2][:, 0:HALF], ACT.Gelu, bias=b1[:, FT + f:FT + f + 1]).then_inc(gl_done, 1)
                            if f == 1:
                                squares(i)
                            if f == 3:
                                deviation(i)
                        scaled(i)

            @block.vector
            def _(dve):
                V = nc.vector

                def square_sums(i):
                    dve.wait_ge(sq_done, KD * (i + 1))
                    dve.wait_ge(var_ps, i)
                    V.tensor_tensor(sqsum[:, :], sq[:, 0, :], sq[:, 1, :], ALU.add).then_inc(sqsum_done, 1)

                def centred(b, hf, i):
                    dve.wait_ge(mu_ps, i + 1)
                    dve.wait_ge(xn_done, KD * i)
                    dve.wait_ge(sq_done, KD * i)
                    dve.sem_inc(G["passed"], 1)
                    for k in range(KD):
                        V.tensor_tensor(xc[:, k, :], shifted(b, k, hf), BANK_MU, ALU.subtract).then_inc(xc_done, 1)

                def inverse(i, q):
                    dve.wait_ge(sd_done, i + 1)
                    dve.wait_ge(xn_done, KD * i)
                    V.reciprocal(rs[:, q * QW:(q + 1) * QW], sd[:, q * QW:(q + 1) * QW]).then_inc(rs_done, 1)

                def tile_sums(b, hf, i):
                    dve.wait_ge(mu_ps, i)
                    dve.sem_inc(G["passed"], 1)
                    V.tensor_tensor(xsum[:, :], shifted(b, 0, hf), shifted(b, 1, hf), ALU.add).then_inc(xsum_done, 1)

                def low_w1(f):
                    dve.wait_ge(w1_high, FT * l + f + 1)
                    V.tensor_tensor(w1_tile(w1s[1], f), w1_tile(w1, f), w1_tile(w1s[0], f).bitcast(F32),
                                    ALU.subtract).then_inc(w1_low, 1)

                def high(i, n):
                    for k in range(KD):
                        dve.wait_ge(hn_done, KD * i + k + 1)
                        V.tensor_copy(hns[0][:, n % 2, k, :], hn[:, k, :]).then_inc(hn_high, 1)

                first = norm_of(l * B, 0)
                tile_sums(l * B, 0, first)
                dve.wait_ge(G["ld_ffn"], LD_FFN * (l + 1))
                centred(l * B, 0, first)
                low_w1(0)
                low_w1(1)
                square_sums(first)
                for f in range(2, 5):
                    low_w1(f)
                for q in range(2):
                    inverse(first, q)
                dve.wait_ge(rs_done, 2 * (first + 1))
                for k in range(KD):
                    V.tensor_tensor(xn[:, k, :], xc[:, k, :], rs[:, :], ALU.mult).then_inc(xn_done, 1)
                low_w1(5)
                high(first, 0)
                for k in range(KD):
                    dve.wait_ge(hn_high, KD * first + k + 1)
                    V.tensor_tensor(hns[1][:, 0, k, :], hn[:, k, :], hns[0][:, 0, k, :].bitcast(F32), ALU.subtract).then_inc(hn_low, 1)
                with dve.Fori(l * B, (l + 1) * B) as b:
                    for hf in range(NH):
                        i = norm_of(b, hf) + 1
                        if hf + 1 == NH:
                            dve.wait_ge(y_done, KD * (NH * b + 1))
                        tile_sums(*following(b, hf), i)
                        for f in range(FT):
                            u, s = FT * (NH * b + hf) + f, f % 2
                            dve.wait_ge(gl_done, u + 1)
                            dve.wait_ge(a_ps, u + 1)
                            V.scalar_tensor_tensor(out=hid[:, s, :], in0=PB[2 + s][:, HALF:2 * HALF], scalar=b1[:, f:f + 1],
                                                   in1=gl[:, s, :], op0=ALU.add, op1=ALU.mult).then_inc(hid_done, 1)
                            dve.wait_ge(hid_done, u + 1)
                            V.tensor_copy(hids[0][:, f, :], hid[:, s, :]).then_inc(hid_high, 1)
                            dve.wait_ge(hid_high, u + 1)
                            V.tensor_tensor(hids[1][:, f, :], hid[:, s, :], hids[0][:, f, :].bitcast(F32),
                                            ALU.subtract).then_inc(hid_low, 1)
                            if f == 0:
                                centred(*following(b, hf), i)
                            if f == 1:
                                square_sums(i)
                            if f in (3, 4):
                                inverse(i, f - 3)
                        high(i, hf + 1)
                        for m in range(KD):
                            dve.wait_ge(y_ps, KD * (NH * b + hf) + m + 1)
                            xs = xr[:, m, tokens(b), 1 + hf * HALF:1 + (hf + 1) * HALF].rearrange("p o t -> p (o t)")
                            V.scalar_tensor_tensor(out=xs, in0=PB[0][:, m * HALF:(m + 1) * HALF], scalar=b2[:, m:m + 1],
                                                   in1=xs, op0=ALU.add, op1=ALU.add).then_inc(y_done, 1)


def program(nc, A, out):
    with ExitStack() as top:
        def sb(n, s, dt=F32, ctx=top, side="left"):
            return ctx.enter_context(nc.sbuf_tensor(n, s, dt, side=side))

        G = {"PB": [top.enter_context(nc.psum_tensor(f"bank{i}", [P, 2 * HALF], F32)) for i in range(4)],
             "x1": nc.dram_tensor("x1", [D, N], F32, kind="Internal").ap(),
             "scr": nc.dram_tensor("qk_parts", [2, 3, D, N], BF16, kind="Internal").ap()}
        for n in ("ld_att", "ld_ffn", "ld_tab", "passed", "ld_phi", "phi_high", "phi_low", "wqkv_copy", "wqkv_low", "wqkv_high", "x1_ready", "x1_out"):
            G[n] = top.enter_context(nc.semaphore("g_" + n))
        G["early_sems"] = []

        def early_sem(n):
            G["early_sems"].append(nc.alloc_semaphore(n))
            return G["early_sems"][-1]

        G["early_sem"] = early_sem
        layer_sems = {}

        def layer_sem(n):
            if n not in layer_sems:
                layer_sems[n] = top.enter_context(nc.semaphore(n))
            return layer_sems[n]

        G["layer_sem"] = layer_sem
        G["ident"] = sb("ident", [P, P])
        G["rot"] = sb("rot", [P, KD, D])
        G["csum"] = sb("csum", [P, KD, B])
        heads, values, mixed, moe = ExitStack(), ExitStack(), ExitStack(), ExitStack()
        G["gate"] = sb("gate", [P, B * TT * H0], ctx=heads, side="right")
        G["fa"] = sb("fa", [P, TT, B], ctx=heads, side="right")
        G["vsum"] = sb("vsum", [P, B, D], ctx=heads, side="right")
        G["v"] = sb("v", [P, 2 * B, TT, P], ctx=values)
        G["qa"] = [sb(f"qa{s}", [KA, HG, T], BF16, ctx=values) for s in range(GB)]
        G["ka"] = [sb(f"ka{s}", [KA, HG, T], BF16, ctx=values) for s in range(GB)]
        G["staged"] = [top.enter_context(nc.semaphore(f"staged{s}")) for s in range(GB)]
        stage_project(nc, G, A)
        G["OT"] = sb("OT", [P, 2 * HG, T], ctx=heads, side="right")
        stage_attention0(nc, G, A)
        values.close()
        G["X0T"] = [sb(f"X0T_{c}", [P, KD, N], F32R, ctx=mixed) for c in range(2)]
        G["X0"] = [sb(f"X0_{c}", [P, B * TT, D], F32R, ctx=mixed) for c in range(2)]
        G["phi"] = sb("phi", [P, KD, CS], ctx=mixed)
        G["phis"] = [sb(f"phi_{c}", [P, KD, CS], F32R, ctx=mixed) for c in range(2)]
        stage_out0(nc, G, A)
        heads.close()
        G["O"] = sb("O", [P, B * TT, D], ctx=moe, side="right")
        G["den"] = sb("den", [P, B * TT], ctx=moe, side="right")
        stage_moe(nc, G, A)
        mixed.close()
        G["xr"] = sb("xr", [P, KD, B, 1 + T])
        with ExitStack() as place:
            G["wqkv1_raw"] = sb("wqkv1_raw", [P, KD, 3 * INNER], ctx=place)
        G["wqkv1"] = [sb(f"wqkv1_{c}", [P, KD, 3 * INNER], F32R) for c in range(2)]
        G["wo"] = sb("wo", [P, HP, D])
        G["mask"] = sb("mask", [P, 2 * WIN])
        G["qks"] = sb("qks", [P, LAYERS, 4, HD1])
        G["w1"] = sb("w1", [P, KD, 2 * HIDP])
        G["w2"] = sb("w2", [P, FT, D])
        G["lg"], G["lb"], G["b2"] = (sb(n, [P, KD]) for n in ("lg", "lb", "b2"))
        G["b1"] = sb("b1", [P, 2 * FT])
        stage_rotate(nc, G, A)
        moe.close()
        for l in range(LAYERS):
            stage_attention1(nc, G, A, l)
            stage_ffn1(nc, G, A, l, out)


def constants():
    f = np.float32
    c = {}
    inv = f(10000.0) ** np.repeat(np.arange(0, D, 2, dtype=f) / f(D), 2)
    c["peT"] = np.sin(np.arange(T, dtype=f)[:, None] / inv[None, :]).astype(f).T
    half = np.arange(0, HD1, 2, dtype=f)
    t = np.arange(T, dtype=f)
    freqs = t[:, None] * (f(1.0) / f(10000.0) ** (half / f(HD1)))[None, :]
    freqs = np.concatenate([freqs, freqs], -1)
    scale = ((half + f(0.4 * HD1)) / f(1.4 * HD1))[None, :] ** ((t - T // 2) / f(WIN // 2))[:, None]
    scale = np.concatenate([scale, scale], -1)
    cos, sin = np.cos(freqs), np.sin(freqs)
    sin = np.concatenate([-sin[:, :HD1 // 2], sin[:, HD1 // 2:]], -1)
    c["tables"] = np.stack([cos * scale, sin * scale, cos / scale, sin / scale]).astype(f)
    i, j = np.arange(WIN)[:, None], np.arange(WIN)[None, :]
    c["mask"] = np.concatenate([np.where(j >= i, 0.0, MASKED), np.where(j <= i, 0.0, MASKED)], 1).astype(f)
    c["ident"] = np.eye(P, dtype=f)
    ham = np.zeros((4, 4, 4))
    for k, terms in enumerate((((0, 0, 1), (1, 1, -1), (2, 2, -1), (3, 3, -1)), ((0, 1, 1), (1, 0, 1), (2, 3, 1), (3, 2, -1)),
                               ((0, 2, 1), (1, 3, -1), (2, 0, 1), (3, 1, 1)), ((0, 3, 1), (1, 2, 1), (2, 1, -1), (3, 0, 1)))):
        for a, b, s in terms:
            ham[k, a, b] = s
    conj = np.array([1.0, -1.0, -1.0, -1.0])
    c["sgn"] = np.einsum("iak,kjb,b->abij", ham, ham, conj).reshape(16, 16).astype(f)
    return c


def kernel(**inputs):
    import concourse.bacc as _bacc
    from concourse.bass_utils import run_bass_kernel_spmd as _run

    I = {n: np.asarray(v) for n, v in inputs.items()}
    c0, f1 = "L0_cond_", "L1_ffn_"
    col = lambda v: v.reshape(-1, P).T
    rep = lambda v, n: np.broadcast_to(v, (n,) + v.shape)
    pad = lambda a, n: np.pad(a, [(0, 0)] * (a.ndim - 1) + [(0, n - a.shape[-1])])
    cond, qr = I["cond_256"], I["L1_cond_q_right"]
    w1, b1 = I[f1 + "w1"], I[f1 + "b1"]
    phi = I["L0_ffn_phi"].reshape(D, SLOTS)
    w1 = np.concatenate([pad(w1[..., :HID], HIDP), pad(w1[..., HID:], HIDP)], -1)
    b1 = np.concatenate([pad(b1[..., :HID], HIDP), pad(b1[..., HID:], HIDP)], -1)
    qs, ks = I[f1 + "q_scale"], I[f1 + "k_scale"]
    swap = lambda v: np.concatenate([v[:, HD1 // 2:], v[:, :HD1 // 2]], -1)
    rows = [0] * 4 + [1] * 12
    arrays = {
        **constants(),
        "xT": I["x"].reshape(N, D).T,
        "wqkv0T": I[c0 + "Wqkv"].T, "bqk": col(I[c0 + "bqkv"][:2 * D]), "bvB": rep(I[c0 + "bqkv"][2 * D:], P),
        "wc1xT": I[c0 + "Wc1"][:, :D].T, "wc1cT": I[c0 + "Wc1"][:, D:].T, "bc1": col(I[c0 + "bc1"]),
        "wc2T": I[c0 + "Wc2"].T, "bc2B": rep(I[c0 + "bc2"], P),
        "csT": cond.T, "we1T": I[c0 + "We1"].T, "be1": col(I[c0 + "be1"]), "we2T": I[c0 + "We2"].T,
        "rows2": rep(np.stack([I[c0 + "be2"], I[c0 + "ln_g"], I[c0 + "ln_b"]]), B),
        "woutT": I[c0 + "Wout"].T, "bout": col(I[c0 + "bout"]), "boutB": rep(I[c0 + "bout"], P),
        "phi": np.concatenate([phi, phi[:, :CS]], 1), "W": I["L0_ffn_W"], "bexp": np.repeat(I["L0_ffn_b"], NP_, 0),
        "ql": cond[rows], "qr": np.tile(qr, (4, 1)), "gate": rep(I["L1_cond_spectral_gate"].reshape(64), 16),
        "qall": rep(np.concatenate([cond, qr], 0), 16),
        "wqkv1": I[f1 + "wqkv"], "wo": I[f1 + "wo"], "w1": w1,
        "w2": np.pad(I[f1 + "w2"], [(0, 0), (0, HIDP - HID), (0, 0)]),
        "lg": np.stack([col(v) for v in I[f1 + "ln_g"]]), "lb": np.stack([col(v) for v in I[f1 + "ln_b"]]),
        "b1": np.stack([col(v) for v in b1]), "b2": np.stack([col(v) for v in I[f1 + "b2"]]),
        "qks": rep(np.stack([qs, swap(qs), ks, swap(ks)], 1), P),
    }
    arrays = {f"in_{n}": np.ascontiguousarray(a) for n, a in arrays.items()}
    nc = _bacc.Bacc("TRN2", target_bir_lowering=False, num_devices=1)
    A = {n[3:]: nc.dram_tensor(n, a.shape, mybir.dt.from_np(a.dtype), kind="ExternalInput").ap() for n, a in arrays.items()}
    out = nc.dram_tensor("out_T", (D, N), F32, kind="ExternalOutput").ap()
    program(nc, A, out)
    r = _run(nc, [arrays], core_ids=[0])
    return np.ascontiguousarray(r.results[0]["out_T"].T).reshape(B, T, D)
```
